# Optimizing a Trainium2 kernel written in Bass

```python
import numpy as np
import jax
import jax.numpy as jnp

def _softmax(x, axis=-1):
    return jax.nn.softmax(x, axis=axis)

def _gelu(x):
    return jax.nn.gelu(x, approximate=True)

def _silu(x):
    return jax.nn.silu(x)

def _sigmoid(x):
    return jax.nn.sigmoid(x)

def _layernorm(x, axis=-1, eps=1e-05):
    m = jnp.mean(x, axis=axis, keepdims=True)
    v = jnp.var(x, axis=axis, keepdims=True)
    return (x - m) / jnp.sqrt(v + eps)

def _scatter_add(tgt, idx, src, axis=0):
    return tgt.at[idx].add(src)

def _segment_sum(src, seg, n):
    return jax.ops.segment_sum(src, seg, n)
kernel_name = 'mk_gnn_ffn_d4_gnn_r32_24700e'

def setup_inputs(seed: int=0):
    np.random.seed(seed)
    _w = jnp.asarray

    def _rec_inputs():
        import jax
        import jax.numpy as jnp
        _gk = jax.random.key(seed)
        x = -0.0003713 + 1 * jax.random.normal(jax.random.fold_in(_gk, 1), (3125, 256), jnp.float32)
        src = jax.random.randint(jax.random.fold_in(_gk, 2), (50000,), 0, 3125, jnp.int32)
        dst = jax.random.randint(jax.random.fold_in(_gk, 3), (50000,), 0, 3125, jnp.int32)
        _o = jnp.argsort(dst, stable=True)
        src = src[_o]
        dst = dst[_o]
        edge_weight = jax.random.uniform(jax.random.fold_in(_gk, 13), (50000,), jnp.float32, 0.0, 1)
        return (x, src, dst, edge_weight)
    x, src, dst, edge_weight = _rec_inputs()

    def _L0_gnn_setup():
        import jax, jax.numpy as jnp
        import numpy as np
        BN_EPS = 1e-05
        CHANNELS = [256, 512, 1024, 512, 256]

        def _bn(h, gamma, beta):
            m = h.mean(axis=0)
            v = h.var(axis=0)
            return gamma * (h - m) * jax.lax.rsqrt(v + BN_EPS) + beta
        key = jax.random.key(seed)
        N, E = (50000, 25000)
        ks = jax.random.split(key, 16)
        inp = {'x': jax.random.normal(ks[0], (N, CHANNELS[0]), dtype=jnp.float32), 'edge_index': jax.random.randint(ks[1], (2, E), 0, N, dtype=jnp.int32), 'eps': jnp.float32(0.1)}
        for i in range(4):
            cin, cout = (CHANNELS[i], CHANNELS[i + 1])
            inp[f'W{i + 1}'] = jax.random.normal(ks[2 + 3 * i], (cin, cout), dtype=jnp.float32) * (1.0 / np.sqrt(cin))
            inp[f'b{i + 1}'] = jnp.zeros((cout,), dtype=jnp.float32)
            if i < 3:
                inp[f'g{i + 1}'] = jnp.ones((cout,), dtype=jnp.float32)
                inp[f'beta{i + 1}'] = jnp.zeros((cout,), dtype=jnp.float32)
        return inp
    _L0_gnn_all = _L0_gnn_setup()
    _L0_gnn_in = {k: v for k, v in _L0_gnn_all.items() if k in ('eps', 'W1', 'b1', 'g1', 'beta1', 'W2', 'b2', 'g2', 'beta2', 'W3', 'b3', 'g3', 'beta3', 'W4', 'b4')}
    del _L0_gnn_all

    def _L0_ffn_setup():
        import jax, jax.numpy as jnp
        import numpy as np
        E, D, H, TOP_K = (6, 256, 256, 2)
        ROUTER_H = D // 2
        key = jax.random.key(seed)
        ks = jax.random.split(key, 12)
        s = 1.0 / np.sqrt(D)
        sh = 1.0 / np.sqrt(H)
        sr = 1.0 / np.sqrt(ROUTER_H)
        return {'features': jax.random.normal(ks[0], (8, 128, D), dtype=jnp.float32), 'router_w1': jax.random.uniform(ks[1], (D, ROUTER_H), jnp.float32, -s, s), 'router_b1': jnp.zeros((ROUTER_H,), jnp.float32), 'router_w2': jax.random.uniform(ks[2], (ROUTER_H, E), jnp.float32, -sr, sr), 'router_b2': jnp.zeros((E,), jnp.float32), 'expert_w1': jax.random.uniform(ks[3], (E, D, H), jnp.float32, -s, s), 'expert_b1': jnp.zeros((E, H), jnp.float32), 'expert_w2': jax.random.uniform(ks[4], (E, H, H), jnp.float32, -sh, sh), 'expert_b2': jnp.zeros((E, H), jnp.float32), 'expert_w3': jax.random.uniform(ks[5], (E, H, D), jnp.float32, -sh, sh), 'expert_b3': jnp.zeros((E, D), jnp.float32)}
    _L0_ffn_all = _L0_ffn_setup()
    _L0_ffn_in = {k: v for k, v in _L0_ffn_all.items() if k in ('router_w1', 'router_b1', 'router_w2', 'router_b2', 'expert_w1', 'expert_b1', 'expert_w2', 'expert_b2', 'expert_w3', 'expert_b3')}
    del _L0_ffn_all

    def _L1_gnn_setup():
        import jax, jax.numpy as jnp
        import numpy as np
        N_NODES = 3125
        N_EDGES = 100000
        F_IN = 256
        F_OUT = 256
        key = jax.random.key(seed)
        k1, k2, k3, k4, k5 = jax.random.split(key, 5)
        features = jax.random.normal(k1, (N_NODES, F_IN), dtype=jnp.float32)
        edge_row = jax.random.randint(k2, (N_EDGES,), 0, N_NODES, dtype=jnp.int32)
        edge_col = jax.random.randint(k3, (N_EDGES,), 0, N_NODES, dtype=jnp.int32)
        edge_vals = jax.random.uniform(k4, (N_EDGES,), dtype=jnp.float32)
        limit = float(np.sqrt(6.0 / (F_IN + F_OUT)))
        kernel = jax.random.uniform(k5, (F_IN, F_OUT), dtype=jnp.float32, minval=-limit, maxval=limit)
        bias = jnp.zeros((F_OUT,), dtype=jnp.float32)
        return {'features': features, 'edge_vals': edge_vals, 'kernel': kernel, 'bias': bias, 'edge_row': edge_row, 'edge_col': edge_col}
    _L1_gnn_all = _L1_gnn_setup()
    _L1_gnn_in = {k: v for k, v in _L1_gnn_all.items() if k in ('kernel', 'bias')}
    del _L1_gnn_all

    def _L1_ffn_setup():
        import jax, jax.numpy as jnp
        import numpy as np
        B, S, D = (8, 128, 256)
        H = 4 * D
        CAPACITY = 0.5
        key = jax.random.key(seed)
        ks = jax.random.split(key, 6)
        x = jax.random.normal(ks[0], (B, S, D), dtype=jnp.float32)
        attention_mask = jnp.zeros((B, 1, 1, S), dtype=jnp.float32)
        wr = jax.random.normal(ks[1], (D, 1), dtype=jnp.float32) * 0.02
        br = jnp.zeros((1,), dtype=jnp.float32)
        w1 = jax.random.normal(ks[2], (D, H), dtype=jnp.float32) * 0.02
        b1 = jnp.zeros((H,), dtype=jnp.float32)
        w2 = jax.random.normal(ks[3], (H, D), dtype=jnp.float32) * 0.02
        b2 = jnp.zeros((D,), dtype=jnp.float32)
        return {'x': x, 'attention_mask': attention_mask, 'wr': wr, 'br': br, 'w1': w1, 'b1': b1, 'w2': w2, 'b2': b2}
    _L1_ffn_all = _L1_ffn_setup()
    _L1_ffn_in = {k: v for k, v in _L1_ffn_all.items() if k in ('attention_mask', 'wr', 'br', 'w1', 'b1', 'w2', 'b2')}
    del _L1_ffn_all

    def _L2_gnn_setup():
        import jax, jax.numpy as jnp
        import numpy as np
        N = 50000
        E = 25000
        IN, HID, OUT = (256, 512, 256)
        key = jax.random.key(seed)
        ks = jax.random.split(key, 8)
        x = jax.random.normal(ks[0], (N, IN), dtype=jnp.float32)
        edge_index = jax.random.randint(ks[1], (2, E), 0, N, dtype=jnp.int64)

        def lin(k, fan_out, fan_in):
            s = 1.0 / np.sqrt(fan_in)
            return jax.random.uniform(k, (fan_out, fan_in), jnp.float32, -s, s)
        return {'x': x, 'edge_index': edge_index, 'W1l': lin(ks[2], HID, IN), 'b1': jnp.zeros((HID,), jnp.float32), 'W1r': lin(ks[3], HID, IN), 'W2l': lin(ks[4], OUT, HID), 'b2': jnp.zeros((OUT,), jnp.float32), 'W2r': lin(ks[5], OUT, HID)}
    _L2_gnn_all = _L2_gnn_setup()
    _L2_gnn_in = {k: v for k, v in _L2_gnn_all.items() if k in ('W1l', 'b1', 'W1r', 'W2l', 'b2', 'W2r')}
    del _L2_gnn_all

    def _L2_ffn_setup():
        import jax, jax.numpy as jnp
        import numpy as np
        B, N, D = (16, 128, 256)
        NUM_EXPERTS, TOP_K, HEADS = (4, 2, 4)
        N_EDGES = 32768
        LN_EPS = 1e-05

        def _layernorm(x, g, b):
            mu = x.mean(-1, keepdims=True)
            var = ((x - mu) ** 2).mean(-1, keepdims=True)
            return (x - mu) * jax.lax.rsqrt(var + LN_EPS) * g + b

        def _forward(x, edge_index, W_gat, att_src, att_dst, b_gat, ln_gamma, ln_beta, W1, b1, W2, b2):
            Bc, Nc, Dc = x.shape
            M = Bc * Nc
            x_flat = x.reshape(M, Dc)
            h = (x_flat @ W_gat).reshape(M, HEADS, NUM_EXPERTS)
            loops = jnp.arange(M, dtype=edge_index.dtype)
            src = jnp.concatenate([edge_index[0], loops])
            dst = jnp.concatenate([edge_index[1], loops])
            a_src = (h * att_src).sum(-1)
            a_dst = (h * att_dst).sum(-1)
            e = jax.nn.leaky_relu(a_src[src] + a_dst[dst], negative_slope=0.2)
            e_max = jax.ops.segment_max(e, dst, num_segments=M)
            ee = jnp.exp(e - e_max[dst])
            denom = jax.ops.segment_sum(ee, dst, num_segments=M)
            alpha = ee / (denom[dst] + 1e-16)
            msg = h[src] * alpha[:, :, None]
            agg = jax.ops.segment_sum(msg, dst, num_segments=M).reshape(M, HEADS * NUM_EXPERTS) + b_gat
            scores = _layernorm(agg, ln_gamma, ln_beta).reshape(M, HEADS, NUM_EXPERTS).mean(1)
            scores = scores.reshape(Bc, Nc, NUM_EXPERTS)
            topk_s, topk_i = jax.lax.top_k(scores, TOP_K)
            w = jax.nn.softmax(topk_s, axis=-1)
            out = jnp.zeros_like(x)
            for ei in range(NUM_EXPERTS):
                g = jnp.where(topk_i == ei, w, 0.0).sum(-1)
                hh = jax.nn.gelu(x @ W1[ei] + b1[ei], approximate=False)
                out = out + g[..., None] * (hh @ W2[ei] + b2[ei])
            return out
        key = jax.random.key(seed)
        ks = jax.random.split(key, 8)
        s = 0.05
        return {'x': jax.random.normal(ks[0], (B, N, D), jnp.float32), 'W_gat': jax.random.normal(ks[1], (D, HEADS * NUM_EXPERTS), jnp.float32) * s, 'att_src': jax.random.normal(ks[2], (HEADS, NUM_EXPERTS), jnp.float32) * s, 'att_dst': jax.random.normal(ks[3], (HEADS, NUM_EXPERTS), jnp.float32) * s, 'b_gat': jnp.zeros((HEADS * NUM_EXPERTS,), jnp.float32), 'ln_gamma': jnp.ones((HEADS * NUM_EXPERTS,), jnp.float32), 'ln_beta': jnp.zeros((HEADS * NUM_EXPERTS,), jnp.float32), 'W1': jax.random.normal(ks[4], (NUM_EXPERTS, D, 2 * D), jnp.float32) * s, 'b1': jnp.zeros((NUM_EXPERTS, 2 * D), jnp.float32), 'W2': jax.random.normal(ks[5], (NUM_EXPERTS, 2 * D, D), jnp.float32) * s, 'b2': jnp.zeros((NUM_EXPERTS, D), jnp.float32), 'edge_index': jax.random.randint(ks[6], (2, N_EDGES), 0, B * N, jnp.int32)}
    _L2_ffn_all = _L2_ffn_setup()
    _L2_ffn_in = {k: v for k, v in _L2_ffn_all.items() if k in ('W_gat', 'att_src', 'att_dst', 'b_gat', 'ln_gamma', 'ln_beta', 'W1', 'b1', 'W2', 'b2', 'edge_index')}
    del _L2_ffn_all

    def _L3_gnn_setup():
        import jax, jax.numpy as jnp
        import numpy as np
        N_NODES = 3125
        N_EDGES = 50000
        IN_DIM = 256
        OUT_DIM = 256
        key = jax.random.key(seed)
        k1, k2, k3 = jax.random.split(key, 3)
        x = jax.random.normal(k1, (N_NODES, IN_DIM), dtype=jnp.float32)
        limit = 0.1 * np.sqrt(6.0 / (IN_DIM + OUT_DIM))
        W = jax.random.uniform(k2, (OUT_DIM, IN_DIM), dtype=jnp.float32, minval=-limit, maxval=limit)
        b = jnp.zeros((OUT_DIM,), dtype=jnp.float32)
        edge_index = jax.random.randint(k3, (2, N_EDGES), 0, N_NODES, dtype=jnp.int64)
        return {'x': x, 'W': W, 'b': b, 'edge_index': edge_index}
    _L3_gnn_all = _L3_gnn_setup()
    _L3_gnn_in = {k: v for k, v in _L3_gnn_all.items() if k in ('W', 'b')}
    del _L3_gnn_all

    def _L3_ffn_setup():
        import jax, jax.numpy as jnp
        import numpy as np
        B, S, H, F, E, K = (8, 128, 256, 512, 16, 2)
        EPS = 1e-05
        key = jax.random.key(seed)
        ks = jax.random.split(key, 9)
        sc = 0.02
        return {'x': jax.random.normal(ks[0], (B, S, H), dtype=jnp.float32), 'gate_w': jax.random.normal(ks[1], (H, E), dtype=jnp.float32) * sc, 'gate_b': jnp.zeros((E,), dtype=jnp.float32), 'w1': jax.random.normal(ks[2], (E, H, F), dtype=jnp.float32) * sc, 'b1': jnp.zeros((E, F), dtype=jnp.float32), 'w2': jax.random.normal(ks[3], (E, F, H), dtype=jnp.float32) * sc, 'b2': jnp.zeros((E, H), dtype=jnp.float32), 'gamma': jnp.ones((H,), dtype=jnp.float32), 'beta': jnp.zeros((H,), dtype=jnp.float32)}
    _L3_ffn_all = _L3_ffn_setup()
    _L3_ffn_in = {k: v for k, v in _L3_ffn_all.items() if k in ('gate_w', 'gate_b', 'w1', 'b1', 'w2', 'b2', 'gamma', 'beta')}
    del _L3_ffn_all
    return {'x': x, 'src': src, 'dst': dst, 'edge_weight': edge_weight, 'L0_gnn_eps': _L0_gnn_in['eps'], 'L0_gnn_W1': _L0_gnn_in['W1'], 'L0_gnn_b1': _L0_gnn_in['b1'], 'L0_gnn_g1': _L0_gnn_in['g1'], 'L0_gnn_beta1': _L0_gnn_in['beta1'], 'L0_gnn_W2': _L0_gnn_in['W2'], 'L0_gnn_b2': _L0_gnn_in['b2'], 'L0_gnn_g2': _L0_gnn_in['g2'], 'L0_gnn_beta2': _L0_gnn_in['beta2'], 'L0_gnn_W3': _L0_gnn_in['W3'], 'L0_gnn_b3': _L0_gnn_in['b3'], 'L0_gnn_g3': _L0_gnn_in['g3'], 'L0_gnn_beta3': _L0_gnn_in['beta3'], 'L0_gnn_W4': _L0_gnn_in['W4'], 'L0_gnn_b4': _L0_gnn_in['b4'], 'L0_ffn_router_w1': _L0_ffn_in['router_w1'], 'L0_ffn_router_b1': _L0_ffn_in['router_b1'], 'L0_ffn_router_w2': _L0_ffn_in['router_w2'], 'L0_ffn_router_b2': _L0_ffn_in['router_b2'], 'L0_ffn_expert_w1': _L0_ffn_in['expert_w1'], 'L0_ffn_expert_b1': _L0_ffn_in['expert_b1'], 'L0_ffn_expert_w2': _L0_ffn_in['expert_w2'], 'L0_ffn_expert_b2': _L0_ffn_in['expert_b2'], 'L0_ffn_expert_w3': _L0_ffn_in['expert_w3'], 'L0_ffn_expert_b3': _L0_ffn_in['expert_b3'], 'L1_gnn_kernel': _L1_gnn_in['kernel'], 'L1_gnn_bias': _L1_gnn_in['bias'], 'L1_ffn_attention_mask': _L1_ffn_in['attention_mask'], 'L1_ffn_wr': _L1_ffn_in['wr'], 'L1_ffn_br': _L1_ffn_in['br'], 'L1_ffn_w1': _L1_ffn_in['w1'], 'L1_ffn_b1': _L1_ffn_in['b1'], 'L1_ffn_w2': _L1_ffn_in['w2'], 'L1_ffn_b2': _L1_ffn_in['b2'], 'L2_gnn_W1l': _L2_gnn_in['W1l'], 'L2_gnn_b1': _L2_gnn_in['b1'], 'L2_gnn_W1r': _L2_gnn_in['W1r'], 'L2_gnn_W2l': _L2_gnn_in['W2l'], 'L2_gnn_b2': _L2_gnn_in['b2'], 'L2_gnn_W2r': _L2_gnn_in['W2r'], 'L2_ffn_W_gat': _L2_ffn_in['W_gat'], 'L2_ffn_att_src': _L2_ffn_in['att_src'], 'L2_ffn_att_dst': _L2_ffn_in['att_dst'], 'L2_ffn_b_gat': _L2_ffn_in['b_gat'], 'L2_ffn_ln_gamma': _L2_ffn_in['ln_gamma'], 'L2_ffn_ln_beta': _L2_ffn_in['ln_beta'], 'L2_ffn_W1': _L2_ffn_in['W1'], 'L2_ffn_b1': _L2_ffn_in['b1'], 'L2_ffn_W2': _L2_ffn_in['W2'], 'L2_ffn_b2': _L2_ffn_in['b2'], 'L2_ffn_edge_index': _L2_ffn_in['edge_index'], 'L3_gnn_W': _L3_gnn_in['W'], 'L3_gnn_b': _L3_gnn_in['b'], 'L3_ffn_gate_w': _L3_ffn_in['gate_w'], 'L3_ffn_gate_b': _L3_ffn_in['gate_b'], 'L3_ffn_w1': _L3_ffn_in['w1'], 'L3_ffn_b1': _L3_ffn_in['b1'], 'L3_ffn_w2': _L3_ffn_in['w2'], 'L3_ffn_b2': _L3_ffn_in['b2'], 'L3_ffn_gamma': _L3_ffn_in['gamma'], 'L3_ffn_beta': _L3_ffn_in['beta']}

def reference(x, src, dst, edge_weight, L0_gnn_eps, L0_gnn_W1, L0_gnn_b1, L0_gnn_g1, L0_gnn_beta1, L0_gnn_W2, L0_gnn_b2, L0_gnn_g2, L0_gnn_beta2, L0_gnn_W3, L0_gnn_b3, L0_gnn_g3, L0_gnn_beta3, L0_gnn_W4, L0_gnn_b4, L0_ffn_router_w1, L0_ffn_router_b1, L0_ffn_router_w2, L0_ffn_router_b2, L0_ffn_expert_w1, L0_ffn_expert_b1, L0_ffn_expert_w2, L0_ffn_expert_b2, L0_ffn_expert_w3, L0_ffn_expert_b3, L1_gnn_kernel, L1_gnn_bias, L1_ffn_attention_mask, L1_ffn_wr, L1_ffn_br, L1_ffn_w1, L1_ffn_b1, L1_ffn_w2, L1_ffn_b2, L2_gnn_W1l, L2_gnn_b1, L2_gnn_W1r, L2_gnn_W2l, L2_gnn_b2, L2_gnn_W2r, L2_ffn_W_gat, L2_ffn_att_src, L2_ffn_att_dst, L2_ffn_b_gat, L2_ffn_ln_gamma, L2_ffn_ln_beta, L2_ffn_W1, L2_ffn_b1, L2_ffn_W2, L2_ffn_b2, L2_ffn_edge_index, L3_gnn_W, L3_gnn_b, L3_ffn_gate_w, L3_ffn_gate_b, L3_ffn_w1, L3_ffn_b1, L3_ffn_w2, L3_ffn_b2, L3_ffn_gamma, L3_ffn_beta):
    import jax
    import jax.numpy as jnp

    def _L0_gnn_ref(x, edge_index, eps, W1, b1, g1, beta1, W2, b2, g2, beta2, W3, b3, g3, beta3, W4, b4):
        import jax, jax.numpy as jnp
        import numpy as np
        BN_EPS = 1e-05
        CHANNELS = [256, 512, 1024, 512, 256]

        def _bn(h, gamma, beta):
            m = h.mean(axis=0)
            v = h.var(axis=0)
            return gamma * (h - m) * jax.lax.rsqrt(v + BN_EPS) + beta
        src, dst = (edge_index[0], edge_index[1])
        agg = jax.ops.segment_sum(x[src], dst, num_segments=x.shape[0])
        h = (1.0 + eps) * x + agg
        h = jax.nn.elu(_bn(h @ W1 + b1, g1, beta1))
        h = jax.nn.elu(_bn(h @ W2 + b2, g2, beta2))
        h = jax.nn.elu(_bn(h @ W3 + b3, g3, beta3))
        return h @ W4 + b4

    def _L0_ffn_ref(features, router_w1, router_b1, router_w2, router_b2, expert_w1, expert_b1, expert_w2, expert_b2, expert_w3, expert_b3):
        import jax, jax.numpy as jnp
        import numpy as np
        E, D, H, TOP_K = (6, 256, 256, 2)
        ROUTER_H = D // 2
        rh = jax.nn.relu(features @ router_w1 + router_b1)
        expert_logits = jax.nn.softmax(rh @ router_w2 + router_b2, axis=-1)
        top_w, top_i = jax.lax.top_k(expert_logits, TOP_K)
        routing_weights = jax.nn.softmax(top_w, axis=-1)
        h1 = jax.nn.relu(jnp.einsum('bsd,edh->bseh', features, expert_w1) + expert_b1)
        h2 = jax.nn.relu(jnp.einsum('bseh,ehf->bsef', h1, expert_w2) + expert_b2)
        expert_out = jnp.einsum('bsef,efo->bseo', h2, expert_w3) + expert_b3
        sel = jnp.take_along_axis(expert_out, top_i[:, :, :, None], axis=2)
        combined = jnp.sum(sel * routing_weights[..., None], axis=2)
        return combined

    def _L1_gnn_ref(features, edge_vals, kernel, bias, edge_row, edge_col):
        import jax, jax.numpy as jnp
        import numpy as np
        N_NODES = 3125
        N_EDGES = 100000
        F_IN = 256
        F_OUT = 256
        xw = features @ kernel
        msgs = edge_vals[:, None] * xw[edge_col]
        out = jax.ops.segment_sum(msgs, edge_row, num_segments=features.shape[0])
        return out + bias

    def _L1_ffn_ref(x, attention_mask, wr, br, w1, b1, w2, b2):
        import jax, jax.numpy as jnp
        import numpy as np
        B, S, D = (8, 128, 256)
        H = 4 * D
        CAPACITY = 0.5
        b, s, d = x.shape
        weights = (jnp.einsum('bsd,do->bso', x, wr) + br)[..., 0]
        k = max(1, int(CAPACITY * s))
        kk = k - 1 if k > 1 else 1
        _, idx = jax.lax.top_k(weights, k)
        sel_idx = idx[:, :kk]
        sel = jnp.take_along_axis(x, sel_idx[:, :, None], axis=1)
        h = jax.nn.gelu(jnp.einsum('bkd,dh->bkh', sel, w1) + b1)
        y = jnp.einsum('bkh,hd->bkd', h, w2) + b2
        w_sel = jnp.take_along_axis(weights, sel_idx, axis=1)
        y = y * w_sel[..., None]
        batch_idx = jnp.arange(b)[:, None]
        processed = jnp.zeros_like(x).at[batch_idx, sel_idx].set(y)
        return processed + x

    def _L2_gnn_ref(x, edge_index, W1l, b1, W1r, W2l, b2, W2r):
        import jax, jax.numpy as jnp
        import numpy as np
        N = 50000
        E = 25000
        IN, HID, OUT = (256, 512, 256)
        src, dst = (edge_index[0], edge_index[1])
        n = x.shape[0]
        deg = jax.ops.segment_sum(jnp.ones((src.shape[0],), x.dtype), dst, num_segments=n)
        inv_deg = 1.0 / jnp.maximum(deg, 1.0)

        def sage(h, Wl, b, Wr):
            agg = jax.ops.segment_sum(h[src], dst, num_segments=n) * inv_deg[:, None]
            return agg @ Wl.T + b + h @ Wr.T
        h = jax.nn.relu(sage(x, W1l, b1, W1r))
        z = sage(h, W2l, b2, W2r)
        return z

    def _L2_ffn_ref(x, W_gat, att_src, att_dst, b_gat, ln_gamma, ln_beta, W1, b1, W2, b2, edge_index):
        import jax, jax.numpy as jnp
        import numpy as np
        B, N, D = (16, 128, 256)
        NUM_EXPERTS, TOP_K, HEADS = (4, 2, 4)
        N_EDGES = 32768
        LN_EPS = 1e-05

        def _layernorm(x, g, b):
            mu = x.mean(-1, keepdims=True)
            var = ((x - mu) ** 2).mean(-1, keepdims=True)
            return (x - mu) * jax.lax.rsqrt(var + LN_EPS) * g + b

        def _forward(x, edge_index, W_gat, att_src, att_dst, b_gat, ln_gamma, ln_beta, W1, b1, W2, b2):
            Bc, Nc, Dc = x.shape
            M = Bc * Nc
            x_flat = x.reshape(M, Dc)
            h = (x_flat @ W_gat).reshape(M, HEADS, NUM_EXPERTS)
            loops = jnp.arange(M, dtype=edge_index.dtype)
            src = jnp.concatenate([edge_index[0], loops])
            dst = jnp.concatenate([edge_index[1], loops])
            a_src = (h * att_src).sum(-1)
            a_dst = (h * att_dst).sum(-1)
            e = jax.nn.leaky_relu(a_src[src] + a_dst[dst], negative_slope=0.2)
            e_max = jax.ops.segment_max(e, dst, num_segments=M)
            ee = jnp.exp(e - e_max[dst])
            denom = jax.ops.segment_sum(ee, dst, num_segments=M)
            alpha = ee / (denom[dst] + 1e-16)
            msg = h[src] * alpha[:, :, None]
            agg = jax.ops.segment_sum(msg, dst, num_segments=M).reshape(M, HEADS * NUM_EXPERTS) + b_gat
            scores = _layernorm(agg, ln_gamma, ln_beta).reshape(M, HEADS, NUM_EXPERTS).mean(1)
            scores = scores.reshape(Bc, Nc, NUM_EXPERTS)
            topk_s, topk_i = jax.lax.top_k(scores, TOP_K)
            w = jax.nn.softmax(topk_s, axis=-1)
            out = jnp.zeros_like(x)
            for ei in range(NUM_EXPERTS):
                g = jnp.where(topk_i == ei, w, 0.0).sum(-1)
                hh = jax.nn.gelu(x @ W1[ei] + b1[ei], approximate=False)
                out = out + g[..., None] * (hh @ W2[ei] + b2[ei])
            return out
        return _forward(x, edge_index, W_gat, att_src, att_dst, b_gat, ln_gamma, ln_beta, W1, b1, W2, b2)

    def _L3_gnn_ref(x, W, b, edge_index):
        import jax, jax.numpy as jnp
        import numpy as np
        N_NODES = 3125
        N_EDGES = 50000
        IN_DIM = 256
        OUT_DIM = 256
        num_nodes = x.shape[0]
        src, tgt = (edge_index[0], edge_index[1])
        xt = jnp.einsum('ni,oi->no', x, W) + b
        out = jax.ops.segment_sum(xt[src], tgt, num_segments=num_nodes)
        deg = jax.ops.segment_sum(jnp.ones_like(tgt, dtype=x.dtype), tgt, num_segments=num_nodes)
        out = out / (deg + 1.0)[:, None]
        return out

    def _L3_ffn_ref(x, gate_w, gate_b, w1, b1, w2, b2, gamma, beta):
        import jax, jax.numpy as jnp
        import numpy as np
        B, S, H, F, E, K = (8, 128, 256, 512, 16, 2)
        EPS = 1e-05
        gate_logits = x @ gate_w + gate_b
        topk_vals, topk_idx = jax.lax.top_k(gate_logits, K)
        topk_w = jax.nn.softmax(topk_vals, axis=-1)
        h = jax.nn.relu(jnp.einsum('bsh,ehf->bsef', x, w1) + b1)
        expert_out = jnp.einsum('bsef,efh->bseh', h, w2) + b2
        sel = jnp.take_along_axis(expert_out, topk_idx[:, :, :, None], axis=2)
        moe = jnp.sum(topk_w[..., None] * sel, axis=2)
        y = x + moe
        mu = jnp.mean(y, axis=-1, keepdims=True)
        var = jnp.var(y, axis=-1, keepdims=True)
        return (y - mu) / jnp.sqrt(var + EPS) * gamma + beta
    edge_index = jnp.stack([src, dst])
    x = x + _L0_gnn_ref(_layernorm(x, axis=-1), edge_index, L0_gnn_eps, L0_gnn_W1, L0_gnn_b1, L0_gnn_g1, L0_gnn_beta1, L0_gnn_W2, L0_gnn_b2, L0_gnn_g2, L0_gnn_beta2, L0_gnn_W3, L0_gnn_b3, L0_gnn_g3, L0_gnn_beta3, L0_gnn_W4, L0_gnn_b4)
    x = x + _L0_ffn_ref(_layernorm(x, axis=-1)[None], L0_ffn_router_w1, L0_ffn_router_b1, L0_ffn_router_w2, L0_ffn_router_b2, L0_ffn_expert_w1, L0_ffn_expert_b1, L0_ffn_expert_w2, L0_ffn_expert_b2, L0_ffn_expert_w3, L0_ffn_expert_b3)[0]
    x = x + _L1_gnn_ref(_layernorm(x, axis=-1), edge_weight, L1_gnn_kernel, L1_gnn_bias, src, dst)
    x = x + _L1_ffn_ref(_layernorm(x, axis=-1)[None], L1_ffn_attention_mask, L1_ffn_wr, L1_ffn_br, L1_ffn_w1, L1_ffn_b1, L1_ffn_w2, L1_ffn_b2)[0]
    x = x + _L2_gnn_ref(_layernorm(x, axis=-1), edge_index, L2_gnn_W1l, L2_gnn_b1, L2_gnn_W1r, L2_gnn_W2l, L2_gnn_b2, L2_gnn_W2r)
    x = x + _L2_ffn_ref(_layernorm(x, axis=-1)[None], L2_ffn_W_gat, L2_ffn_att_src, L2_ffn_att_dst, L2_ffn_b_gat, L2_ffn_ln_gamma, L2_ffn_ln_beta, L2_ffn_W1, L2_ffn_b1, L2_ffn_W2, L2_ffn_b2, L2_ffn_edge_index)[0]
    x = x + _L3_gnn_ref(_layernorm(x, axis=-1), L3_gnn_W, L3_gnn_b, edge_index)
    x = x + _L3_ffn_ref(_layernorm(x, axis=-1)[None], L3_ffn_gate_w, L3_ffn_gate_b, L3_ffn_w1, L3_ffn_b1, L3_ffn_w2, L3_ffn_b2, L3_ffn_gamma, L3_ffn_beta)[0]
    return x

_drawn_inputs = setup_inputs


def setup_inputs(seed=0):
    import zlib

    import numpy as np

    out = dict(_drawn_inputs(seed))
    spreads = {'L0_gnn_b1': (0.0, 2.0),
     'L0_gnn_g1': (1.0, 0.2),
     'L0_gnn_beta1': (0.0, 0.293),
     'L0_gnn_b2': (0.0, 2.0),
     'L0_gnn_g2': (1.0, 0.2),
     'L0_gnn_beta2': (0.0, 0.293),
     'L0_gnn_b3': (0.0, 2.0),
     'L0_gnn_g3': (1.0, 0.2),
     'L0_gnn_beta3': (0.0, 0.1),
     'L0_gnn_b4': (0.0, 0.1),
     'L0_ffn_router_b1': (0.0, 0.295),
     'L0_ffn_router_b2': (0.0, 0.1),
     'L0_ffn_expert_b1': (0.0, 0.528),
     'L0_ffn_expert_b2': (0.0, 0.1),
     'L0_ffn_expert_b3': (0.0, 0.1),
     'L1_gnn_bias': (0.0, 0.1),
     'L1_ffn_b1': (0.0, 0.8),
     'L1_ffn_b2': (0.0, 0.8),
     'L2_gnn_b1': (0.0, 1.58),
     'L2_gnn_b2': (0.0, 1.021),
     'L2_ffn_b_gat': (0.0, 0.47),
     'L2_ffn_ln_gamma': (1.0, 0.6),
     'L2_ffn_ln_beta': (0.0, 2.0),
     'L2_ffn_b1': (0.0, 1.795),
     'L2_ffn_b2': (0.0, 1.32),
     'L3_gnn_b': (0.0, 1.047),
     'L3_ffn_gate_b': (0.0, 0.595),
     'L3_ffn_b1': (0.0, 2.0),
     'L3_ffn_b2': (0.0, 2.0),
     'L3_ffn_gamma': (1.0, 0.6),
     'L3_ffn_beta': (0.0, 1.232)}
    factors = {'L1_ffn_wr': 8.0,
     'L1_ffn_w1': 8.0,
     'L1_ffn_w2': 8.0,
     'L2_ffn_att_src': 36.481,
     'L2_ffn_att_dst': 182.663,
     'L3_gnn_W': 13.985,
     'L3_ffn_gate_w': 2.949,
     'L3_ffn_w1': 4.64,
     'L3_ffn_w2': 3.721,
     'L2_gnn_W1l': 4.038,
     'L2_gnn_W1r': 2.805}
    for name, (base, spread) in spreads.items():
        noise = np.random.default_rng([zlib.crc32(name.encode()), seed]).standard_normal(out[name].shape)
        drawn = base * np.exp(spread * noise) if base else spread * noise
        out[name] = jnp.asarray(drawn.astype(out[name].dtype))
    for name, factor in factors.items():
        out[name] = (out[name] * factor).astype(out[name].dtype)
    return out
```

```python
from contextlib import ExitStack

import numpy as np
import concourse.bass as bass
import concourse.mybir as mybir

F32 = mybir.dt.float32
I32 = mybir.dt.int32
U32 = mybir.dt.uint32
ALU = mybir.AluOpType
ACT = mybir.ActivationFunctionType
AX = mybir.AxisListType

N = 3125
P = 125
NT = N // P
D = 256
DK = D // 128
LANES = 128
GROUP = 8
STEP = 2 * GROUP
RING = 4
QUADS = 2 * RING
E_MAIN = 50000
E_GAT = 32768
CHUNK = 4 * P
FULL = N // CHUNK
CHUNKS = [(c * CHUNK, min(CHUNK, N - c * CHUNK)) for c in range(FULL + 1)]
ROUND = 12582912.0
EPS = 1e-5
BIG = 1e30


def edge_tiles(edges):
    most = (edges + NT * (LANES - 1)) // LANES
    return -(-most // (RING * GROUP)) * (RING * GROUP)


T_MAIN = edge_tiles(E_MAIN)
T_GAT = edge_tiles(E_GAT)

X_AT = 0
Y_AT = X_AT + NT * D
ACC_AT = Y_AT + NT * D
YT_AT = ACC_AT + NT * D
TMP_AT = YT_AT + DK * N
REC_MAIN = 4 * T_MAIN
REC_GAT = 4 * T_GAT
ARENA = TMP_AT + 8 * N
REC_AT = ARENA - 2 * REC_MAIN - REC_GAT
EARLY_AT = REC_AT - (LANES + 2 * T_MAIN)


class Steps:

    def __init__(self, eng, sem):
        self.eng, self.sem, self.n, self.turn = eng, sem, 0, 0

    def done(self, ins):
        ins.then_inc(self.sem, 1)
        self.n += 1

    def then(self, ins):
        self.done(ins)
        self.eng.wait_ge(self.sem, self.turn + self.n)

    def enter(self, i, each):
        self.first, self.each, self.turn = self.n, each, i * each

    def leave(self, turns):
        assert self.n == self.first + self.each, (self.n - self.first, self.each)
        self.n, self.turn = self.first + self.each * turns, 0


class PoolDma:

    def __init__(self, nc, ctx):
        self.sems = [ctx.enter_context(nc.semaphore(f"pool_dma{h}")) for h in range(RING)]
        self.base = [0] * RING

    def wait(self, eng, h, dmas):
        eng.wait_ge(self.sems[h], dmas * 16 + self.base[h])

    def finished(self, h, dmas):
        self.base[h] += 16 * dmas


class Phase:

    cleared = []

    def __init__(self, nc, name):
        self.nc, self.name, self.ctx = nc, name, ExitStack()

        self.sems = []

    def __enter__(self):
        self.ctx.__enter__()
        return self

    def __exit__(self, *e):
        self.ctx.__exit__(*e)
        if e[0] is None:
            for s in Phase.cleared:
                self.nc.release_semaphore(s)
            for s in self.sems:
                self.nc.gpsimd.sem_clear(s)
            Phase.cleared = self.sems

    def sem(self, name):
        self.sems.append(self.nc.alloc_semaphore(f"{self.name}_{name}"))
        return self.sems[-1]

    def psum(self, name, shape):
        return self.ctx.enter_context(self.nc.psum_tensor(f"{self.name}_{name}", shape, F32))

    def block(self):
        return self.ctx.enter_context(self.nc.Block())


class Arena:

    def __init__(self, tensor, at, end=ARENA):
        self.t, self.at, self.end = tensor, at, end

    def take(self, *shape, rows=LANES, dtype=None):
        words = int(np.prod(shape))
        assert self.at + words <= self.end, (self.at, words, self.end)
        v = self.t[0:rows, self.at:self.at + words]
        self.at += words
        if dtype is not None:
            v = v.bitcast(dtype)
        if len(shape) == 2:
            v = v.rearrange("p (a b) -> p a b", a=shape[0])
        elif len(shape) == 3:
            v = v.rearrange("p (a b c) -> p a b c", a=shape[0], b=shape[1])
        return v


def over(ap, n):
    return ap.unsqueeze(2).to_broadcast([ap.shape[0], ap.shape[1], n])


def across(ap, n):
    return ap.unsqueeze(1).to_broadcast([ap.shape[0], n, ap.shape[1]])


def constants(nc, ctx, arena):
    def sb(name, shape):
        return ctx.enter_context(nc.sbuf_tensor(name, shape, F32))[:, :]

    a, early = Arena(arena, 0), Arena(arena, EARLY_AT)
    c = {
        "ident": sb("ident", [LANES, LANES]),
        "ones": sb("ones", [LANES, LANES]),
        "before": early.take(LANES),
        "after": sb("after", [LANES, LANES]),
        "lane": sb("lane", [LANES, LANES]),
        "tile": early.take(T_MAIN),
        "bucket_of": early.take(T_MAIN, rows=P),
        "pool_dma": PoolDma(nc, ctx),
        "lane_i": a.take(LANES, dtype=I32),
        "tile_i": a.take(T_MAIN, dtype=I32),
    }
    with Phase(nc, "const") as ph:
        s = ph.sem("set")
        block = ph.block()

        @block.gpsimd
        def _(pool):
            st = Steps(pool, s)
            pool.memset(c["ident"], 0.0).then_inc(s, 1)
            pool.memset(c["ones"], 1.0).then_inc(s, 1)
            pool.memset(c["before"], 0.0).then_inc(s, 1)
            pool.iota(c["lane_i"], pattern=[[1, LANES]], base=0, channel_multiplier=0).then_inc(s, 1)
            pool.iota(c["tile_i"], pattern=[[1, T_MAIN]], base=0, channel_multiplier=0).then_inc(s, 1)
            st.n = 5
            pool.wait_ge(s, 5)
            st.done(pool.affine_select(out=c["ident"], in_=c["ident"], compare_op=ALU.not_equal, fill=1.0,
                                       base=0, pattern=[[-1, LANES]], channel_multiplier=1))
            st.done(pool.affine_select(out=c["before"], in_=c["before"], compare_op=ALU.is_ge, fill=1.0,
                                       base=0, pattern=[[-1, LANES]], channel_multiplier=1))
            st.done(pool.affine_select(out=c["after"], in_=c["ones"], compare_op=ALU.is_ge, fill=0.0,
                                       base=-1, pattern=[[-1, LANES]], channel_multiplier=1))
            pool.wait_ge(s, 8)

        @block.vector
        def _(dve):
            dve.wait_ge(s, 5)
            dve.tensor_copy(c["lane"], c["lane_i"])
            dve.tensor_copy(c["tile"], c["tile_i"])
    return c


def bucket_sort(nc, name, c, arena, key, other, weight, parts, tiles, place_scale, table, places, places_all):
    n_each = key.shape[0] // parts
    a = Arena(arena, 0)
    key_i = a.take(n_each, rows=parts, dtype=I32)
    oth_i = a.take(n_each, rows=parts, dtype=I32)
    wgt = a.take(n_each, rows=parts)
    key_f = a.take(n_each, rows=parts)
    bucket = a.take(n_each, rows=parts)
    slot_f = a.take(n_each, rows=parts)
    slot_i = a.take(n_each, rows=parts, dtype=I32)
    rec = a.take(n_each, 4, rows=parts)
    hot = a.take(NT, n_each, rows=parts)
    run = a.take(2, n_each, rows=parts)
    pads = a.take(tiles, 4)
    total = a.take(NT, rows=parts)
    count = a.take(NT)
    tiles_of = a.take(NT)
    upto = a.take(NT)
    first = a.take(NT)
    cmp = a.take(tiles, NT)
    place_f = a.take(tiles)
    rec_ring = a.take(2, GROUP, 4, rows=parts)
    slot_ring = a.take(2, GROUP, rows=parts, dtype=I32)
    bodies = n_each // STEP
    assert bodies * STEP == n_each and parts * n_each == key.shape[0]

    with Phase(nc, name) as ph:
        loaded = ph.sem("edges_loaded")
        step = ph.sem("dve_step")
        counted = ph.sem("counted")
        padded = ph.sem("pads_set")
        table_clear = ph.sem("table_clear")
        slots_ready = ph.sem("slots_ready")
        turns = ph.sem("pool_turns")
        ring_ready = [ph.sem(f"ring_ready{h}") for h in range(2)]
        scattered = c["pool_dma"]
        ps = ph.psum("sums", [LANES, 2, 512])
        block = ph.block()

        @block.sync
        def _(sp):
            view = lambda v: v.rearrange("(p i) -> p i", p=parts)
            sp.dma_start(key_i, view(key)).then_inc(loaded, 16)
            sp.dma_start(oth_i, view(other)).then_inc(loaded, 16)
            if weight is not None:
                sp.dma_start(wgt, view(weight)).then_inc(loaded, 16)
            sp.wait_ge(padded, 1)
            sp.dma_start(table.rearrange("(p t) c -> p (t c)", p=LANES),
                         pads.rearrange("p t c -> p (t c)")).then_inc(table_clear, 16)
            sp.wait_ge(table_clear, 16)

        @block.vector
        def _(dve):
            st = Steps(dve, step)
            dve.memset(pads, 0.0).then_inc(step, 1)
            st.n = 1
            dve.wait_ge(step, 1)
            dve.memset(pads[:, :, 1], -1.0).then_inc(padded, 1)
            dve.wait_ge(loaded, 32 if weight is None else 48)
            st.then(dve.tensor_copy(key_f, key_i))
            st.then(dve.tensor_scalar(bucket, key_f, -float(P // 2), 1.0 / P, ALU.add, ALU.mult))
            st.then(dve.tensor_scalar_add(bucket, bucket, ROUND))
            st.then(dve.tensor_scalar_add(bucket, bucket, -ROUND))
            st.done(dve.tensor_copy(rec[:, :, 0].bitcast(I32), oth_i))
            st.done(dve.tensor_copy(rec[:, :, 3].bitcast(I32), key_i))
            if weight is None:
                st.done(dve.memset(rec[:, :, 2], 0.0))
            else:
                st.done(dve.tensor_copy(rec[:, :, 2], wgt))
            st.done(dve.scalar_tensor_tensor(rec[:, :, 1], bucket, -float(P), key_f, ALU.mult, ALU.add))
            with dve.Fori(0, NT) as b:
                dve.tensor_scalar(hot[:, bass.ds(b, 1), :].rearrange("p a i -> p (a i)"), bucket,
                                  c["lane"][0:parts, bass.ds(b, 1)], None, ALU.is_equal, ALU.add,
                                  accum_out=total[:, bass.ds(b, 1)]).then_inc(step, 1)
            st.n += NT
            dve.wait_ge(counted, 1)
            st.then(dve.tensor_copy(count, ps[:, 0, 0:NT]))
            st.then(dve.tensor_scalar(tiles_of, count, LANES / 2 - 0.5, 1.0 / LANES, ALU.add, ALU.mult))
            st.then(dve.tensor_scalar_add(tiles_of, tiles_of, ROUND))
            st.then(dve.tensor_scalar_add(tiles_of, tiles_of, -ROUND))
            st.then(dve.tensor_tensor_scan(upto, c["ones"][:, 0:NT], tiles_of, 0.0, ALU.mult, ALU.add))
            st.then(dve.tensor_tensor(first, upto, tiles_of, ALU.subtract))
            st.then(dve.tensor_scalar(first, first, float(LANES), -1.0, ALU.mult, ALU.add))
            st.then(dve.tensor_tensor(first[0:parts], first[0:parts], ps[0:parts, 1, 0:NT], ALU.add))
            each = 2
            with dve.Fori(0, NT) as b:
                st.enter(b, each)
                row = hot[:, bass.ds(b, 1), :].rearrange("p a i -> p (a i)")
                st.then(dve.tensor_tensor_scan(run[:, 0, :], c["ones"][0:parts, 0:1].to_broadcast([parts, n_each]),
                                               row, first[0:parts, bass.ds(b, 1)], ALU.mult, ALU.add))
                st.then(dve.tensor_tensor(row, row, run[:, 0, :], ALU.mult))
            st.leave(NT)
            st.then(dve.tensor_reduce(slot_f, hot.rearrange("p b i -> p i b"), AX.X, ALU.add))
            dve.tensor_copy(slot_i, slot_f).then_inc(slots_ready, 1)
            for rows, out, scale in ((1, places, float(place_scale)), (P, places_all, 1.0)):
                if out is None:
                    continue
                st.then(dve.tensor_tensor(cmp[0:rows], across(upto[0:rows], tiles),
                                          over(c["tile"][0:rows, 0:tiles], NT), ALU.is_le))
                st.then(dve.tensor_reduce(place_f[0:rows], cmp[0:rows], AX.X, ALU.add))
                st.then(dve.tensor_scalar(out, place_f[0:rows], float(NT - 1), scale, ALU.min, ALU.mult))

        @block.tensor
        def _(pe):
            pe.wait_ge(step, 1 + 8 + NT)
            pe.matmul(ps[:, 0, 0:NT], c["ones"][0:parts, :], total, start=True, stop=True)
            pe.matmul(ps[:, 1, 0:NT], c["before"][0:parts, :], total, start=True, stop=True).then_inc(counted, 1)

        @block.scalar
        def _(act):
            act.wait_ge(slots_ready, 1)

            def copy_group(g, h):
                act.copy(rec_ring[:, h, :, :], rec[:, bass.ds(g * GROUP, GROUP), :])
                act.copy(slot_ring[:, h, :], slot_i[:, bass.ds(g * GROUP, GROUP)]).then_inc(ring_ready[h], 1)

            for h in range(2):
                copy_group(h, h)
            with act.Fori(1, bodies) as i:
                for h in range(2):
                    scattered.wait(act, h, i * GROUP)
                    copy_group(i * 2 + h, h)

        @block.gpsimd
        def _(pool):
            pool.wait_ge(table_clear, 16)
            with pool.Fori(0, bodies) as i:
                for h in range(2):
                    pool.wait_ge(ring_ready[h], i + 1)
                    pool.sem_inc(turns, 1)
                    for j in range(GROUP):
                        pool.indirect_dma_start(
                            table, bass.IndirectOffsetOnAxis(ap=slot_ring[:, h, j:j + 1].bitcast(U32), axis=0),
                            rec_ring[:, h, j, :], None).then_inc(scattered.sems[h], 16)
            for h in range(2):
                scattered.wait(pool, h, GROUP * bodies)
                scattered.finished(h, GROUP * bodies)


def load_records(nc, name, loads):
    with Phase(nc, name) as ph:
        s = ph.sem("loaded")
        block = ph.block()

        @block.sync
        def _(sp):
            for view, table in loads:
                sp.dma_start(view, table.rearrange("(t p) c -> p t c", p=LANES)).then_inc(s, 16)
            sp.wait_ge(s, 16 * len(loads))


def graph_sum(nc, name, c, arena, rows, rec, places, acc, tiles, weighted, degree=None, places_all=None):
    a = Arena(arena, TMP_AT, REC_AT)
    msg = a.take(RING, GROUP, D)
    hot = a.take(RING, GROUP, P)
    idx = a.take(RING, GROUP, dtype=I32)
    mark = a.take(tiles) if degree is not None else None
    bodies = tiles // (RING * GROUP)
    with Phase(nc, name) as ph:
        turns = ph.sem("pool_turns")
        idx_ready = [ph.sem(f"idx_ready{h}") for h in range(RING)]
        gathered = c["pool_dma"]
        hot_ready = [ph.sem(f"hot_ready{h}") for h in range(RING)]
        summed = ph.sem("quads_summed")
        freed = ph.sem("psum_freed")
        step = ph.sem("dve_step")
        ps = ph.psum("sum", [LANES, 2, 4, D])
        ps_deg = ph.psum("deg", [LANES, 512]) if degree is not None else None
        block = ph.block()

        @block.scalar
        def _(act):
            with act.Fori(0, bodies) as i:
                for h in range(RING):
                    act.wait_ge(summed, i * QUADS + (2 * h + 2))
                    act.copy(idx[:, h, :], rec[:, bass.ds((i * RING + h) * GROUP, GROUP), 0].bitcast(I32))\
                       .then_inc(idx_ready[h], 1)

        @block.gpsimd
        def _(pool):
            with pool.Fori(0, bodies) as i:
                for h in range(RING):
                    pool.wait_ge(idx_ready[h], i + 1)
                    pool.sem_inc(turns, 1)
                    for j in range(GROUP):
                        pool.indirect_dma_start(
                            msg[:, h, j, :], None, rows,
                            bass.IndirectOffsetOnAxis(ap=idx[:, h, j:j + 1].bitcast(U32), axis=0))\
                            .then_inc(gathered.sems[h], 16)

        @block.tensor
        def _(pe):
            pe.sem_inc(summed, QUADS)
            with pe.Fori(0, bodies) as i:
                for h in range(RING):
                    pe.wait_ge(hot_ready[h], i + 1)
                    gathered.wait(pe, h, i * GROUP + GROUP)
                    for q in range(2):
                        pe.wait_ge(freed, i * QUADS + (2 * h + q + 1))
                        for j in range(4):
                            t = 4 * q + j
                            if degree is not None:
                                col = (i * RING + h) * GROUP + t
                                pe.matmul(ps_deg[0:P, bass.ds(col, 1)], hot[:, h, t, :], c["ones"][:, 0:1],
                                          start=True, stop=True)
                            last = pe.matmul(ps[0:P, q, j, :], hot[:, h, t, :], msg[:, h, t, :],
                                             start=True, stop=True)
                        last.then_inc(summed, 1)

        for h in range(RING):
            gathered.finished(h, GROUP * bodies)

        @block.vector
        def _(dve):
            st = Steps(dve, step)
            dve.sem_inc(freed, 2)
            st.then(dve.memset(acc, 0.0))
            each = RING * GROUP + (RING if weighted else 0)
            with dve.Fori(0, bodies) as i:
                st.enter(i, each)
                for h in range(RING):
                    dve.wait_ge(summed, i * QUADS + (2 * h + 2))
                    of = rec[:, bass.ds((i * RING + h) * GROUP, GROUP), :]
                    hit = dve.tensor_tensor(hot[:, h, :, :], over(of[:, :, 1], P), across(c["lane"][:, 0:P], GROUP),
                                            ALU.is_equal)
                    if weighted:
                        st.then(hit)
                        hit = dve.tensor_tensor(hot[:, h, :, :], hot[:, h, :, :], over(of[:, :, 2], P), ALU.mult)
                    hit.then_inc(hot_ready[h], 1)
                for h in range(RING):
                    _, place = nc.values_load_multi_w_load_instructions(
                        places[0:1, bass.ds((i * RING + h) * GROUP, GROUP)], engines=(mybir.EngineType.DVE,),
                        min_val=0, max_val=(NT - 1) * D)
                    for q in range(2):
                        dve.wait_ge(summed, i * QUADS + (QUADS + 2 * h + q + 1))
                        for j in range(4):
                            to = acc[:, bass.ds(place[4 * q + j], D)]
                            st.then(dve.tensor_tensor(to, to, ps[0:P, q, j, :], ALU.add))
                        dve.sem_inc(freed, 1)
            st.leave(bodies)
            if degree is not None:
                with dve.Fori(0, NT) as b:
                    st.enter(b, 2)
                    st.then(dve.tensor_scalar(mark[0:P], places_all, c["lane"][0:P, bass.ds(b, 1)], None,
                                              ALU.is_equal))
                    st.then(dve.scalar_tensor_tensor(mark[0:P], mark[0:P], 1.0, ps_deg[0:P, 0:tiles], ALU.mult,
                                                     ALU.mult, accum_out=degree[:, bass.ds(b, 1)]))
                st.leave(NT)


OUT_BANKS = 4


def quads():
    return [(t, min(4, NT - t)) for t in range(0, NT, 4)]


def flat(ap):
    return ap.rearrange("p a b -> p (a b)")


def to_features(nc, name, c, arena, y, yt, prepare, table=None, loads=(), roots=None):
    with Phase(nc, name) as ph:
        loaded = ph.sem("loaded")
        step = ph.sem("dve_step")
        quad_ready = ph.sem("quad_ready")
        transposed = ph.sem("transposed")
        copied = ph.sem("copied")
        stored = ph.sem("stored")
        asked = ph.sem("root_asked")
        rooted = ph.sem("root_ready")
        ps = ph.psum("t", [LANES, 8, 512])
        block = ph.block()

        @block.sync
        def _(sp):
            for to, of in loads:
                sp.dma_start(to, of).then_inc(loaded, 16)
            if table is not None:
                rows = table.rearrange("(t p) d -> p t d", p=P)
                for q, (t, n) in enumerate(quads()):
                    sp.wait_ge(quad_ready, q + 1)
                    sp.dma_start(rows[:, t:t + n, :], y[:, t:t + n, :]).then_inc(stored, 16)
                sp.wait_ge(stored, 16 * len(quads()))

        @block.vector
        def _(dve):
            st = Steps(dve, step)
            if loads:
                dve.wait_ge(loaded, 16 * len(loads))
            prepare(dve, st, quad_ready, asked, rooted)

        @block.tensor
        def _(pe):
            for q, (t, n) in enumerate(quads()):
                pe.wait_ge(quad_ready, q + 1)
                for k in range(DK):
                    u = DK * q + k
                    if u >= 8:
                        pe.wait_ge(copied, u - 7)
                    for j in range(n):
                        last = pe.transpose(ps[:, u % 8, j * P:(j + 1) * P],
                                            y[:, t + j, k * LANES:(k + 1) * LANES], c["ident"][0:P, 0:P])
                    last.then_inc(transposed, 1)

        @block.scalar
        def _(act):
            if roots is not None:
                act.wait_ge(asked, 1)
                act.activation(roots, roots, ACT.Sqrt).then_inc(rooted, 1)
            for q, (t, n) in enumerate(quads()):
                for k in range(DK):
                    u = DK * q + k
                    act.wait_ge(transposed, u + 1)
                    act.copy(yt[:, k, t * P:(t + n) * P], ps[:, u % 8, 0:n * P]).then_inc(copied, 1)


def row_statistics(dve, st, x, stats, mean, root, spare):
    with dve.Fori(0, NT) as t:
        dve.bn_stats(stats[:, bass.ds(t, 1), :].rearrange("p a b -> p (a b)"),
                     x[:, bass.ds(t, 1), :].rearrange("p a b -> p (a b)")).then_inc(st.sem, 1)
    st.n += NT
    st.eng.wait_ge(st.sem, st.n)
    half = D // 2
    st.then(dve.tensor_tensor(mean, stats[:, :, 1], stats[:, :, 4], ALU.add))
    st.then(dve.tensor_scalar_mul(mean, mean, 0.5))
    st.then(dve.tensor_tensor(spare, stats[:, :, 1], mean, ALU.subtract))
    st.then(dve.tensor_tensor(spare, spare, spare, ALU.mult))
    st.then(dve.tensor_tensor(root, stats[:, :, 2], stats[:, :, 5], ALU.add))
    st.then(dve.scalar_tensor_tensor(root, root, 1.0 / (2 * half), spare, ALU.mult, ALU.add))
    return dve.tensor_scalar_add(root, root, EPS)


def layer_norm(nc, name, c, arena, x, y, yt, table=None, loads=()):
    a = Arena(arena, TMP_AT)
    stats = a.take(NT, 6, rows=P)
    mean, root, spare = (a.take(NT, rows=P) for _ in range(3))

    def prepare(dve, st, quad_ready, asked, rooted):
        row_statistics(dve, st, x, stats, mean, root, spare).then_inc(asked, 1)
        dve.wait_ge(rooted, 1)
        st.then(dve.reciprocal(root, root))
        for t, n in quads():
            part = y[:, t:t + n, :]
            st.then(dve.tensor_tensor(part, x[:, t:t + n, :], over(mean[:, t:t + n], D), ALU.subtract))
            dve.tensor_tensor(part, part, over(root[:, t:t + n], D), ALU.mult).then_inc(quad_ready, 1)

    to_features(nc, name, c, arena, y, yt, prepare, table, loads, roots=root)


def dense(nc, name, products, bias, out, func, stats=None):
    m = out.shape[1]
    with Phase(nc, name) as ph:
        loaded = ph.sem("weights_loaded")
        multiplied = ph.sem("multiplied")
        written = ph.sem("written")
        free = ph.sem("psum_free")
        counted = ph.sem("stats_done")
        ps = ph.psum("out", [LANES, m, 512])
        block = ph.block()

        @block.sync
        def _(sp):
            for _, w, w_dram in products:
                sp.dma_start(w, w_dram.rearrange("(k p) f -> p k f", p=LANES)).then_inc(loaded, 16)

        @block.tensor
        def _(pe):
            pe.wait_ge(loaded, 16 * len(products) + 16)

            def chunk(n, at, cols):
                for fo in range(m):
                    pe.wait_ge(free, n * m + (fo + 1))
                    parts = [(rhs, w, k) for rhs, w, _ in products for k in range(w.shape[1])]
                    for i, (rhs, w, k) in enumerate(parts):
                        last = pe.matmul(ps[:, fo, 0:cols], w[:, k, fo * LANES:(fo + 1) * LANES],
                                         rhs[:, k, bass.ds(at, cols)], start=(i == 0), stop=(i == len(parts) - 1))
                    last.then_inc(multiplied, 1)

            with pe.Fori(0, FULL) as n:
                chunk(n, n * CHUNK, CHUNK)
            chunk(FULL, FULL * CHUNK, N - FULL * CHUNK)

        @block.scalar
        def _(act):
            with nc.allow_non_contiguous_dma(reason="a column of biases"):
                act.dma_start(bias[0], bias[1].rearrange("(m p) -> p m", p=LANES)).then_inc(loaded, 16)
            act.wait_ge(loaded, 16 * len(products) + 16)
            act.sem_inc(free, m)

            def chunk(n, at, cols):
                for fo in range(m):
                    act.wait_ge(multiplied, n * m + (fo + 1))
                    act.activation(out[:, fo, bass.ds(at, cols)], ps[:, fo, 0:cols], func,
                                   bias=bias[0][:, fo:fo + 1]).then_inc(free, 1)

            with act.Fori(0, FULL) as n:
                chunk(n, n * CHUNK, CHUNK)
            chunk(FULL, FULL * CHUNK, N - FULL * CHUNK)

        @block.vector
        def _(dve):
            if stats is None:
                return

            def chunk(n, at, cols):
                for fo in range(m):
                    dve.wait_ge(free, n * m + (m + fo + 1))
                    dve.bn_stats(stats[:, fo, bass.ds(n * 6, 6)], out[:, fo, bass.ds(at, cols)])

            with dve.Fori(0, FULL) as n:
                chunk(n, n * CHUNK, CHUNK)
            chunk(FULL, FULL * CHUNK, N - FULL * CHUNK)


def batch_norm_elu(nc, name, a, h, stats, gamma, beta):
    m = h.shape[1]
    mv = a.take(m, 2)
    g, b, scale, shift = (a.take(m) for _ in range(4))
    e = a.take(2, N)
    with Phase(nc, name) as ph:
        loaded = ph.sem("loaded")
        step = ph.sem("dve_step")
        asked = ph.sem("root_asked")
        rooted = ph.sem("root_ready")
        scaled = ph.sem("scale_ready")
        act_step = ph.sem("act_step")
        split = ph.sem("split_ready")
        freed = ph.sem("exp_freed")
        block = ph.block()

        @block.sync
        def _(sp):
            with nc.allow_non_contiguous_dma(reason="a column of parameters"):
                sp.dma_start(g, gamma.rearrange("(m p) -> p m", p=LANES)).then_inc(loaded, 16)
                sp.dma_start(b, beta.rearrange("(m p) -> p m", p=LANES)).then_inc(loaded, 16)

        @block.vector
        def _(dve):
            st = Steps(dve, step)
            for f in range(m):
                st.done(dve.bn_aggr(mv[:, f, :], stats[:, f, :]))
            dve.wait_ge(step, m)
            dve.tensor_scalar_add(scale, mv[:, :, 1], EPS).then_inc(asked, 1)
            dve.wait_ge(rooted, 1)
            st.then(dve.reciprocal(scale, scale))
            dve.wait_ge(loaded, 32)
            st.then(dve.tensor_tensor(scale, scale, g, ALU.mult))
            st.then(dve.tensor_tensor(shift, mv[:, :, 0], scale, ALU.mult))
            dve.tensor_tensor(shift, b, shift, ALU.subtract).then_inc(scaled, 1)
            for f in range(m):
                dve.wait_ge(split, f + 1)
                st.then(dve.tensor_scalar(e[:, f % 2, :], e[:, f % 2, :], 1.0, -1.0, ALU.min, ALU.add))
                dve.tensor_tensor(h[:, f, :], h[:, f, :], e[:, f % 2, :], ALU.add).then_inc(freed, 1)

        @block.scalar
        def _(act):
            act.wait_ge(asked, 1)
            act.activation(scale, scale, ACT.Sqrt).then_inc(rooted, 1)
            act.wait_ge(scaled, 1)
            for f in range(m):
                if f >= 2:
                    act.wait_ge(freed, f - 1)
                act.activation(e[:, f % 2, :], h[:, f, :], ACT.Exp, bias=shift[:, f:f + 1],
                               scale=scale[:, f:f + 1]).then_inc(act_step, 1)
                act.wait_ge(act_step, f + 1)
                act.activation(h[:, f, :], h[:, f, :], ACT.Relu, bias=shift[:, f:f + 1],
                               scale=scale[:, f:f + 1]).then_inc(split, 1)


def project(nc, name, ht, w, w_dram, out, bias=None, add=False, loads=(), table=None):
    with Phase(nc, name) as ph:
        loaded = ph.sem("loaded")
        multiplied = ph.sem("multiplied")
        added = ph.sem("added")
        step = ph.sem("dve_step")
        stored = ph.sem("stored")
        ps = ph.psum("out", [LANES, 8, 512])
        block = ph.block()
        ks = w.shape[1]
        n_loads = 1 + (bias is not None) + len(loads)

        @block.sync
        def _(sp):
            sp.dma_start(w, w_dram.rearrange("(k p) f -> p k f", p=LANES)).then_inc(loaded, 16)
            if bias is not None:
                sp.dma_start(bias[0], bias[1].unsqueeze(0).to_broadcast([P, D])).then_inc(loaded, 16)
            for to, of in loads:
                sp.dma_start(to, of).then_inc(loaded, 16)
            if table is not None:
                rows = table.rearrange("(t p) d -> p t d", p=P)
                for t, n in quads():
                    sp.wait_ge(added, t + n)
                    sp.dma_start(rows[:, t:t + n, :], out[:, t:t + n, :]).then_inc(stored, 16)
                sp.wait_ge(stored, 16 * len(quads()))

        @block.tensor
        def _(pe):
            pe.wait_ge(loaded, 16 * n_loads)
            for t in range(NT):
                if t >= 8:
                    pe.wait_ge(added, t - 7)
                for k in range(ks):
                    last = pe.matmul(ps[0:P, t % 8, 0:D], ht[:, k, t * P:(t + 1) * P], w[:, k, :],
                                     start=(k == 0), stop=(k == ks - 1))
                last.then_inc(multiplied, 1)

        @block.vector
        def _(dve):
            st = Steps(dve, step)
            dve.wait_ge(loaded, 16 * n_loads)
            if add and bias is not None:
                st.then(dve.tensor_tensor(out, out, across(bias[0], NT), ALU.add))
            for t in range(NT):
                dve.wait_ge(multiplied, t + 1)
                if add:
                    dve.tensor_tensor(out[:, t, :], out[:, t, :], ps[0:P, t % 8, 0:D], ALU.add).then_inc(added, 1)
                elif bias is not None:
                    dve.tensor_tensor(out[:, t, :], bias[0], ps[0:P, t % 8, 0:D], ALU.add).then_inc(added, 1)
                else:
                    dve.tensor_copy(out[:, t, :], ps[0:P, t % 8, 0:D]).then_inc(added, 1)


def add_scaled(nc, name, x, acc, scale=None, bias=None):
    with Phase(nc, name) as ph:
        loaded = ph.sem("loaded")
        step = ph.sem("dve_step")
        block = ph.block()

        @block.sync
        def _(sp):
            if bias is not None:
                sp.dma_start(bias[0], bias[1].unsqueeze(0).to_broadcast([P, D])).then_inc(loaded, 16)

        @block.vector
        def _(dve):
            st = Steps(dve, step)
            if scale is not None:
                st.then(dve.tensor_tensor(acc, acc, over(scale, D), ALU.mult))
            if bias is not None:
                dve.wait_ge(loaded, 16)
                st.then(dve.tensor_tensor(acc, acc, across(bias[0], NT), ALU.add))
            st.then(dve.tensor_tensor(x, x, acc, ALU.add))


def experts(nc, name, c, a, yt, target, hidden, last_w, gates, bias_gates, last_b, count, func):
    widths = [w.shape[2] for w, _ in hidden]
    ins = [D] + widths
    w_sb = [a.take(2, ins[i] // LANES * widths[i]).rearrange("p h (k f) -> p h k f", f=widths[i])
            for i in range(len(hidden))]
    b_sb = [a.take(2, widths[i] // LANES) for i in range(len(hidden))]
    wl_sb = a.take(2, widths[-1] // LANES * D).rearrange("p h (k f) -> p h k f", f=D)
    h_sb = [a.take(2, widths[i] // LANES * CHUNK).rearrange("p h (k f) -> p h k f", f=CHUNK)
            for i in range(len(hidden))]
    gate = a.take(2, NT, rows=P)
    n_bias = bias_gates.shape[2]
    gates_t = a.take(N, rows=n_bias)
    lb_sb = a.take(D, rows=n_bias)
    turns = count // 2
    assert turns * 2 == count
    n_w = 2 * len(hidden) + 1
    stages = len(hidden) + 1
    n_ch = len(CHUNKS)
    units = [w // LANES for w in widths]

    def order():
        for at in range(n_ch + stages - 1):
            for s in range(stages):
                if 0 <= at - s < n_ch:
                    yield s, at - s

    with Phase(nc, name) as ph:
        loaded = [ph.sem(f"weights_loaded{h}") for h in range(2)]
        small_loaded = ph.sem("last_bias_loaded")
        multiplied = [ph.sem(f"multiplied{s}") for s in range(stages)]
        written = [ph.sem(f"written{s}") for s in range(stages - 1)]
        added = ph.sem("added")
        gate_ready = ph.sem("gate_ready")
        g_t = ph.sem("gates_transposed")
        g_c = ph.sem("gates_copied")
        b_m = ph.sem("bias_multiplied")
        step = ph.sem("dve_step")
        ps_h = ph.psum("hidden", [LANES, 4, 512])
        ps_o = ph.psum("out", [LANES, OUT_BANKS, 2, D])
        banks = [list(range(4))] if stages == 2 else [[0, 1], [2, 3]]
        block = ph.block()

        def hid(i, h, n, s):
            return i * (2 * n_ch * units[s]) + (h * n_ch + n) * units[s]

        pairs = [(t, min(2, NT - t)) for t in range(0, NT, 2)]
        per_turn = 2 * len(pairs)

        def last_use(u):
            return max(v for v in range(-per_turn, u) if v % per_turn % OUT_BANKS == u % OUT_BANKS) + 1 + per_turn

        @block.sync
        def _(sp):
            sp.dma_start(lb_sb, last_b).then_inc(small_loaded, 16)
            with sp.Fori(0, turns) as i:
                for h in range(2):
                    e = i * 2 + h
                    sp.wait_ge(multiplied[-1], i * per_turn + (h + 1) * len(pairs))
                    for j, (w, b) in enumerate(hidden):
                        sp.dma_start(w_sb[j][:, h, :, :],
                                     w[bass.ds(e, 1), :, :].rearrange("e (k p) f -> p (e k) f", p=LANES))\
                            .then_inc(loaded[h], 16)
                        with nc.allow_non_contiguous_dma(reason="a column of biases"):
                            sp.dma_start(b_sb[j][:, h, :], b[bass.ds(e, 1), :].rearrange("e (m p) -> p (e m)", p=LANES))\
                                .then_inc(loaded[h], 16)
                    sp.dma_start(wl_sb[:, h, :, :],
                                 last_w[bass.ds(e, 1), :, :].rearrange("e (k p) f -> p (e k) f", p=LANES))\
                        .then_inc(loaded[h], 16)

        @block.tensor
        def _(pe):
            for q, (t, n) in enumerate(quads()):
                if q >= 4:
                    pe.wait_ge(g_c, q - 3)
                for j in range(n):
                    last = pe.transpose(ps_h[0:n_bias, q % 4, j * P:(j + 1) * P], bias_gates[:, t + j, :],
                                        c["ident"][0:P, 0:P])
                last.then_inc(g_t, 1)
            pe.wait_ge(small_loaded, 16)
            for t in range(NT):
                if t % 4 == 0:
                    pe.wait_ge(g_c, t // 4 + 1)
                if t >= OUT_BANKS:
                    pe.wait_ge(step, t - OUT_BANKS + 1)
                pe.matmul(ps_o[0:P, t % OUT_BANKS, 0, :], gates_t[:, t * P:(t + 1) * P], lb_sb, start=True, stop=True)\
                    .then_inc(b_m, 1)
            pe.wait_ge(step, NT)
            pe.sem_inc(multiplied[-1], per_turn)
            with pe.Fori(0, turns) as i:
                for h in range(2):
                    pe.wait_ge(loaded[h], i * (16 * n_w) + 16 * n_w)
                    for s, n in order():
                        at, cols = CHUNKS[n]
                        if s < stages - 1:
                            if s > 0:
                                pe.wait_ge(written[s - 1], hid(i, h, n + 1, s - 1) + len(banks[s - 1]))
                            for m in range(units[s]):
                                pe.wait_ge(written[s], hid(i, h, n, s) + (m + 1))
                                ks = ins[s] // LANES
                                bank = banks[s][m % len(banks[s])]
                                for k in range(ks):
                                    rhs = yt[:, k, at:at + cols] if s == 0 else h_sb[s - 1][:, n % 2, k, 0:cols]
                                    last = pe.matmul(ps_h[:, bank, 0:cols],
                                                     w_sb[s][:, h, k, m * LANES:(m + 1) * LANES], rhs,
                                                     start=(k == 0), stop=(k == ks - 1))
                                last.then_inc(multiplied[s], 1)
                        else:
                            pe.wait_ge(written[s - 1], hid(i, h, n + 1, s - 1) + len(banks[s - 1]))
                            ks = widths[-1] // LANES
                            for u, (t, tiles) in enumerate(pairs):
                                if not 4 * n <= t < 4 * n + 4:
                                    continue
                                v = h * len(pairs) + u
                                pe.wait_ge(added, i * per_turn + last_use(v))
                                for j in range(tiles):
                                    col = (t + j - 4 * n) * P
                                    for k in range(ks):
                                        last = pe.matmul(ps_o[0:P, v % OUT_BANKS, j, :],
                                                         h_sb[s - 1][:, n % 2, k, col:col + P], wl_sb[:, h, k, :],
                                                         start=(k == 0), stop=(k == ks - 1))
                                last.then_inc(multiplied[s], 1)

        @block.scalar
        def _(act):
            for q, (t, n) in enumerate(quads()):
                act.wait_ge(g_t, q + 1)
                act.copy(gates_t[:, t * P:(t + n) * P], ps_h[0:n_bias, q % 4, 0:n * P]).then_inc(g_c, 1)
            for s in range(stages - 1):
                act.sem_inc(written[s], len(banks[s]))
            with act.Fori(0, turns) as i:
                for h in range(2):
                    act.wait_ge(loaded[h], i * (16 * n_w) + 16 * n_w)
                    for s, n in order():
                        if s == stages - 1:
                            continue
                        at, cols = CHUNKS[n]
                        for m in range(units[s]):
                            act.wait_ge(multiplied[s], hid(i, h, n, s) + (m + 1))
                            act.activation(h_sb[s][:, n % 2, m, 0:cols],
                                           ps_h[:, banks[s][m % len(banks[s])], 0:cols], func,
                                           bias=b_sb[s][:, h, m:m + 1]).then_inc(written[s], 1)

        @block.vector
        def _(dve):
            st = Steps(dve, step)
            for t in range(NT):
                dve.wait_ge(b_m, t + 1)
                st.done(dve.tensor_tensor(target[:, t, :], target[:, t, :], ps_o[0:P, t % OUT_BANKS, 0, :], ALU.add))
            dve.wait_ge(step, NT)
            dve.sem_inc(added, per_turn)
            with dve.Fori(0, turns) as i:
                dve.wait_ge(added, i * per_turn + per_turn)
                for h in range(2):
                    dve.tensor_copy(gate[:, h, :], gates[:, :, bass.ds(i * 2 + h, 1)].rearrange("p t e -> p (t e)"))\
                       .then_inc(gate_ready, 1)
                for h in range(2):
                    dve.wait_ge(gate_ready, i * 2 + 2)
                    for u, (t, tiles) in enumerate(pairs):
                        v = h * len(pairs) + u
                        dve.wait_ge(multiplied[-1], i * per_turn + (per_turn + v + 1))
                        for j in range(tiles):
                            last = dve.scalar_tensor_tensor(target[:, t + j, :], ps_o[0:P, v % OUT_BANKS, j, :],
                                                            gate[:, h, t + j:t + j + 1], target[:, t + j, :],
                                                            ALU.mult, ALU.add)
                        last.then_inc(added, 1)


def best_two(dve, st, c, scores, gates, tmp, asked, answered):
    e = scores.shape[2]
    rank, one, two, rest, m1, m2, exp, total = tmp
    pick = dve.tensor_tensor
    st.then(dve.tensor_scalar(rank, c["lane"][0:P, 0:e], -1.0, float(e), ALU.mult, ALU.add))

    def best(of, out, value):
        st.then(dve.tensor_reduce(value, of, AX.X, ALU.max))
        st.then(pick(out, of, over(value, e), ALU.is_equal))
        st.then(pick(out, out, across(rank, NT), ALU.mult))
        st.then(dve.tensor_reduce(total, out, AX.X, ALU.max))
        st.then(pick(out, out, over(total, e), ALU.is_equal))

    best(scores, one, m1)
    st.then(dve.scalar_tensor_tensor(rest, one, -BIG, scores, ALU.mult, ALU.add))
    best(rest, two, m2)
    pick(exp, m2, m1, ALU.subtract).then_inc(asked, 1)
    dve.wait_ge(answered, 1)
    st.then(dve.tensor_scalar_add(total, exp, 1.0))
    st.then(dve.reciprocal(total, total))
    st.then(pick(exp, exp, total, ALU.mult))
    st.then(pick(one, one, over(total, e), ALU.mult))
    st.then(pick(two, two, over(exp, e), ALU.mult))
    st.then(pick(gates, one, two, ALU.add))


def best_two_places(a, e):
    return (a.take(e, rows=P), a.take(NT, e, rows=P), a.take(NT, e, rows=P), a.take(NT, e, rows=P),
            a.take(NT, rows=P), a.take(NT, rows=P), a.take(NT, rows=P), a.take(NT, rows=P))


def router(nc, name, c, a, src_t, w_dram, b_dram, scores, gates=None, softmax=False):
    e = scores.shape[2]
    ks = src_t.shape[1]
    w = a.take(ks, e)
    b = a.take(e, rows=P)
    top, total = a.take(NT, rows=P), a.take(NT, rows=P)
    tmp = best_two_places(a, e) if gates is not None else None
    with Phase(nc, name) as ph:
        loaded = ph.sem("loaded")
        multiplied = ph.sem("multiplied")
        step = ph.sem("dve_step")
        soft = ph.sem("softmax_asked")
        soft_done = ph.sem("softmax_done")
        asked = ph.sem("exp_asked")
        answered = ph.sem("exp_done")
        ps = ph.psum("scores", [LANES, 512])
        view = ps[0:P, 0:NT * e].rearrange("p (t e) -> p t e", e=e)
        block = ph.block()

        @block.sync
        def _(sp):
            with nc.allow_non_contiguous_dma(reason="few scores: short rows"):
                sp.dma_start(w, w_dram.rearrange("(k p) e -> p k e", p=LANES)).then_inc(loaded, 16)
            sp.dma_start(b, b_dram.unsqueeze(0).to_broadcast([P, e])).then_inc(loaded, 16)

        @block.tensor
        def _(pe):
            pe.wait_ge(loaded, 32)
            for t in range(NT):
                for k in range(ks):
                    last = pe.matmul(view[:, t, :], src_t[:, k, t * P:(t + 1) * P], w[:, k, :],
                                     start=(k == 0), stop=(k == ks - 1))
            last.then_inc(multiplied, 1)

        @block.vector
        def _(dve):
            st = Steps(dve, step)
            dve.wait_ge(loaded, 32)
            dve.wait_ge(multiplied, 1)
            st.then(dve.tensor_tensor(scores, across(b, NT), view, ALU.add))
            if softmax:
                st.then(dve.tensor_reduce(top, scores, AX.X, ALU.max))
                dve.tensor_tensor(scores, scores, over(top, e), ALU.subtract).then_inc(soft, 1)
                dve.wait_ge(soft_done, 1)
                st.then(dve.tensor_reduce(total, scores, AX.X, ALU.add))
                st.then(dve.reciprocal(total, total))
                st.then(dve.tensor_tensor(scores, scores, over(total, e), ALU.mult))
            if gates is not None:
                best_two(dve, st, c, scores, gates, tmp, asked, answered)

        @block.scalar
        def _(act):
            if softmax:
                act.wait_ge(soft, 1)
                act.activation(scores, scores, ACT.Exp).then_inc(soft_done, 1)
            if gates is not None:
                act.wait_ge(asked, 1)
                act.activation(tmp[6], tmp[6], ACT.Exp).then_inc(answered, 1)


def choose_half(nc, name, c, a, scores, gate, row_dram, chosen):
    row = a.take(N, rows=P)
    spare = a.take(N, rows=P)
    part = a.take(4, NT, rows=P)
    rank = a.take(NT, rows=P)
    with Phase(nc, name) as ph:
        moved = ph.sem("row_moved")
        step = ph.sem("dve_step")
        block = ph.block()

        @block.sync
        def _(sp):
            with nc.allow_non_contiguous_dma(reason="one word of each partition"):
                sp.dma_start(row_dram.rearrange("(t p) -> p t", p=P), scores).then_inc(moved, 16)
            sp.wait_ge(moved, 16)
            sp.dma_start(row, row_dram.unsqueeze(0).to_broadcast([P, N])).then_inc(moved, 16)
            sp.wait_ge(moved, 32)

        @block.vector
        def _(dve):
            st = Steps(dve, step)
            st.then(dve.memset(part, 0.0))
            dve.wait_ge(moved, 32)
            for t in range(NT):
                own, lo, hi = scores[:, t:t + 1], t * P, (t + 1) * P
                if t > 0:
                    st.then(dve.tensor_scalar(spare[:, 0:lo], row[:, 0:lo], own, None, ALU.is_ge, ALU.add,
                                              accum_out=part[:, 0, t:t + 1]))
                st.then(dve.tensor_scalar(spare[:, lo:N], row[:, lo:N], own, None, ALU.is_gt, ALU.add,
                                          accum_out=part[:, 1, t:t + 1]))
                st.then(dve.scalar_tensor_tensor(spare[:, lo:hi], row[:, lo:hi], own, c["after"][0:P, 0:P],
                                                 ALU.is_equal, ALU.mult, accum_out=part[:, 2, t:t + 1]))
            st.then(dve.tensor_tensor(rank, part[:, 0, :], part[:, 1, :], ALU.add))
            st.then(dve.tensor_tensor(rank, rank, part[:, 2, :], ALU.add))
            st.then(dve.scalar_tensor_tensor(gate, rank, float(chosen), scores, ALU.is_lt, ALU.mult))


HEADS = 4
GE = 4
ROW = HEADS * GE + HEADS
SRC_ROW = 24
DST_ROW = 8


def attention_scores(nc, name, c, arena, src_t, rec, places, w, scores_out, gates, src_table, dst_table):
    a = Arena(arena, Y_AT, YT_AT)
    node = a.take(NT, SRC_ROW, rows=P)
    best = a.take(NT, ROW, rows=P)
    target = a.take(NT, DST_ROW, rows=P)
    sums = a.take(NT, ROW, rows=P)
    att = a.take(2, HEADS * GE, rows=P)
    w_sb = a.take(DK, HEADS * GE)
    prod = a.take(NT, HEADS * GE, rows=P)
    self_e = a.take(NT, HEADS, rows=P)
    zero_b = a.take(HEADS * GE, rows=P)
    z_at = a.at
    b = Arena(arena, TMP_AT, REC_AT)
    edge = b.take(T_GAT, ROW)
    edge_dst = b.take(T_GAT, DST_ROW)
    weight = b.take(T_GAT, HEADS)
    ring = b.take(RING, GROUP, SRC_ROW)
    idx = b.take(RING, GROUP, dtype=I32)
    hot = b.take(RING, GROUP, P)
    head = lambda v: v.rearrange("p t (h g) -> p t h g", h=HEADS)

    def node_terms():
        with Phase(nc, name + "_terms") as ph:
            loaded, multiplied, step, stored = (ph.sem(x) for x in ("loaded", "multiplied", "dve_step", "stored"))
            ready = ph.sem("node_ready")
            ps = ph.psum("h", [LANES, 512])
            view = ps[0:P, 0:NT * HEADS * GE].rearrange("p (t e) -> p t e", e=HEADS * GE)
            block = ph.block()

            @block.sync
            def _(sp):
                sp.dma_start(w_sb, w["W_gat"].rearrange("(k p) e -> p k e", p=LANES)).then_inc(loaded, 16)
                for i, n in enumerate(("att_src", "att_dst")):
                    sp.dma_start(att[:, i, :], w[n].rearrange("h g -> (h g)").unsqueeze(0)
                                 .to_broadcast([P, HEADS * GE])).then_inc(loaded, 16)
                sp.wait_ge(ready, 1)
                sp.dma_start(src_table.rearrange("(t p) d -> p t d", p=P), node).then_inc(stored, 16)
                sp.wait_ge(stored, 16)

            @block.tensor
            def _(pe):
                pe.wait_ge(loaded, 48)
                for t in range(NT):
                    for k in range(DK):
                        last = pe.matmul(view[:, t, :], src_t[:, k, t * P:(t + 1) * P], w_sb[:, k, :],
                                         start=(k == 0), stop=(k == DK - 1))
                last.then_inc(multiplied, 1)

            @block.vector
            def _(dve):
                st = Steps(dve, step)
                dve.wait_ge(loaded, 48)
                dve.wait_ge(multiplied, 1)
                st.then(dve.tensor_copy(node[:, :, 0:16], view))
                for i in range(2):
                    st.then(dve.tensor_tensor(prod, node[:, :, 0:16], across(att[:, i, :], NT), ALU.mult))
                    st.then(dve.tensor_reduce(node[:, :, 16 + HEADS * i:16 + HEADS * (i + 1)], head(prod),
                                              AX.X, ALU.add))
                st.then(dve.tensor_copy(best[:, :, 0:HEADS], node[:, :, 16:20]))
                dve.sem_inc(ready, 1)

    def gather(ph, table, column, width, keep):
        turns = ph.sem("pool_turns")
        idx_ready = [ph.sem(f"idx_ready{h}") for h in range(RING)]
        gathered = c["pool_dma"]
        kept = ph.sem("groups_kept")
        bodies = T_GAT // (RING * GROUP)
        rows = flat(ring.rearrange("p r g w -> p (r g) w"))[:, 0:RING * GROUP * width]\
            .rearrange("p (r g w) -> p r g w", r=RING, g=GROUP)

        def pool_side(pool):
            with pool.Fori(0, bodies) as i:
                for h in range(RING):
                    pool.wait_ge(idx_ready[h], i + 1)
                    pool.sem_inc(turns, 1)
                    for j in range(GROUP):
                        pool.indirect_dma_start(
                            rows[:, h, j, :], None, table,
                            bass.IndirectOffsetOnAxis(ap=idx[:, h, j:j + 1].bitcast(U32), axis=0))\
                            .then_inc(gathered.sems[h], 16)

        def act_side(act):
            def index(g, h):
                act.copy(idx[:, h, :], rec[:, bass.ds(g * GROUP, GROUP), column].bitcast(I32))\
                   .then_inc(idx_ready[h], 1)

            for h in range(RING):
                index(h, h)

            def keep_group(g, h, i):
                gathered.wait(act, h, i * GROUP + GROUP)
                act.copy(keep[:, bass.ds(g * GROUP, GROUP), :], rows[:, h, :, 0:keep.shape[2]]).then_inc(kept, 1)

            with act.Fori(0, bodies - 1) as i:
                for h in range(RING):
                    g = i * RING + h
                    keep_group(g, h, i)
                    act.wait_ge(kept, g + 1)
                    index(g + RING, h)
            for h in range(RING):
                keep_group((bodies - 1) * RING + h, h, bodies - 1)
                gathered.finished(h, GROUP * bodies)

        return pool_side, act_side, kept

    def maxima():
        z = Arena(arena, z_at, YT_AT)
        miss = z.take(GROUP, P)
        masked = z.take(GROUP, HEADS * P)
        with Phase(nc, name + "_max") as ph:
            pool_side, act_side, kept = gather(ph, src_table, 0, SRC_ROW, edge)
            step = ph.sem("dve_step")
            masked_ready = ph.sem("masked_ready")
            turned = ph.sem("tile_turned")
            ps = ph.psum("t", [LANES, 8, 512])
            bodies = T_GAT // (RING * GROUP)
            new = ph.ctx.enter_context(nc.sbuf_tensor(name + "_new", [P, GROUP, HEADS], F32))[:, :, :]
            block = ph.block()

            @block.gpsimd
            def _(pool):
                pool_side(pool)

            @block.scalar
            def _(act):
                act_side(act)

            @block.vector
            def _(dve):
                st = Steps(dve, step)
                each = RING * (2 + 1 + GROUP)
                with dve.Fori(0, bodies) as i:
                    st.enter(i, each)
                    for h in range(RING):
                        g = i * RING + h
                        of = rec[:, bass.ds(g * GROUP, GROUP), :]
                        st.then(dve.tensor_tensor(miss, over(of[:, :, 1], P), across(c["lane"][:, 0:P], GROUP),
                                                  ALU.is_equal))
                        st.then(dve.tensor_scalar(miss, miss, -1.0, BIG, ALU.add, ALU.mult))
                        dve.wait_ge(kept, g + 1)
                        dve.wait_ge(turned, g * GROUP + 1)
                        for q in range(HEADS):
                            done = dve.tensor_tensor(
                                masked[:, :, q * P:(q + 1) * P], miss,
                                over(edge[:, bass.ds(g * GROUP, GROUP), 16 + q], P), ALU.add)
                        done.then_inc(masked_ready, 1)
                        _, place = nc.values_load_multi_w_load_instructions(
                            places[0:1, bass.ds(g * GROUP, GROUP)], engines=(mybir.EngineType.DVE,),
                            min_val=0, max_val=(NT - 1) * ROW)
                        dve.wait_ge(turned, g * GROUP + (GROUP + 1))
                        st.then(dve.tensor_reduce(new, ps[0:P, :, :].rearrange("p g (q e) -> p g q e", q=HEADS),
                                                  AX.X, ALU.max))
                        for j in range(GROUP):
                            to = flat(best)[:, bass.ds(place[j], HEADS)]
                            st.then(dve.tensor_tensor(to, to, new[:, j, :], ALU.max))
                st.leave(bodies)

            @block.tensor
            def _(pe):
                pe.sem_inc(turned, 1)
                with pe.Fori(0, bodies) as i:
                    for h in range(RING):
                        pe.wait_ge(masked_ready, i * RING + (h + 1))
                        for j in range(GROUP):
                            for q in range(HEADS):
                                last = pe.transpose(ps[0:P, j, q * LANES:(q + 1) * LANES],
                                                    masked[:, j, q * P:(q + 1) * P], c["ident"])
                            last.then_inc(turned, 1)

    def target_terms():
        with Phase(nc, name + "_targets") as ph:
            step, ready, stored, asked, answered = (ph.sem(x) for x in
                                                    ("dve_step", "ready", "stored", "exp_asked", "exp_done"))
            block = ph.block()

            @block.sync
            def _(sp):
                sp.wait_ge(ready, 1)
                sp.dma_start(dst_table.rearrange("(t p) d -> p t d", p=P), target).then_inc(stored, 16)
                sp.wait_ge(stored, 16)

            @block.vector
            def _(dve):
                st = Steps(dve, step)
                tt = dve.tensor_tensor
                a_dst, a_src, m = node[:, :, 20:24], node[:, :, 16:20], target[:, :, HEADS:2 * HEADS]
                st.then(dve.tensor_copy(target[:, :, 0:HEADS], a_dst))
                st.then(tt(m, best[:, :, 0:HEADS], a_dst, ALU.add))
                st.then(dve.scalar_tensor_tensor(m, m, 0.2, m, ALU.mult, ALU.max))
                dve.sem_inc(ready, 1)
                st.then(tt(self_e, a_src, a_dst, ALU.add))
                st.then(dve.scalar_tensor_tensor(self_e, self_e, 0.2, self_e, ALU.mult, ALU.max))
                st.then(tt(self_e, self_e, m, ALU.subtract))
                dve.sem_inc(asked, 1)
                dve.wait_ge(answered, 1)
                st.then(dve.tensor_copy(sums[:, :, 16:20], self_e))
                for h in range(HEADS):
                    st.then(tt(sums[:, :, GE * h:GE * (h + 1)], node[:, :, GE * h:GE * (h + 1)],
                               over(self_e[:, :, h], GE), ALU.mult))

            @block.scalar
            def _(act):
                act.wait_ge(asked, 1)
                act.activation(self_e, self_e, ACT.Exp).then_inc(answered, 1)

    def target_gather():
        with Phase(nc, name + "_dst") as ph:
            pool_side, act_side, kept = gather(ph, dst_table, 3, DST_ROW, edge_dst)
            block = ph.block()

            @block.gpsimd
            def _(pool):
                pool_side(pool)

            @block.scalar
            def _(act):
                act_side(act)

    def edge_weights():
        with Phase(nc, name + "_edges") as ph:
            step, asked, answered = (ph.sem(x) for x in ("dve_step", "exp_asked", "exp_done"))
            block = ph.block()

            @block.vector
            def _(dve):
                st = Steps(dve, step)
                tt = dve.tensor_tensor
                st.then(tt(weight, edge[:, :, 16:20], edge_dst[:, :, 0:HEADS], ALU.add))
                st.then(dve.scalar_tensor_tensor(weight, weight, 0.2, weight, ALU.mult, ALU.max))
                st.then(tt(weight, weight, edge_dst[:, :, HEADS:2 * HEADS], ALU.subtract))
                st.then(dve.tensor_scalar_min(weight, weight, 0.0))
                dve.sem_inc(asked, 1)
                dve.wait_ge(answered, 1)
                for h in range(HEADS):
                    st.then(tt(edge[:, :, GE * h:GE * (h + 1)], edge[:, :, GE * h:GE * (h + 1)],
                               over(weight[:, :, h], GE), ALU.mult))
                st.then(dve.tensor_copy(edge[:, :, 16:20], weight))

            @block.scalar
            def _(act):
                act.wait_ge(asked, 1)
                act.activation(weight, weight, ACT.Exp).then_inc(answered, 1)

    def edge_sums():
        with Phase(nc, name + "_sum") as ph:
            step = ph.sem("dve_step")
            hot_ready = ph.sem("hot_ready")
            summed = ph.sem("groups_summed")
            ps = ph.psum("sum", [LANES, RING, 512])
            bodies = T_GAT // (RING * GROUP)
            block = ph.block()

            @block.vector
            def _(dve):
                st = Steps(dve, step)
                with dve.Fori(0, bodies) as i:
                    st.enter(i, RING * GROUP)
                    for h in range(RING):
                        dve.wait_ge(summed, i * RING + (h + 1))
                        of = rec[:, bass.ds((i * RING + h) * GROUP, GROUP), :]
                        dve.tensor_tensor(hot[:, h, :, :], over(of[:, :, 1], P), across(c["lane"][:, 0:P], GROUP),
                                          ALU.is_equal).then_inc(hot_ready, 1)
                    for h in range(RING):
                        _, place = nc.values_load_multi_w_load_instructions(
                            places[0:1, bass.ds((i * RING + h) * GROUP, GROUP)],
                            engines=(mybir.EngineType.DVE,), min_val=0, max_val=(NT - 1) * ROW)
                        dve.wait_ge(summed, i * RING + (RING + h + 1))
                        for j in range(GROUP):
                            to = flat(sums)[:, bass.ds(place[j], ROW)]
                            st.then(dve.tensor_tensor(to, to, ps[0:P, h, j * ROW:(j + 1) * ROW], ALU.add))
                st.leave(bodies)

            @block.tensor
            def _(pe):
                pe.sem_inc(summed, RING)
                with pe.Fori(0, bodies) as i:
                    for h in range(RING):
                        pe.wait_ge(hot_ready, i * RING + (h + 1))
                        for j in range(GROUP):
                            last = pe.matmul(ps[0:P, h, j * ROW:(j + 1) * ROW], hot[:, h, j, :],
                                             edge[:, bass.ds((i * RING + h) * GROUP + j, 1), :]
                                             .rearrange("p a b -> p (a b)"), start=True, stop=True)
                        last.then_inc(summed, 1)

    def finish():
        k = HEADS * GE
        f = Arena(arena, TMP_AT, REC_AT)
        agg = f.take(NT, k, rows=P)
        sq = f.take(NT, k, rows=P)
        mean = f.take(NT, rows=P)
        root = f.take(NT, rows=P)
        par = f.take(3, k, rows=P)
        tmp = best_two_places(f, GE)
        with Phase(nc, name + "_norm") as ph:
            loaded, step, asked, rooted, e_asked, e_done = (
                ph.sem(x) for x in ("loaded", "dve_step", "root_asked", "root_ready", "exp_asked", "exp_done"))
            block = ph.block()

            @block.sync
            def _(sp):
                for i, n in enumerate(("b_gat", "ln_gamma", "ln_beta")):
                    sp.dma_start(par[:, i, :], w[n].unsqueeze(0).to_broadcast([P, k])).then_inc(loaded, 16)

            @block.vector
            def _(dve):
                st = Steps(dve, step)
                tt = dve.tensor_tensor
                st.then(dve.tensor_scalar_add(self_e, sums[:, :, 16:20], 1e-16))
                st.then(dve.reciprocal(self_e, self_e))
                for h in range(HEADS):
                    st.then(tt(agg[:, :, GE * h:GE * (h + 1)], sums[:, :, GE * h:GE * (h + 1)],
                               over(self_e[:, :, h], GE), ALU.mult))
                dve.wait_ge(loaded, 48)
                st.then(tt(agg, agg, across(par[:, 0, :], NT), ALU.add))
                st.then(dve.tensor_reduce(mean, agg, AX.X, ALU.add))
                st.then(dve.tensor_scalar_mul(mean, mean, 1.0 / k))
                st.then(tt(agg, agg, over(mean, k), ALU.subtract))
                st.then(tt(sq, agg, agg, ALU.mult))
                st.then(dve.tensor_reduce(root, sq, AX.X, ALU.add))
                st.then(dve.tensor_scalar(root, root, 1.0 / k, EPS, ALU.mult, ALU.add))
                dve.sem_inc(asked, 1)
                dve.wait_ge(rooted, 1)
                st.then(dve.reciprocal(root, root))
                st.then(tt(agg, agg, over(root, k), ALU.mult))
                st.then(tt(agg, agg, across(par[:, 1, :], NT), ALU.mult))
                st.then(tt(agg, agg, across(par[:, 2, :], NT), ALU.add))
                st.then(dve.tensor_reduce(scores_out, agg.rearrange("p t (h g) -> p t g h", h=HEADS), AX.X, ALU.add))
                st.then(dve.tensor_scalar_mul(flat(scores_out), flat(scores_out), 1.0 / HEADS))
                best_two(dve, st, c, scores_out, gates, tmp, e_asked, e_done)

            @block.scalar
            def _(act):
                act.wait_ge(asked, 1)
                act.activation(root, root, ACT.Sqrt).then_inc(rooted, 1)
                act.wait_ge(e_asked, 1)
                act.activation(tmp[6], tmp[6], ACT.Exp).then_inc(e_done, 1)

    node_terms()
    maxima()
    target_terms()
    target_gather()
    edge_weights()
    edge_sums()
    finish()


def last_norm(nc, name, a, x, y, gamma, beta, out):
    stats = a.take(NT, 6, rows=P)
    mean, root, spare = (a.take(NT, rows=P) for _ in range(3))
    g = a.take(D, rows=P)
    b = a.take(D, rows=P)
    with Phase(nc, name) as ph:
        loaded, step, asked, rooted, ready, stored = (
            ph.sem(s) for s in ("loaded", "dve_step", "root_asked", "root_ready", "quad_ready", "stored"))
        block = ph.block()

        @block.sync
        def _(sp):
            sp.dma_start(g, gamma.unsqueeze(0).to_broadcast([P, D])).then_inc(loaded, 16)
            sp.dma_start(b, beta.unsqueeze(0).to_broadcast([P, D])).then_inc(loaded, 16)
            rows = out.rearrange("(t p) d -> p t d", p=P)
            for q, (t, n) in enumerate(quads()):
                sp.wait_ge(ready, q + 1)
                sp.dma_start(rows[:, t:t + n, :], x[:, t:t + n, :]).then_inc(stored, 16)
            sp.wait_ge(stored, 16 * len(quads()))

        @block.vector
        def _(dve):
            st = Steps(dve, step)
            row_statistics(dve, st, y, stats, mean, root, spare).then_inc(asked, 1)
            dve.wait_ge(rooted, 1)
            st.then(dve.reciprocal(root, root))
            dve.wait_ge(loaded, 32)
            for t, n in quads():
                part, xs = y[:, t:t + n, :], x[:, t:t + n, :]
                st.then(dve.tensor_tensor(part, part, over(mean[:, t:t + n], D), ALU.subtract))
                st.then(dve.tensor_tensor(part, part, over(root[:, t:t + n], D), ALU.mult))
                st.then(dve.tensor_tensor(part, part, across(g, n), ALU.mult))
                st.then(dve.tensor_tensor(part, part, across(b, n), ALU.add))
                dve.tensor_tensor(xs, xs, part, ALU.add).then_inc(ready, 1)

        @block.scalar
        def _(act):
            act.wait_ge(asked, 1)
            act.activation(root, root, ACT.Sqrt).then_inc(rooted, 1)


def residual_layers(nc, w, out):
    Phase.cleared = []
    dram = lambda name, shape, dt=F32: nc.dram_tensor(name, shape, dt, kind="Internal").ap()
    by_dst = dram("edges_by_dst", (T_MAIN * LANES, 4))
    by_src = dram("edges_by_src", (T_MAIN * LANES, 4))
    by_gat = dram("gat_edges_by_dst", (T_GAT * LANES, 4))
    rows = [dram(f"rows{i}", (N, D)) for i in range(5)]
    src_table = dram("gat_src_rows", (N, SRC_ROW))
    dst_table = dram("gat_dst_rows", (N, DST_ROW))
    score_row = dram("score_row", (N,))

    with ExitStack() as ctx:
        arena = ctx.enter_context(nc.sbuf_tensor("arena", [LANES, ARENA], F32))[:, :]
        sb = lambda name, shape, dt=F32: ctx.enter_context(nc.sbuf_tensor(name, shape, dt))[:, :]
        c = constants(nc, ctx, arena)
        at_dst = sb("places_by_dst", [1, T_MAIN], I32)
        at_src = sb("places_by_src", [1, T_MAIN], I32)
        at_gat = sb("places_gat", [1, T_GAT], I32)
        bucket_of = c["bucket_of"]
        degree = sb("degree", [P, NT])

        bucket_sort(nc, "sort_dst", c, arena, w["dst"], w["src"], None, P, T_MAIN, D, by_dst, at_dst, bucket_of)
        bucket_sort(nc, "sort_src", c, arena, w["src"], w["dst"], w["edge_weight"], P, T_MAIN, D, by_src, at_src, None)
        e = w["L2_ffn_edge_index"]
        bucket_sort(nc, "sort_gat", c, arena, e[1, :], e[0, :], None, LANES, T_GAT, ROW, by_gat, at_gat, None)

        def node(at, rows=P):
            return arena[0:rows, at:at + NT * D].rearrange("p (t d) -> p t d", d=D)

        x, y, acc = node(X_AT), node(Y_AT), node(ACC_AT)
        yt = arena[:, YT_AT:YT_AT + DK * N].rearrange("p (k n) -> p k n", k=DK)
        rec = Arena(arena, REC_AT)
        rec_dst, rec_src, rec_gat = rec.take(T_MAIN, 4), rec.take(T_MAIN, 4), rec.take(T_GAT, 4)
        tmp = lambda: Arena(arena, TMP_AT, REC_AT)

        load_records(nc, "load_dst", [(rec_dst, by_dst)])
        x_view = w["x"].rearrange("(t p) d -> p t d", p=P)
        eps1 = sb("one_plus_eps", [P, 1])
        layer_norm(nc, "L0g_norm", c, arena, x, y, yt, rows[0],
                   loads=[(x, x_view), (eps1, w["L0_gnn_eps"].unsqueeze(0).to_broadcast([P, 1]))])
        graph_sum(nc, "L0g_sum", c, arena, rows[0], rec_dst, at_dst, flat(acc), T_MAIN, False, degree, bucket_of)

        def mix(dve, st, quad_ready, asked, rooted):
            st.then(dve.tensor_scalar_add(eps1, eps1, 1.0))
            for t, n in quads():
                dve.scalar_tensor_tensor(y[:, t:t + n, :], y[:, t:t + n, :], eps1, acc[:, t:t + n, :],
                                         ALU.mult, ALU.add).then_inc(quad_ready, 1)

        to_features(nc, "L0g_mix", c, arena, y, yt, mix)
        wide = lambda at, m: arena[:, at:at + m * N].rearrange("p (m n) -> p m n", m=m)
        weight = lambda at, k, f: arena[:, at:at + k * f].rearrange("p (k f) -> p k f", k=k)
        small = sb("column_bias", [LANES, 8])
        stats = sb("batch_stats", [LANES, 8 * 6 * len(CHUNKS)]).rearrange("p (m s) -> p m s", m=8)
        h1, h2, h3 = wide(X_AT, 4), wide(TMP_AT, 8), wide(ACC_AT, 4)
        w1, w2, w3, w4 = weight(ACC_AT, 2, 512), weight(ACC_AT, 4, 1024), weight(X_AT, 8, 512), weight(Y_AT, 4, 256)
        spaces = {1: TMP_AT, 2: X_AT, 3: TMP_AT}
        for i, (src, h, ws) in enumerate(((yt, h1, w1), (h1, h2, w2), (h2, h3, w3)), 1):
            m = h.shape[1]
            dense(nc, f"L0g_mlp{i}", [(src, ws, w[f"L0_gnn_W{i}"])], (small[:, 0:m], w[f"L0_gnn_b{i}"]), h,
                  ACT.Identity, stats[:, 0:m, :])
            batch_norm_elu(nc, f"L0g_bn{i}", Arena(arena, spaces[i]), h, stats[:, 0:m, :],
                           w[f"L0_gnn_g{i}"], w[f"L0_gnn_beta{i}"])
        row_bias = sb("row_bias", [P, D])
        project(nc, "L0g_out", h3, w4, w["L0_gnn_W4"], x, (row_bias, w["L0_gnn_b4"]), add=True, loads=[(x, x_view)])
        load_records(nc, "load_all", [(rec_dst, by_dst), (rec_src, by_src), (rec_gat, by_gat)])

        layer_norm(nc, "L0f_norm", c, arena, x, y, yt)
        a = tmp()
        rh = a.take(1, N)
        wr = a.take(2, LANES)
        dense(nc, "L0f_hidden", [(yt, wr, w["L0_ffn_router_w1"])], (small[:, 0:1], w["L0_ffn_router_b1"]), rh, ACT.Relu)
        a2 = tmp()
        a2.at = a.at
        scores, gates = a2.take(NT, 6, rows=P), a2.take(NT, 6, rows=P)
        router(nc, "L0f_router", c, a2, rh, w["L0_ffn_router_w2"], w["L0_ffn_router_b2"], scores, gates, softmax=True)
        a2.at = a.at + 2 * NT * 6
        experts(nc, "L0f", c, a2, yt, x, [(w["L0_ffn_expert_w1"], w["L0_ffn_expert_b1"]),
                                          (w["L0_ffn_expert_w2"], w["L0_ffn_expert_b2"])],
                w["L0_ffn_expert_w3"], gates, gates, w["L0_ffn_expert_b3"], 6, ACT.Relu)

        layer_norm(nc, "L1g_norm", c, arena, x, y, yt)
        wk = tmp().take(2, D)
        project(nc, "L1g_rows", yt, wk, w["L1_gnn_kernel"], acc, table=rows[1])
        graph_sum(nc, "L1g_sum", c, arena, rows[1], rec_src, at_src, flat(acc), T_MAIN, True)
        add_scaled(nc, "L1g_add", x, acc, bias=(row_bias, w["L1_gnn_bias"]))

        layer_norm(nc, "L1f_norm", c, arena, x, y, yt)
        a = tmp()
        scores, gate2, gate1 = a.take(NT, 1, rows=P), a.take(NT, 2, rows=P), a.take(NT, 1, rows=P)
        at = a.at
        router(nc, "L1f_router", c, a, yt, w["L1_ffn_wr"], w["L1_ffn_br"], scores)
        a.at = at
        choose_half(nc, "L1f_choose", c, a, flat(scores), flat(gate1), score_row, max(1, int(0.5 * N)) - 1)
        add_gates(nc, "L1f_gates", x, y, gate1, gate2)
        a.at = at
        hidden_w, hidden_b, out_w = w["L1_ffn_w1"], w["L1_ffn_b1"], w["L1_ffn_w2"]
        experts(nc, "L1f", c, a, yt, x, [(hidden_w, hidden_b)], out_w, gate2, gate1, w["L1_ffn_b2"].unsqueeze(0), 2,
                ACT.Gelu_apprx_tanh)

        layer_norm(nc, "L2g_norm", c, arena, x, y, yt, rows[2])
        graph_sum(nc, "L2g_sum1", c, arena, rows[2], rec_dst, at_dst, flat(acc), T_MAIN, False)
        inv = sb("inverse_degree", [P, NT])
        inverse(nc, "L2g_inverse", degree, inv, lambda dve: dve.tensor_scalar_max(inv, degree, 1.0))
        agg_t = arena[:, Y_AT:Y_AT + DK * N].rearrange("p (k n) -> p k n", k=DK)

        def mean(dve, st, quad_ready, asked, rooted):
            for t, n in quads():
                dve.tensor_tensor(acc[:, t:t + n, :], acc[:, t:t + n, :], over(inv[:, t:t + n], D),
                                  ALU.mult).then_inc(quad_ready, 1)

        to_features(nc, "L2g_mean", c, arena, acc, agg_t, mean)
        a = tmp()
        ht = a.take(4, N)
        w1l, w1r, w2l, w2r = a.take(2, 512), a.take(2, 512), a.take(4, D), a.take(4, D)
        dense(nc, "L2g_hidden", [(agg_t, w1l, w["L2_gnn_W1l"]), (yt, w1r, w["L2_gnn_W1r"])],
              (small[:, 0:4], w["L2_gnn_b1"]), ht, ACT.Relu)
        project(nc, "L2g_rows", ht, w2l, w["L2_gnn_W2l"], acc, table=rows[3])
        project(nc, "L2g_own", ht, w2r, w["L2_gnn_W2r"], x, (row_bias, w["L2_gnn_b2"]), add=True)
        graph_sum(nc, "L2g_sum2", c, arena, rows[3], rec_dst, at_dst, flat(acc), T_MAIN, False)
        add_scaled(nc, "L2g_add", x, acc, scale=inv)

        layer_norm(nc, "L2f_norm", c, arena, x, y, yt)
        scores4 = sb("gat_scores", [P, NT * GE]).rearrange("p (t e) -> p t e", e=GE)
        gates4 = sb("gat_gates", [P, NT * GE]).rearrange("p (t e) -> p t e", e=GE)
        attention_scores(nc, "L2f_gat", c, arena, yt, rec_gat, at_gat,
                         {n: w["L2_ffn_" + n] for n in ("W_gat", "att_src", "att_dst", "b_gat", "ln_gamma", "ln_beta")},
                         scores4, gates4, src_table, dst_table)
        experts(nc, "L2f", c, tmp(), yt, x, [(w["L2_ffn_W1"], w["L2_ffn_b1"])], w["L2_ffn_W2"], gates4, gates4,
                w["L2_ffn_b2"], 4, ACT.Gelu)

        layer_norm(nc, "L3g_norm", c, arena, x, y, yt)
        wk = tmp().take(2, D)
        project(nc, "L3g_rows", yt, wk, w["L3_gnn_W"], acc, (row_bias, w["L3_gnn_b"]), table=rows[4])
        graph_sum(nc, "L3g_sum", c, arena, rows[4], rec_dst, at_dst, flat(acc), T_MAIN, False)
        inverse(nc, "L3g_inverse", degree, inv, lambda dve: dve.tensor_scalar_add(inv, degree, 1.0))
        add_scaled(nc, "L3g_add", x, acc, scale=inv)

        layer_norm(nc, "L3f_norm", c, arena, x, y, yt)
        a = tmp()
        gates = a.take(NT, 16, rows=P)
        at = a.at
        scores = a.take(NT, 16, rows=P)
        router(nc, "L3f_router", c, a, yt, w["L3_ffn_gate_w"], w["L3_ffn_gate_b"], scores, gates)
        a.at = at
        experts(nc, "L3f", c, a, yt, y, [(w["L3_ffn_w1"], w["L3_ffn_b1"])], w["L3_ffn_w2"], gates, gates,
                w["L3_ffn_b2"], 16, ACT.Relu)
        last_norm(nc, "L3f_last", tmp(), x, y, w["L3_ffn_gamma"], w["L3_ffn_beta"], out)


def add_gates(nc, name, x, y, gate, gates):
    with Phase(nc, name) as ph:
        block = ph.block()

        @block.vector
        def _(dve):
            dve.tensor_tensor(x, x, y, ALU.add)
            dve.tensor_copy(gates[:, :, 0:1], gate)
            dve.tensor_copy(gates[:, :, 1:2], gate)


def inverse(nc, name, degree, inv, first):
    with Phase(nc, name) as ph:
        step = ph.sem("dve_step")
        block = ph.block()

        @block.vector
        def _(dve):
            st = Steps(dve, step)
            st.then(first(dve))
            dve.reciprocal(inv, inv)


def kernel(**inputs):
    import concourse.bacc as bacc
    from concourse.bass_utils import run_bass_kernel_spmd

    arrays = {k: np.asarray(v) for k, v in inputs.items()}
    arrays["L0_gnn_eps"] = arrays["L0_gnn_eps"].reshape(1)
    for name in ("L2_gnn_W1l", "L2_gnn_W1r", "L2_gnn_W2l", "L2_gnn_W2r", "L3_gnn_W"):
        arrays[name] = arrays[name].T
    w1, b1, w2 = arrays["L1_ffn_w1"], arrays["L1_ffn_b1"], arrays["L1_ffn_w2"]
    arrays["L1_ffn_w1"] = w1.reshape(D, 2, -1).transpose(1, 0, 2)
    arrays["L1_ffn_b1"] = b1.reshape(2, -1)
    arrays["L1_ffn_w2"] = w2.reshape(2, -1, D)
    del arrays["L1_ffn_attention_mask"]
    arrays = {k: np.ascontiguousarray(v) for k, v in arrays.items()}

    nc = bacc.Bacc("TRN2", target_bir_lowering=False, num_devices=1)
    aps = {k: nc.dram_tensor("in_" + k, v.shape, mybir.dt.from_np(v.dtype), kind="ExternalInput").ap()
           for k, v in arrays.items()}
    out = nc.dram_tensor("out", (N, D), F32, kind="ExternalOutput").ap()
    residual_layers(nc, aps, out)
    r = run_bass_kernel_spmd(nc, [{"in_" + k: v for k, v in arrays.items()}], core_ids=[0])
    return r.results[0]["out"]
```

```python
from contextlib import ExitStack

import numpy as np
import concourse.bass as bass
import concourse.mybir as mybir

F32 = mybir.dt.float32
I32 = mybir.dt.int32
U32 = mybir.dt.uint32
ALU = mybir.AluOpType
ACT = mybir.ActivationFunctionType
AX = mybir.AxisListType

N = 3125
P = 125
NT = N // P
D = 256
DK = D // 128
LANES = 128
GROUP = 8
STEP = 2 * GROUP
RING = 4
QUADS = 2 * RING
E_MAIN = 50000
E_GAT = 32768
CHUNK = 4 * P
FULL = N // CHUNK
CHUNKS = [(c * CHUNK, min(CHUNK, N - c * CHUNK)) for c in range(FULL + 1)]
ROUND = 12582912.0
EPS = 1e-5
BIG = 1e30


def edge_tiles(edges):
    most = (edges + NT * (LANES - 1)) // LANES
    return -(-most // (RING * GROUP)) * (RING * GROUP)


T_MAIN = edge_tiles(E_MAIN)
T_GAT = edge_tiles(E_GAT)

Y_AT = 0
ACC_AT = Y_AT + NT * D
LATER_AT = ACC_AT + NT * D
WEIGHTS_AT = LATER_AT + 2304
YT_AT = WEIGHTS_AT + 4096
X_AT = YT_AT + DK * N
TMP_AT = X_AT + NT * D
ARENA = X_AT + 8 * N
REC_MAIN = 4 * T_MAIN
REC_GAT = 4 * T_GAT
REC_AT = ARENA - 2 * REC_MAIN - REC_GAT
EARLY_AT = REC_AT - (LANES + T_MAIN)


class Steps:

    def __init__(self, eng, sem):
        self.eng, self.sem, self.n, self.turn = eng, sem, 0, 0

    def done(self, ins):
        ins.then_inc(self.sem, 1)
        self.n += 1

    def then(self, ins):
        self.done(ins)
        self.eng.wait_ge(self.sem, self.turn + self.n)

    def ahead(self, n):
        self.eng.sem_inc(self.sem, n)
        self.n += n

    def lag(self, ins, behind):
        self.done(ins)
        self.eng.wait_ge(self.sem, self.turn + self.n - behind)

    def all(self):
        self.eng.wait_ge(self.sem, self.turn + self.n)

    def enter(self, i, each):
        self.first, self.each, self.turn = self.n, each, i * each

    def leave(self, turns):
        assert self.n == self.first + self.each, (self.n - self.first, self.each)
        self.n, self.turn = self.first + self.each * turns, 0


class PoolDma:

    def __init__(self, nc, ctx):
        self.sems = [ctx.enter_context(nc.semaphore(f"pool_dma{h}")) for h in range(RING)]
        self.base = [0] * RING

    def wait(self, eng, h, dmas):
        eng.wait_ge(self.sems[h], dmas * 16 + self.base[h])

    def finished(self, h, dmas):
        self.base[h] += 16 * dmas


class Phase:

    cleared = []

    def __init__(self, nc, name):
        self.nc, self.name, self.ctx = nc, name, ExitStack()

        self.sems = []

    def __enter__(self):
        self.ctx.__enter__()
        return self

    def __exit__(self, *e):
        self.ctx.__exit__(*e)
        if e[0] is None:
            for s in Phase.cleared:
                self.nc.release_semaphore(s)
            for s in self.sems:
                self.nc.gpsimd.sem_clear(s)
            Phase.cleared = self.sems

    def sem(self, name):
        self.sems.append(self.nc.alloc_semaphore(f"{self.name}_{name}"))
        return self.sems[-1]

    def psum(self, name, shape):
        return self.ctx.enter_context(self.nc.psum_tensor(f"{self.name}_{name}", shape, F32))

    def block(self):
        return self.ctx.enter_context(self.nc.Block())


class Arena:

    def __init__(self, tensor, at, end=ARENA):
        self.t, self.at, self.end = tensor, at, end

    def take(self, *shape, rows=LANES, dtype=None):
        words = int(np.prod(shape))
        assert self.at + words <= self.end, (self.at, words, self.end)
        v = self.t[0:rows, self.at:self.at + words]
        self.at += words
        if dtype is not None:
            v = v.bitcast(dtype)
        if len(shape) == 2:
            v = v.rearrange("p (a b) -> p a b", a=shape[0])
        elif len(shape) == 3:
            v = v.rearrange("p (a b c) -> p a b c", a=shape[0], b=shape[1])
        return v


def over(ap, n):
    return ap.unsqueeze(2).to_broadcast([ap.shape[0], ap.shape[1], n])


def across(ap, n):
    return ap.unsqueeze(1).to_broadcast([ap.shape[0], n, ap.shape[1]])


def constants(nc, ctx, arena):
    def sb(name, shape):
        return ctx.enter_context(nc.sbuf_tensor(name, shape, F32))[:, :]

    a, early = Arena(arena, 0), Arena(arena, EARLY_AT)
    c = {
        "ident": sb("ident", [LANES, LANES]),
        "ones": sb("ones", [LANES, LANES]),
        "before": early.take(LANES),
        "after": sb("after", [LANES, LANES]),
        "lane": sb("lane", [LANES, LANES]),
        "tile": early.take(T_MAIN),
        "pool_dma": PoolDma(nc, ctx),
        "lane_i": a.take(LANES, dtype=I32),
        "tile_i": a.take(T_MAIN, dtype=I32),
    }
    with Phase(nc, "const") as ph:
        s = ph.sem("set")
        block = ph.block()

        @block.gpsimd
        def _(pool):
            st = Steps(pool, s)
            pool.memset(c["ident"], 0.0).then_inc(s, 1)
            pool.memset(c["ones"], 1.0).then_inc(s, 1)
            pool.memset(c["before"], 0.0).then_inc(s, 1)
            pool.iota(c["lane_i"], pattern=[[1, LANES]], base=0, channel_multiplier=0).then_inc(s, 1)
            pool.iota(c["tile_i"], pattern=[[1, T_MAIN]], base=0, channel_multiplier=0).then_inc(s, 1)
            st.n = 5
            pool.wait_ge(s, 5)
            st.done(pool.affine_select(out=c["ident"], in_=c["ident"], compare_op=ALU.not_equal, fill=1.0,
                                       base=0, pattern=[[-1, LANES]], channel_multiplier=1))
            st.done(pool.affine_select(out=c["before"], in_=c["before"], compare_op=ALU.is_ge, fill=1.0,
                                       base=0, pattern=[[-1, LANES]], channel_multiplier=1))
            st.done(pool.affine_select(out=c["after"], in_=c["ones"], compare_op=ALU.is_ge, fill=0.0,
                                       base=-1, pattern=[[-1, LANES]], channel_multiplier=1))
            pool.wait_ge(s, 8)

        @block.vector
        def _(dve):
            dve.wait_ge(s, 5)
            dve.tensor_copy(c["lane"], c["lane_i"])
            dve.tensor_copy(c["tile"], c["tile_i"])
    return c


def clear_table(nc, ctx, c, arena, table):
    words = table.shape[0] * D // LANES
    width = 2560
    assert words % width == 0
    zeros = arena[:, YT_AT:YT_AT + width]
    c["table_zero"] = ctx.enter_context(nc.semaphore("table_zero"))
    c["table_zero_dmas"] = words // width
    view = table.rearrange("(p r) d -> p (r d)", p=LANES)
    with Phase(nc, "clear") as ph:
        ready = ph.sem("zeros_ready")
        block = ph.block()

        @block.vector
        def _(dve):
            dve.memset(zeros, 0.0).then_inc(ready, 1)

        @block.sync
        def _(sp):
            sp.wait_ge(ready, 1)
            for i in range(words // width):
                sp.dma_start(view[:, i * width:(i + 1) * width], zeros).then_inc(c["table_zero"], 16)


class Scatter:

    def __init__(self, c, a, parts, n_each, table):
        self.dma, self.table, self.parts, self.n_each = c["pool_dma"], table, parts, n_each
        self.turns, self.at = n_each // STEP, 0
        assert self.turns * STEP == n_each
        self.place(a)

    def place(self, a):
        self.rec = a.take(self.n_each, 4, rows=self.parts)
        self.slot = a.take(self.n_each, rows=self.parts, dtype=I32)
        self.rec_ring = a.take(2, GROUP, 4, rows=self.parts)
        self.slot_ring = a.take(2, GROUP, rows=self.parts, dtype=I32)

    def run(self, ph, pool, turns=None):
        turns = self.turns - self.at if turns is None else turns
        copied = ph.sem("ring_copied")
        counts = ph.sem("ring_turns")

        def turn(i, at, first=False):
            for h in range(2):
                if not first:
                    self.dma.wait(pool, h, at * GROUP)
                of = (at * 2 + h) * GROUP
                pool.tensor_copy(self.rec_ring[:, h, :, :], self.rec[:, bass.ds(of, GROUP), :])
                pool.tensor_copy(self.slot_ring[:, h, :], self.slot[:, bass.ds(of, GROUP)]).then_inc(copied, 1)
                pool.wait_ge(copied, i * 2 + (h + 1))
                pool.sem_inc(counts, 1)
                for j in range(GROUP):
                    pool.indirect_dma_start(
                        self.table,
                        bass.IndirectOffsetOnAxis(ap=self.slot_ring[:, h, j:j + 1].bitcast(U32), axis=0),
                        self.rec_ring[:, h, j, :], None).then_inc(self.dma.sems[h], 16)

        first = 0
        if self.at == 0:
            turn(0, 0, first=True)
            first = 1
        if turns > first:
            with pool.Fori(first, turns) as i:
                turn(i, i + self.at)
        self.at += turns
        if self.at == self.turns:
            for h in range(2):
                self.dma.wait(pool, h, self.turns * GROUP)
                self.dma.finished(h, self.turns * GROUP)


def beside_work(ph, block, job):
    if job is not None:
        @block.gpsimd
        def _(pool):
            job[0].run(ph, pool, job[1])


def bucket_sort(nc, name, c, arena, key, other, weight, parts, tiles, place_scale, scatter, places, spill=None, beside=None):
    n_each = key.shape[0] // parts
    table, rec, slot_i = scatter.table, scatter.rec, scatter.slot
    a = Arena(arena, X_AT, EARLY_AT)
    key_i = a.take(n_each, rows=parts, dtype=I32)
    oth_i = a.take(n_each, rows=parts, dtype=I32)
    wgt = a.take(n_each, rows=parts)
    key_f = a.take(n_each, rows=parts)
    bucket = a.take(n_each, rows=parts)
    slot_f = a.take(n_each, rows=parts)
    shared = a.take(NT * max(n_each, tiles))
    hot = shared[0:parts, 0:NT * n_each].rearrange("p (b i) -> p b i", b=NT)
    run = a.take(2, n_each, rows=parts)
    pads = a.take(tiles, 4)
    total = a.take(NT, rows=parts)
    count = a.take(NT)
    tiles_of = a.take(NT)
    upto = a.take(NT)
    first = a.take(NT)
    cmp = shared[0:1, 0:NT * tiles].rearrange("p (t b) -> p t b", b=NT)
    place_f = a.take(tiles, rows=1)

    with Phase(nc, name) as ph:
        loaded = ph.sem("edges_loaded")
        step = ph.sem("dve_step")
        counted = ph.sem("counted")
        padded = ph.sem("pads_set")
        table_clear = ph.sem("table_clear")
        slots_ready = ph.sem("slots_ready")
        spilled = ph.sem("spilled")
        ps = ph.psum("sums", [LANES, 2, 512])
        block = ph.block()

        @block.sync
        def _(sp):
            view = lambda v: v.rearrange("(p i) -> p i", p=parts)
            sp.dma_start(key_i, view(key)).then_inc(loaded, 16)
            sp.dma_start(oth_i, view(other)).then_inc(loaded, 16)
            if weight is not None:
                sp.dma_start(wgt, view(weight)).then_inc(loaded, 16)
            sp.wait_ge(padded, 1)
            sp.dma_start(table.rearrange("(p t) c -> p (t c)", p=LANES),
                         pads.rearrange("p t c -> p (t c)")).then_inc(table_clear, 16)
            sp.wait_ge(table_clear, 16)

        @block.vector
        def _(dve):
            st = Steps(dve, step)
            dve.memset(pads, 0.0).then_inc(step, 1)
            st.n = 1
            dve.wait_ge(step, 1)
            dve.memset(pads[:, :, 1], -1.0).then_inc(padded, 1)
            dve.wait_ge(loaded, 32 if weight is None else 48)
            st.then(dve.tensor_copy(key_f, key_i))
            st.then(dve.tensor_scalar(bucket, key_f, -float(P // 2), 1.0 / P, ALU.add, ALU.mult))
            st.then(dve.tensor_scalar_add(bucket, bucket, ROUND))
            st.then(dve.tensor_scalar_add(bucket, bucket, -ROUND))
            st.done(dve.tensor_copy(rec[:, :, 0].bitcast(I32), oth_i))
            st.done(dve.tensor_copy(rec[:, :, 3].bitcast(I32), key_i))
            if weight is None:
                st.done(dve.memset(rec[:, :, 2], 0.0))
            else:
                st.done(dve.tensor_copy(rec[:, :, 2], wgt))
            st.done(dve.scalar_tensor_tensor(rec[:, :, 1], bucket, -float(P), key_f, ALU.mult, ALU.add))
            with dve.Fori(0, NT) as b:
                dve.tensor_scalar(hot[:, bass.ds(b, 1), :].rearrange("p a i -> p (a i)"), bucket,
                                  c["lane"][0:parts, bass.ds(b, 1)], None, ALU.is_equal, ALU.add,
                                  accum_out=total[:, bass.ds(b, 1)]).then_inc(step, 1)
            st.n += NT
            dve.wait_ge(counted, 1)
            st.then(dve.tensor_copy(count, ps[:, 0, 0:NT]))
            st.then(dve.tensor_scalar(tiles_of, count, LANES / 2 - 0.5, 1.0 / LANES, ALU.add, ALU.mult))
            st.then(dve.tensor_scalar_add(tiles_of, tiles_of, ROUND))
            st.then(dve.tensor_scalar_add(tiles_of, tiles_of, -ROUND))
            st.then(dve.tensor_tensor_scan(upto, c["ones"][:, 0:NT], tiles_of, 0.0, ALU.mult, ALU.add))
            st.then(dve.tensor_tensor(first, upto, tiles_of, ALU.subtract))
            st.then(dve.tensor_scalar(first, first, float(LANES), -1.0, ALU.mult, ALU.add))
            st.then(dve.tensor_tensor(first[0:parts], first[0:parts], ps[0:parts, 1, 0:NT], ALU.add))
            each = 2
            with dve.Fori(0, NT) as b:
                st.enter(b, each)
                row = hot[:, bass.ds(b, 1), :].rearrange("p a i -> p (a i)")
                st.then(dve.tensor_tensor_scan(run[:, 0, :], c["ones"][0:parts, 0:1].to_broadcast([parts, n_each]),
                                               row, first[0:parts, bass.ds(b, 1)], ALU.mult, ALU.add))
                st.then(dve.tensor_tensor(row, row, run[:, 0, :], ALU.mult))
            st.leave(NT)
            st.then(dve.tensor_reduce(slot_f, hot.rearrange("p b i -> p i b"), AX.X, ALU.add))
            dve.tensor_copy(slot_i, slot_f).then_inc(slots_ready, 1)
            st.then(dve.tensor_tensor(cmp, across(upto[0:1], tiles), over(c["tile"][0:1, 0:tiles], NT), ALU.is_le))
            st.then(dve.tensor_reduce(place_f, cmp, AX.X, ALU.add))
            st.then(dve.tensor_scalar(places, place_f, float(NT - 1), float(place_scale), ALU.min, ALU.mult))

        @block.tensor
        def _(pe):
            pe.wait_ge(step, 1 + 8 + NT)
            pe.matmul(ps[:, 0, 0:NT], c["ones"][0:parts, :], total, start=True, stop=True)
            pe.matmul(ps[:, 1, 0:NT], c["before"][0:parts, :], total, start=True, stop=True).then_inc(counted, 1)

        beside_work(ph, block, beside)
        if spill is None:
            return

        @block.scalar
        def _(act):
            act.wait_ge(slots_ready, 1)
            for to, of in zip(spill, (flat(rec), slot_i)):
                act.dma_start(to, of).then_inc(spilled, 16)
            act.wait_ge(spilled, 32)


def degrees(nc, name, c, a, scatter, degree, beside):
    parts, n_each = scatter.parts, scatter.n_each
    bf16 = mybir.dt.bfloat16
    key = a.take(n_each, rows=parts)
    bucket = a.take(n_each, rows=parts)
    by_target = a.take(2, GROUP * P // 2, rows=parts).bitcast(bf16).rearrange("p h (g c) -> p h g c", g=GROUP)
    by_bucket = a.take(2, GROUP * 13, rows=parts).bitcast(bf16).rearrange("p h (g c) -> p h g c", g=GROUP)
    with Phase(nc, name) as ph:
        step, ready, used = (ph.sem(x) for x in ("dve_step", "group_ready", "group_used"))
        ps = ph.psum("deg", [LANES, 512])
        block = ph.block()
        beside_work(ph, block, beside)

        @block.vector
        def _(dve):
            st = Steps(dve, step)
            st.then(dve.tensor_copy(key, scatter.rec[:, :, 3].bitcast(I32)))
            st.then(dve.tensor_tensor(bucket, key, scatter.rec[:, :, 1], ALU.subtract))
            st.then(dve.tensor_scalar_mul(bucket, bucket, 1.0 / P))
            st.then(dve.tensor_scalar_add(bucket, bucket, ROUND))
            st.then(dve.tensor_scalar_add(bucket, bucket, -ROUND))
            with dve.Fori(0, scatter.turns) as i:
                for h in range(2):
                    dve.wait_ge(used, i * 2 + (h + 1))
                    at = (i * 2 + h) * GROUP
                    dve.tensor_tensor(by_target[:, h, :, :], over(scatter.rec[:, bass.ds(at, GROUP), 1], P),
                                      across(c["lane"][0:parts, 0:P], GROUP), ALU.is_equal)
                    dve.tensor_tensor(by_bucket[:, h, :, 0:NT], over(bucket[:, bass.ds(at, GROUP)], NT),
                                      across(c["lane"][0:parts, 0:NT], GROUP), ALU.is_equal).then_inc(ready, 1)
            dve.wait_ge(used, 2 * scatter.turns + 2)
            st.then(dve.tensor_copy(degree, ps[0:P, 0:NT]))

        @block.tensor
        def _(pe):
            pe.sem_inc(used, 2)

            def turn(i, first=False, final=False):
                for h in range(2):
                    pe.wait_ge(ready, i * 2 + (h + 1))
                    for j in range(GROUP):
                        last = pe.matmul(ps[0:P, 0:NT], by_target[:, h, j, :], by_bucket[:, h, j, 0:NT],
                                         start=(first and h == 0 and j == 0), stop=(final and h == 1 and j == GROUP - 1))
                    last.then_inc(used, 1)

            turn(0, first=True)
            with pe.Fori(1, scatter.turns - 1) as i:
                turn(i)
            turn(scatter.turns - 1, final=True)


def load_records(nc, name, loads):
    with Phase(nc, name) as ph:
        s = ph.sem("loaded")
        block = ph.block()

        @block.sync
        def _(sp):
            for view, table in loads:
                sp.dma_start(view, table.rearrange("(t p) c -> p t c", p=LANES)).then_inc(s, 16)
            sp.wait_ge(s, 16 * len(loads))


def graph_sum(nc, name, c, arena, rows, rec, places, acc, tiles, weighted):
    a = Arena(arena, TMP_AT, REC_AT)
    msg = a.take(RING, GROUP, D)
    hot = a.take(RING, GROUP, P)
    own = a.take(RING, GROUP, 4)
    bodies = tiles // (RING * GROUP)
    with Phase(nc, name) as ph:
        turns = ph.sem("pool_turns")
        idx_ready = [ph.sem(f"idx_ready{h}") for h in range(RING)]
        gathered = c["pool_dma"]
        hot_ready = [ph.sem(f"hot_ready{h}") for h in range(RING)]
        summed = ph.sem("quads_summed")
        freed = ph.sem("psum_freed")
        step = ph.sem("dve_step")
        ps = ph.psum("sum", [LANES, 2, 4, D])
        block = ph.block()

        @block.scalar
        def _(act):
            with act.Fori(0, bodies) as i:
                for h in range(RING):
                    act.wait_ge(summed, i * QUADS + (2 * h + 2))
                    act.copy(own[:, h, :, :], rec[:, bass.ds((i * RING + h) * GROUP, GROUP), :])\
                       .then_inc(idx_ready[h], 1)

        @block.gpsimd
        def _(pool):
            with pool.Fori(0, bodies) as i:
                for h in range(RING):
                    pool.wait_ge(idx_ready[h], i + 1)
                    pool.sem_inc(turns, 1)
                    for j in range(GROUP):
                        pool.indirect_dma_start(
                            msg[:, h, j, :], None, rows,
                            bass.IndirectOffsetOnAxis(ap=own[:, h, j, 0:1].bitcast(U32), axis=0))\
                            .then_inc(gathered.sems[h], 16)

        @block.tensor
        def _(pe):
            pe.sem_inc(summed, QUADS)
            with pe.Fori(0, bodies) as i:
                for h in range(RING):
                    pe.wait_ge(hot_ready[h], i + 1)
                    gathered.wait(pe, h, i * GROUP + GROUP)
                    for q in range(2):
                        pe.wait_ge(freed, i * QUADS + (2 * h + q + 1))
                        for j in range(4):
                            t = 4 * q + j
                            last = pe.matmul(ps[0:P, q, j, :], hot[:, h, t, :], msg[:, h, t, :],
                                             start=True, stop=True)
                        last.then_inc(summed, 1)

        for h in range(RING):
            gathered.finished(h, GROUP * bodies)

        @block.vector
        def _(dve):
            st = Steps(dve, step)
            dve.sem_inc(freed, 2)
            st.then(dve.memset(acc, 0.0))
            def one_hot(i, h):
                dve.wait_ge(summed, i * QUADS + (2 * h + 2))
                dve.wait_ge(idx_ready[h], i + 1)
                if weighted:
                    for j in range(GROUP):
                        hit = dve.tensor_scalar(hot[:, h, j, :], c["lane"][:, 0:P], own[:, h, j, 1:2], own[:, h, j, 2:3],
                                                ALU.is_equal, ALU.mult)
                else:
                    hit = dve.tensor_tensor(hot[:, h, :, :], over(own[:, h, :, 1], P), across(c["lane"][:, 0:P], GROUP),
                                            ALU.is_equal)
                hit.then_inc(hot_ready[h], 1)

            def add_group(i, h):
                _, place = nc.values_load_multi_w_load_instructions(
                    places[0:1, bass.ds((i * RING + h) * GROUP, GROUP)], engines=(mybir.EngineType.DVE,),
                    min_val=0, max_val=(NT - 1) * D)
                for q in range(2):
                    dve.wait_ge(summed, i * QUADS + (QUADS + 2 * h + q + 1))
                    for j in range(4):
                        to = acc[:, bass.ds(place[4 * q + j], D)]
                        st.then(dve.tensor_tensor(to, to, ps[0:P, q, j, :], ALU.add))
                    dve.sem_inc(freed, 1)

            for h in range(RING):
                one_hot(0, h)
            with dve.Fori(0, bodies - 1) as i:
                st.enter(i, RING * GROUP)
                for h in range(RING):
                    add_group(i, h)
                    one_hot(i + 1, h)
            st.leave(bodies - 1)
            for h in range(RING):
                add_group(bodies - 1, h)


OUT_BANKS = 4


def quads():
    return [(t, min(4, NT - t)) for t in range(0, NT, 4)]


def flat(ap):
    return ap.rearrange("p a b -> p (a b)")


def to_features(nc, name, c, arena, y, yt, prepare, table=None, loads=(), roots=None, beside=None):
    with Phase(nc, name) as ph:
        loaded = ph.sem("loaded")
        step = ph.sem("dve_step")
        quad_ready = ph.sem("quad_ready")
        transposed = ph.sem("transposed")
        copied = ph.sem("copied")
        stored = ph.sem("stored")
        asked = ph.sem("root_asked")
        rooted = ph.sem("root_ready")
        ps = ph.psum("t", [LANES, 8, 512])
        block = ph.block()

        beside_work(ph, block, beside)

        @block.sync
        def _(sp):
            for to, of in loads:
                sp.dma_start(to, of).then_inc(loaded, 16)
            if table is not None:
                rows = table.rearrange("(t p) d -> p t d", p=P)
                for q, (t, n) in enumerate(quads()):
                    sp.wait_ge(quad_ready, q + 1)
                    sp.dma_start(rows[:, t:t + n, :], y[:, t:t + n, :]).then_inc(stored, 16)
                sp.wait_ge(stored, 16 * len(quads()))

        @block.vector
        def _(dve):
            st = Steps(dve, step)
            if loads:
                dve.wait_ge(loaded, 16 * len(loads))
            prepare(dve, st, quad_ready, asked, rooted)

        @block.tensor
        def _(pe):
            for q, (t, n) in enumerate(quads()):
                pe.wait_ge(quad_ready, q + 1)
                for k in range(DK):
                    u = DK * q + k
                    if u >= 8:
                        pe.wait_ge(copied, u - 7)
                    for j in range(n):
                        last = pe.transpose(ps[:, u % 8, j * P:(j + 1) * P],
                                            y[:, t + j, k * LANES:(k + 1) * LANES], c["ident"][0:P, 0:P])
                    last.then_inc(transposed, 1)

        @block.scalar
        def _(act):
            if roots is not None:
                act.wait_ge(asked, 1)
                act.activation(roots, roots, ACT.Sqrt).then_inc(rooted, 1)
            for q, (t, n) in enumerate(quads()):
                for k in range(DK):
                    u = DK * q + k
                    act.wait_ge(transposed, u + 1)
                    act.copy(yt[:, k, t * P:(t + n) * P], ps[:, u % 8, 0:n * P]).then_inc(copied, 1)


def row_statistics(dve, st, x, stats, mean, root, spare):
    with dve.Fori(0, NT) as t:
        dve.bn_stats(stats[:, bass.ds(t, 1), :].rearrange("p a b -> p (a b)"),
                     x[:, bass.ds(t, 1), :].rearrange("p a b -> p (a b)")).then_inc(st.sem, 1)
    st.n += NT
    st.eng.wait_ge(st.sem, st.n)
    half = D // 2
    st.then(dve.tensor_tensor(mean, stats[:, :, 1], stats[:, :, 4], ALU.add))
    st.then(dve.tensor_scalar_mul(mean, mean, 0.5))
    st.then(dve.tensor_tensor(spare, stats[:, :, 1], mean, ALU.subtract))
    st.then(dve.tensor_tensor(spare, spare, spare, ALU.mult))
    st.then(dve.tensor_tensor(root, stats[:, :, 2], stats[:, :, 5], ALU.add))
    st.then(dve.scalar_tensor_tensor(root, root, 1.0 / (2 * half), spare, ALU.mult, ALU.add))
    return dve.tensor_scalar_add(root, root, EPS)


def layer_norm(nc, name, c, arena, x, y, yt, table=None, loads=(), beside=None):
    a = Arena(arena, TMP_AT)
    stats = a.take(NT, 6, rows=P)
    mean, root, spare = (a.take(NT, rows=P) for _ in range(3))

    def prepare(dve, st, quad_ready, asked, rooted):
        row_statistics(dve, st, x, stats, mean, root, spare).then_inc(asked, 1)
        dve.wait_ge(rooted, 1)
        st.then(dve.reciprocal(root, root))
        for t, n in quads():
            part = y[:, t:t + n, :]
            st.then(dve.tensor_tensor(part, x[:, t:t + n, :], over(mean[:, t:t + n], D), ALU.subtract))
            dve.tensor_tensor(part, part, over(root[:, t:t + n], D), ALU.mult).then_inc(quad_ready, 1)

    to_features(nc, name, c, arena, y, yt, prepare, table, loads, roots=root, beside=beside)


def dense(nc, name, products, bias, out, func, stats=None, beside=None):
    m = out.shape[1]
    with Phase(nc, name) as ph:
        loaded = ph.sem("weights_loaded")
        multiplied = ph.sem("multiplied")
        written = ph.sem("written")
        free = ph.sem("psum_free")
        counted = ph.sem("stats_done")
        ps = ph.psum("out", [LANES, m, 512])
        block = ph.block()
        beside_work(ph, block, beside)

        @block.sync
        def _(sp):
            for _, w, w_dram in products:
                sp.dma_start(w, w_dram.rearrange("(k p) f -> p k f", p=LANES)).then_inc(loaded, 16)

        @block.tensor
        def _(pe):
            pe.wait_ge(loaded, 16 * len(products) + 16)

            def chunk(n, at, cols):
                for fo in range(m):
                    pe.wait_ge(free, n * m + (fo + 1))
                    parts = [(rhs, w, k) for rhs, w, _ in products for k in range(w.shape[1])]
                    for i, (rhs, w, k) in enumerate(parts):
                        last = pe.matmul(ps[:, fo, 0:cols], w[:, k, fo * LANES:(fo + 1) * LANES],
                                         rhs[:, k, bass.ds(at, cols)], start=(i == 0), stop=(i == len(parts) - 1))
                    last.then_inc(multiplied, 1)

            with pe.Fori(0, FULL) as n:
                chunk(n, n * CHUNK, CHUNK)
            chunk(FULL, FULL * CHUNK, N - FULL * CHUNK)

        @block.scalar
        def _(act):
            with nc.allow_non_contiguous_dma(reason="a column of biases"):
                act.dma_start(bias[0], bias[1].rearrange("(m p) -> p m", p=LANES)).then_inc(loaded, 16)
            act.wait_ge(loaded, 16 * len(products) + 16)
            act.sem_inc(free, m)

            def chunk(n, at, cols):
                for fo in range(m):
                    act.wait_ge(multiplied, n * m + (fo + 1))
                    act.activation(out[:, fo, bass.ds(at, cols)], ps[:, fo, 0:cols], func,
                                   bias=bias[0][:, fo:fo + 1]).then_inc(free, 1)

            with act.Fori(0, FULL) as n:
                chunk(n, n * CHUNK, CHUNK)
            chunk(FULL, FULL * CHUNK, N - FULL * CHUNK)

        @block.vector
        def _(dve):
            if stats is None:
                return

            def chunk(n, at, cols):
                for fo in range(m):
                    dve.wait_ge(free, n * m + (m + fo + 1))
                    dve.bn_stats(stats[:, fo, bass.ds(n * 6, 6)], out[:, fo, bass.ds(at, cols)])

            with dve.Fori(0, FULL) as n:
                chunk(n, n * CHUNK, CHUNK)
            chunk(FULL, FULL * CHUNK, N - FULL * CHUNK)


def batch_norm_elu(nc, name, a, h, stats, gamma, beta, beside=None):
    m = h.shape[1]
    mv = a.take(m, 2)
    g, b, scale, shift = (a.take(m) for _ in range(4))
    e = a.take(2, N)
    with Phase(nc, name) as ph:
        loaded = ph.sem("loaded")
        step = ph.sem("dve_step")
        asked = ph.sem("root_asked")
        rooted = ph.sem("root_ready")
        scaled = ph.sem("scale_ready")
        act_step = ph.sem("act_step")
        split = ph.sem("split_ready")
        freed = ph.sem("exp_freed")
        block = ph.block()
        beside_work(ph, block, beside)

        @block.sync
        def _(sp):
            with nc.allow_non_contiguous_dma(reason="a column of parameters"):
                sp.dma_start(g, gamma.rearrange("(m p) -> p m", p=LANES)).then_inc(loaded, 16)
                sp.dma_start(b, beta.rearrange("(m p) -> p m", p=LANES)).then_inc(loaded, 16)

        @block.vector
        def _(dve):
            st = Steps(dve, step)
            for f in range(m):
                st.done(dve.bn_aggr(mv[:, f, :], stats[:, f, :]))
            dve.wait_ge(step, m)
            dve.tensor_scalar_add(scale, mv[:, :, 1], EPS).then_inc(asked, 1)
            dve.wait_ge(rooted, 1)
            st.then(dve.reciprocal(scale, scale))
            dve.wait_ge(loaded, 32)
            st.then(dve.tensor_tensor(scale, scale, g, ALU.mult))
            st.then(dve.tensor_tensor(shift, mv[:, :, 0], scale, ALU.mult))
            dve.tensor_tensor(shift, b, shift, ALU.subtract).then_inc(scaled, 1)
            for f in range(m):
                dve.wait_ge(split, f + 1)
                st.then(dve.tensor_scalar(e[:, f % 2, :], e[:, f % 2, :], 1.0, -1.0, ALU.min, ALU.add))
                dve.tensor_tensor(h[:, f, :], h[:, f, :], e[:, f % 2, :], ALU.add).then_inc(freed, 1)

        @block.scalar
        def _(act):
            act.wait_ge(asked, 1)
            act.activation(scale, scale, ACT.Sqrt).then_inc(rooted, 1)
            act.wait_ge(scaled, 1)
            for f in range(m):
                if f >= 2:
                    act.wait_ge(freed, f - 1)
                act.activation(e[:, f % 2, :], h[:, f, :], ACT.Exp, bias=shift[:, f:f + 1],
                               scale=scale[:, f:f + 1]).then_inc(act_step, 1)
                act.wait_ge(act_step, f + 1)
                act.activation(h[:, f, :], h[:, f, :], ACT.Relu, bias=shift[:, f:f + 1],
                               scale=scale[:, f:f + 1]).then_inc(split, 1)


def project(nc, name, ht, w, w_dram, out, bias=None, add=False, loads=(), table=None, beside=None):
    with Phase(nc, name) as ph:
        loaded = ph.sem("loaded")
        multiplied = ph.sem("multiplied")
        added = ph.sem("added")
        step = ph.sem("dve_step")
        stored = ph.sem("stored")
        ps = ph.psum("out", [LANES, 8, 512])
        block = ph.block()
        beside_work(ph, block, beside)
        ks = w.shape[1]
        n_loads = 1 + (bias is not None) + len(loads)

        @block.sync
        def _(sp):
            sp.dma_start(w, w_dram.rearrange("(k p) f -> p k f", p=LANES)).then_inc(loaded, 16)
            if bias is not None:
                sp.dma_start(bias[0], bias[1].unsqueeze(0).to_broadcast([P, D])).then_inc(loaded, 16)
            for to, of in loads:
                sp.dma_start(to, of).then_inc(loaded, 16)
            if table is not None:
                rows = table.rearrange("(t p) d -> p t d", p=P)
                for t, n in quads():
                    sp.wait_ge(added, t + n)
                    sp.dma_start(rows[:, t:t + n, :], out[:, t:t + n, :]).then_inc(stored, 16)
                sp.wait_ge(stored, 16 * len(quads()))

        @block.tensor
        def _(pe):
            pe.wait_ge(loaded, 16 * n_loads)
            for t in range(NT):
                if t >= 8:
                    pe.wait_ge(added, t - 7)
                for k in range(ks):
                    last = pe.matmul(ps[0:P, t % 8, 0:D], ht[:, k, t * P:(t + 1) * P], w[:, k, :],
                                     start=(k == 0), stop=(k == ks - 1))
                last.then_inc(multiplied, 1)

        @block.vector
        def _(dve):
            st = Steps(dve, step)
            dve.wait_ge(loaded, 16 * n_loads)
            if add and bias is not None:
                st.then(dve.tensor_tensor(out, out, across(bias[0], NT), ALU.add))
            for t in range(NT):
                dve.wait_ge(multiplied, t + 1)
                if add:
                    dve.tensor_tensor(out[:, t, :], out[:, t, :], ps[0:P, t % 8, 0:D], ALU.add).then_inc(added, 1)
                elif bias is not None:
                    dve.tensor_tensor(out[:, t, :], bias[0], ps[0:P, t % 8, 0:D], ALU.add).then_inc(added, 1)
                else:
                    dve.tensor_copy(out[:, t, :], ps[0:P, t % 8, 0:D]).then_inc(added, 1)


def add_scaled(nc, name, x, acc, scale=None, bias=None):
    with Phase(nc, name) as ph:
        loaded = ph.sem("loaded")
        step = ph.sem("dve_step")
        block = ph.block()

        @block.sync
        def _(sp):
            if bias is not None:
                sp.dma_start(bias[0], bias[1].unsqueeze(0).to_broadcast([P, D])).then_inc(loaded, 16)

        @block.vector
        def _(dve):
            st = Steps(dve, step)
            if scale is not None:
                st.then(dve.tensor_tensor(acc, acc, over(scale, D), ALU.mult))
            if bias is not None:
                dve.wait_ge(loaded, 16)
                st.then(dve.tensor_tensor(acc, acc, across(bias[0], NT), ALU.add))
            st.then(dve.tensor_tensor(x, x, acc, ALU.add))


def experts(nc, name, c, a, yt, target, hidden, last_w, gates, bias_gates, last_b, count, func, beside=None):
    widths = [w.shape[2] for w, _ in hidden]
    ins = [D] + widths
    w_sb = [a.take(2, ins[i] // LANES * widths[i]).rearrange("p h (k f) -> p h k f", f=widths[i])
            for i in range(len(hidden))]
    b_sb = [a.take(2, widths[i] // LANES) for i in range(len(hidden))]
    wl_sb = a.take(2, widths[-1] // LANES * D).rearrange("p h (k f) -> p h k f", f=D)
    h_sb = [a.take(2, widths[i] // LANES * CHUNK).rearrange("p h (k f) -> p h k f", f=CHUNK)
            for i in range(len(hidden))]
    gate = a.take(2, NT, rows=P)
    n_bias = bias_gates.shape[2]
    gates_t = a.take(N, rows=n_bias)
    lb_sb = a.take(D, rows=n_bias)
    turns = count // 2
    assert turns * 2 == count
    n_w = 2 * len(hidden) + 1
    stages = len(hidden) + 1
    n_ch = len(CHUNKS)
    units = [w // LANES for w in widths]

    def order():
        for at in range(n_ch + stages - 1):
            for s in range(stages):
                if 0 <= at - s < n_ch:
                    yield s, at - s

    with Phase(nc, name) as ph:
        loaded = [ph.sem(f"weights_loaded{h}") for h in range(2)]
        small_loaded = ph.sem("last_bias_loaded")
        multiplied = [ph.sem(f"multiplied{s}") for s in range(stages)]
        written = [ph.sem(f"written{s}") for s in range(stages - 1)]
        added = ph.sem("added")
        gate_ready = ph.sem("gate_ready")
        g_t = ph.sem("gates_transposed")
        g_c = ph.sem("gates_copied")
        b_m = ph.sem("bias_multiplied")
        step = ph.sem("dve_step")
        ps_h = ph.psum("hidden", [LANES, 4, 512])
        ps_o = ph.psum("out", [LANES, OUT_BANKS, 2, D])
        banks = [list(range(4))] if stages == 2 else [[0, 1], [2, 3]]
        block = ph.block()
        beside_work(ph, block, beside)

        def hid(i, h, n, s):
            return i * (2 * n_ch * units[s]) + (h * n_ch + n) * units[s]

        pairs = [(t, min(2, NT - t)) for t in range(0, NT, 2)]
        per_turn = 2 * len(pairs)

        def last_use(u):
            return max(v for v in range(-per_turn, u) if v % per_turn % OUT_BANKS == u % OUT_BANKS) + 1 + per_turn

        @block.sync
        def _(sp):
            sp.dma_start(lb_sb, last_b).then_inc(small_loaded, 16)
            with sp.Fori(0, turns) as i:
                for h in range(2):
                    e = i * 2 + h
                    sp.wait_ge(multiplied[-1], i * per_turn + (h + 1) * len(pairs))
                    for j, (w, b) in enumerate(hidden):
                        sp.dma_start(w_sb[j][:, h, :, :],
                                     w[bass.ds(e, 1), :, :].rearrange("e (k p) f -> p (e k) f", p=LANES))\
                            .then_inc(loaded[h], 16)
                        with nc.allow_non_contiguous_dma(reason="a column of biases"):
                            sp.dma_start(b_sb[j][:, h, :], b[bass.ds(e, 1), :].rearrange("e (m p) -> p (e m)", p=LANES))\
                                .then_inc(loaded[h], 16)
                    sp.dma_start(wl_sb[:, h, :, :],
                                 last_w[bass.ds(e, 1), :, :].rearrange("e (k p) f -> p (e k) f", p=LANES))\
                        .then_inc(loaded[h], 16)

        @block.tensor
        def _(pe):
            for q, (t, n) in enumerate(quads()):
                if q >= 4:
                    pe.wait_ge(g_c, q - 3)
                for j in range(n):
                    last = pe.transpose(ps_h[0:n_bias, q % 4, j * P:(j + 1) * P], bias_gates[:, t + j, :],
                                        c["ident"][0:P, 0:P])
                last.then_inc(g_t, 1)
            pe.wait_ge(small_loaded, 16)
            for t in range(NT):
                if t % 4 == 0:
                    pe.wait_ge(g_c, t // 4 + 1)
                if t >= OUT_BANKS:
                    pe.wait_ge(step, t - OUT_BANKS + 1)
                pe.matmul(ps_o[0:P, t % OUT_BANKS, 0, :], gates_t[:, t * P:(t + 1) * P], lb_sb, start=True, stop=True)\
                    .then_inc(b_m, 1)
            pe.wait_ge(step, NT)
            pe.sem_inc(multiplied[-1], per_turn)
            with pe.Fori(0, turns) as i:
                for h in range(2):
                    pe.wait_ge(loaded[h], i * (16 * n_w) + 16 * n_w)
                    for s, n in order():
                        at, cols = CHUNKS[n]
                        if s < stages - 1:
                            if s > 0:
                                pe.wait_ge(written[s - 1], hid(i, h, n + 1, s - 1) + len(banks[s - 1]))
                            for m in range(units[s]):
                                pe.wait_ge(written[s], hid(i, h, n, s) + (m + 1))
                                ks = ins[s] // LANES
                                bank = banks[s][m % len(banks[s])]
                                for k in range(ks):
                                    rhs = yt[:, k, at:at + cols] if s == 0 else h_sb[s - 1][:, n % 2, k, 0:cols]
                                    last = pe.matmul(ps_h[:, bank, 0:cols],
                                                     w_sb[s][:, h, k, m * LANES:(m + 1) * LANES], rhs,
                                                     start=(k == 0), stop=(k == ks - 1))
                                last.then_inc(multiplied[s], 1)
                        else:
                            pe.wait_ge(written[s - 1], hid(i, h, n + 1, s - 1) + len(banks[s - 1]))
                            ks = widths[-1] // LANES
                            for u, (t, tiles) in enumerate(pairs):
                                if not 4 * n <= t < 4 * n + 4:
                                    continue
                                v = h * len(pairs) + u
                                pe.wait_ge(added, i * per_turn + last_use(v))
                                for j in range(tiles):
                                    col = (t + j - 4 * n) * P
                                    for k in range(ks):
                                        last = pe.matmul(ps_o[0:P, v % OUT_BANKS, j, :],
                                                         h_sb[s - 1][:, n % 2, k, col:col + P], wl_sb[:, h, k, :],
                                                         start=(k == 0), stop=(k == ks - 1))
                                last.then_inc(multiplied[s], 1)

        @block.scalar
        def _(act):
            for q, (t, n) in enumerate(quads()):
                act.wait_ge(g_t, q + 1)
                act.copy(gates_t[:, t * P:(t + n) * P], ps_h[0:n_bias, q % 4, 0:n * P]).then_inc(g_c, 1)
            for s in range(stages - 1):
                act.sem_inc(written[s], len(banks[s]))
            with act.Fori(0, turns) as i:
                for h in range(2):
                    act.wait_ge(loaded[h], i * (16 * n_w) + 16 * n_w)
                    for s, n in order():
                        if s == stages - 1:
                            continue
                        at, cols = CHUNKS[n]
                        for m in range(units[s]):
                            act.wait_ge(multiplied[s], hid(i, h, n, s) + (m + 1))
                            act.activation(h_sb[s][:, n % 2, m, 0:cols],
                                           ps_h[:, banks[s][m % len(banks[s])], 0:cols], func,
                                           bias=b_sb[s][:, h, m:m + 1]).then_inc(written[s], 1)

        @block.vector
        def _(dve):
            st = Steps(dve, step)
            for t in range(NT):
                dve.wait_ge(b_m, t + 1)
                st.done(dve.tensor_tensor(target[:, t, :], target[:, t, :], ps_o[0:P, t % OUT_BANKS, 0, :], ALU.add))
            dve.wait_ge(step, NT)
            dve.sem_inc(added, per_turn)
            with dve.Fori(0, turns) as i:
                dve.wait_ge(added, i * per_turn + per_turn)
                for h in range(2):
                    dve.tensor_copy(gate[:, h, :], gates[:, :, bass.ds(i * 2 + h, 1)].rearrange("p t e -> p (t e)"))\
                       .then_inc(gate_ready, 1)
                for h in range(2):
                    dve.wait_ge(gate_ready, i * 2 + 2)
                    for u, (t, tiles) in enumerate(pairs):
                        v = h * len(pairs) + u
                        dve.wait_ge(multiplied[-1], i * per_turn + (per_turn + v + 1))
                        for j in range(tiles):
                            last = dve.scalar_tensor_tensor(target[:, t + j, :], ps_o[0:P, v % OUT_BANKS, j, :],
                                                            gate[:, h, t + j:t + j + 1], target[:, t + j, :],
                                                            ALU.mult, ALU.add)
                        last.then_inc(added, 1)


PAIR_TILE = 256


def pair_tiles(experts_n):
    most = (2 * N + experts_n * (PAIR_TILE - 1)) // PAIR_TILE
    return most + most % 2


PAIR_ROWS = pair_tiles(16) * PAIR_TILE


def send_to_experts(nc, name, c, a, y, one, two, slots, expert_of, table):
    e = one.shape[2]
    tiles = pair_tiles(e)
    both = a.take(NT, e, rows=P)
    run = a.take(NT, e, rows=P)
    total = a.take(e, rows=P)
    tiles_of, upto, first = a.take(e), a.take(e), a.take(e)
    cmp = a.take(tiles, e, rows=1)
    exp_f = a.take(tiles, rows=1)
    slot_f = a.take(NT, rows=P)
    index = a.take(tiles, rows=1)
    index_i = a.take(tiles, rows=1, dtype=I32)
    before = a.take(LANES)
    with Phase(nc, name) as ph:
        step, counted, ready, set_ = (ph.sem(x) for x in ("dve_step", "counted", "slots_ready", "constants_set"))
        totals = ph.sem("totals_ready")
        sent = c["pool_dma"]
        ps = ph.psum("sums", [LANES, 2, 512])
        block = ph.block()

        @block.vector
        def _(dve):
            st = Steps(dve, step)
            tt = dve.tensor_tensor
            st.then(tt(both, one, two, ALU.add))
            tt_total = dve.tensor_reduce(total, both.rearrange("p t e -> p e t"), AX.X, ALU.add)
            tt_total.then_inc(totals, 1)
            dve.wait_ge(counted, 1)
            st.then(dve.tensor_scalar(tiles_of, ps[:, 0, 0:e], PAIR_TILE / 2 - 0.5, 1.0 / PAIR_TILE, ALU.add, ALU.mult))
            st.then(dve.tensor_scalar_add(tiles_of, tiles_of, ROUND))
            st.then(dve.tensor_scalar_add(tiles_of, tiles_of, -ROUND))
            st.then(dve.tensor_tensor_scan(upto, c["ones"][:, 0:e], tiles_of, 0.0, ALU.mult, ALU.add))
            st.then(tt(first, upto, tiles_of, ALU.subtract))
            st.then(dve.tensor_scalar(first, first, float(PAIR_TILE), -1.0, ALU.mult, ALU.add))
            st.then(tt(first[0:P], first[0:P], ps[0:P, 1, 0:e], ALU.add))
            for x in range(e):
                st.done(dve.tensor_tensor_scan(run[:, :, x], c["ones"][0:P, 0:NT], both[:, :, x], first[0:P, x:x + 1],
                                               ALU.mult, ALU.add))
            st.all()
            for i, pick in enumerate((one, two)):
                st.then(tt(both, pick, run, ALU.mult))
                st.then(dve.tensor_reduce(slot_f, both, AX.X, ALU.add))
                st.then(dve.tensor_copy(slots[:, i, :], slot_f))
            dve.sem_inc(ready, 1)
            dve.wait_ge(set_, 4)
            st.then(dve.tensor_copy(index, index_i))
            st.then(tt(cmp, across(upto[0:1], tiles), over(index, e), ALU.is_le))
            st.then(dve.tensor_reduce(exp_f, cmp, AX.X, ALU.add))
            st.then(dve.tensor_scalar(expert_of, exp_f, float(e - 1), 1.0, ALU.min, ALU.mult))

        @block.tensor
        def _(pe):
            pe.wait_ge(totals, 1)
            pe.wait_ge(set_, 4)
            pe.matmul(ps[:, 0, 0:e], c["ones"][0:P, :], total, start=True, stop=True)
            pe.matmul(ps[:, 1, 0:e], before[0:P, :], total, start=True, stop=True).then_inc(counted, 1)

        @block.gpsimd
        def _(pool):
            pool.iota(index_i, pattern=[[1, tiles]], base=0, channel_multiplier=0).then_inc(set_, 1)
            pool.memset(before, 0.0).then_inc(set_, 1)
            pool.wait_ge(set_, 2)
            pool.affine_select(out=before, in_=before, compare_op=ALU.is_ge, fill=1.0, base=0,
                               pattern=[[-1, LANES]], channel_multiplier=1).then_inc(set_, 2)
            pool.wait_ge(ready, 1)
            pool.wait_ge(c["table_zero"], 16 * c["table_zero_dmas"])
            for t in range(NT):
                for i in range(2):
                    pool.indirect_dma_start(
                        table, bass.IndirectOffsetOnAxis(ap=slots[:, i, t:t + 1].bitcast(U32), axis=0),
                        y[:, t, :], None).then_inc(sent.sems[0], 16)
            sent.wait(pool, 0, 2 * NT)
            sent.finished(0, 2 * NT)


def run_experts(nc, name, c, a, table, expert_of, w1, b1, w2, b2, out_table, func):
    e, _, f = w1.shape
    tiles = pair_tiles(e)
    fk = f // LANES
    w1_sb = [a.take(DK, f) for _ in range(2)]
    w2_sb = [a.take(fk, D) for _ in range(2)]
    b1_sb = [a.take(fk) for _ in range(2)]
    b2_sb = [a.take(D) for _ in range(2)]
    xs = [a.take(2, D) for _ in range(2)]
    xt = [a.take(DK, PAIR_TILE) for _ in range(2)]
    hid = [a.take(fk, PAIR_TILE) for _ in range(2)]
    res = [a.take(2, D) for _ in range(2)]
    rows_in = table.rearrange("(t s p) d -> t p s d", p=LANES, s=2)
    rows_out = out_table.rearrange("(t s p) d -> t p s d", p=LANES, s=2)
    with Phase(nc, name) as ph:
        weights = [ph.sem(f"weights_loaded{h}") for h in range(2)]
        rows = [ph.sem(f"rows_loaded{h}") for h in range(2)]
        turned = ph.sem("rows_turned")
        turned_copied = ph.sem("rows_copied")
        first_done = ph.sem("first_products")
        hidden = ph.sem("hidden_written")
        last_done = ph.sem("last_products")
        written = ph.sem("results_written")
        stored = c["pool_dma"]
        counts = ph.sem("pool_turns")
        ps_t = ph.psum("t", [LANES, DK, PAIR_TILE])
        ps_h = ph.psum("h", [LANES, fk, 512])
        ps_o = ph.psum("o", [LANES, 2, 2, D])
        turns = tiles // 2
        block = ph.block()

        @block.sync
        def _(sp):
            def load_rows(t, h):
                sp.dma_start(xs[h], rows_in[bass.ds(t, 1)].rearrange("t p s d -> p (t s) d")).then_inc(rows[h], 16)

            load_rows(0, 0)

            def load_tile(t, h, more=True):
                ex = sp.value_load(expert_of[0:1, bass.ds(t, 1)], min_val=0, max_val=e - 1)
                sp.wait_ge(last_done, t + 1)
                sp.wait_ge(written, t + 1)
                sp.dma_start(w1_sb[h], w1[bass.ds(ex, 1), :, :].rearrange("e (k p) f -> p (e k) f", p=LANES))\
                  .then_inc(weights[h], 16)
                with nc.allow_non_contiguous_dma(reason="a column of biases"):
                    sp.dma_start(b1_sb[h], b1[bass.ds(ex, 1), :].rearrange("e (m p) -> p (e m)", p=LANES))\
                      .then_inc(weights[h], 16)
                sp.dma_start(w2_sb[h], w2[bass.ds(ex, 1), :, :].rearrange("e (k p) f -> p (e k) f", p=LANES))\
                  .then_inc(weights[h], 16)
                sp.dma_start(b2_sb[h], b2[bass.ds(ex, 1), :].to_broadcast([LANES, D])).then_inc(weights[h], 16)
                if more:
                    sp.wait_ge(turned, t + 1)
                    load_rows(t + 1, 1 - h)

            with sp.Fori(0, turns - 1) as i:
                for h in range(2):
                    load_tile(i * 2 + h, h)
            load_tile(tiles - 2, 0)
            load_tile(tiles - 1, 1, more=False)

        @block.tensor
        def _(pe):
            def turn(t, h, n):
                pe.wait_ge(rows[h], n)
                for s in range(2):
                    for k in range(DK):
                        last = pe.transpose(ps_t[:, k, s * LANES:(s + 1) * LANES], xs[h][:, s, k * LANES:(k + 1) * LANES],
                                            c["ident"])
                last.then_inc(turned, 1)

            def first(t, h):
                pe.wait_ge(weights[h], (t - h) * 32 + 64)
                pe.wait_ge(turned_copied, t + 1)
                for m in range(fk):
                    pe.wait_ge(hidden, t * fk + (m + 1))
                    for k in range(DK):
                        last = pe.matmul(ps_h[:, m, 0:PAIR_TILE], w1_sb[h][:, k, m * LANES:(m + 1) * LANES],
                                         xt[h][:, k, :], start=(k == 0), stop=(k == DK - 1))
                    last.then_inc(first_done, 1)

            def second(t, h):
                pe.wait_ge(hidden, t * fk + 2 * fk)
                pe.wait_ge(written, t + 1)
                for s in range(2):
                    for m in range(fk):
                        last = pe.matmul(ps_o[:, h, s, :], hid[h][:, m, s * LANES:(s + 1) * LANES], w2_sb[h][:, m, :],
                                         start=(m == 0), stop=(m == fk - 1))
                last.then_inc(last_done, 1)

            pe.sem_inc(last_done, 2)
            pe.sem_inc(turned, 1)
            turn(0, 0, 16)
            with pe.Fori(0, turns - 1) as i:
                first(i * 2, 0)
                turn(i * 2 + 1, 1, i * 16 + 16)
                second(i * 2, 0)
                first(i * 2 + 1, 1)
                turn(i * 2 + 2, 0, i * 16 + 32)
                second(i * 2 + 1, 1)
            t = tiles - 2
            first(t, 0)
            turn(t + 1, 1, 16 * turns)
            second(t, 0)
            first(t + 1, 1)
            second(t + 1, 1)

        @block.scalar
        def _(act):
            act.sem_inc(hidden, fk)

            def copy_turned(t, h):
                act.wait_ge(turned, t + 2)
                act.copy(xt[h], ps_t[:, :, :]).then_inc(turned_copied, 1)

            def relu(t, h):
                act.wait_ge(weights[h], (t - h) * 32 + 64)
                for m in range(fk):
                    act.wait_ge(first_done, t * fk + (m + 1))
                    act.activation(hid[h][:, m, :], ps_h[:, m, 0:PAIR_TILE], func, bias=b1_sb[h][:, m:m + 1])\
                       .then_inc(hidden, 1)

            copy_turned(0, 0)
            with act.Fori(0, turns - 1) as i:
                relu(i * 2, 0)
                copy_turned(i * 2 + 1, 1)
                relu(i * 2 + 1, 1)
                copy_turned(i * 2 + 2, 0)
            relu(tiles - 2, 0)
            copy_turned(tiles - 1, 1)
            relu(tiles - 1, 1)

        @block.vector
        def _(dve):
            dve.sem_inc(written, 2)
            with dve.Fori(0, turns) as i:
                for h in range(2):
                    t = i * 2 + h
                    dve.wait_ge(weights[h], i * 64 + 64)
                    dve.wait_ge(last_done, t + 3)
                    dve.wait_ge(counts, t + 1)
                    dve.tensor_tensor(res[h], ps_o[:, h, :, :], across(b2_sb[h], 2), ALU.add).then_inc(written, 1)

        @block.gpsimd
        def _(pool):
            pool.sem_inc(counts, 2)

            def store(t, h):
                pool.wait_ge(written, t + 3)
                pool.dma_start(rows_out[bass.ds(t, 1)].rearrange("t p s d -> p (t s) d"), res[h])\
                    .then_inc(stored.sems[h], 16)

            store(0, 0)
            store(1, 1)
            with pool.Fori(1, turns) as i:
                for h in range(2):
                    stored.wait(pool, h, i)
                    pool.sem_inc(counts, 1)
                    store(i * 2 + h, h)
            for h in range(2):
                stored.wait(pool, h, turns)
                stored.finished(h, turns)


def combine(nc, name, c, a, out_table, slots, w_one, w_two, target):
    buf = a.take(RING, 2, D, rows=P)
    with Phase(nc, name) as ph:
        added = ph.sem("rows_added")
        fetched = c["pool_dma"]
        block = ph.block()

        @block.gpsimd
        def _(pool):
            for t in range(NT):
                if t >= RING:
                    pool.wait_ge(added, 2 * (t - RING) + 2)
                for i in range(2):
                    pool.indirect_dma_start(
                        buf[:, t % RING, i, :], None, out_table,
                        bass.IndirectOffsetOnAxis(ap=slots[:, i, t:t + 1].bitcast(U32), axis=0))\
                        .then_inc(fetched.sems[t % RING], 16)

        @block.vector
        def _(dve):
            for t in range(NT):
                fetched.wait(dve, t % RING, 2 * (t // RING) + 2)
                for i, w in enumerate((w_one, w_two)):
                    if i:
                        dve.wait_ge(added, 2 * t + 1)
                    dve.scalar_tensor_tensor(target[:, t, :], buf[:, t % RING, i, :], w[:, t:t + 1],
                                             target[:, t, :], ALU.mult, ALU.add).then_inc(added, 1)

        for h in range(RING):
            fetched.finished(h, 2 * len(range(h, NT, RING)))


def best_two(dve, st, c, scores, gates, tmp, asked, answered):
    e = scores.shape[2]
    rank, one, two, rest, m1, m2, exp, total = tmp
    pick = dve.tensor_tensor
    st.then(dve.tensor_scalar(rank, c["lane"][0:P, 0:e], -1.0, float(e), ALU.mult, ALU.add))

    def best(of, out, value):
        st.then(dve.tensor_reduce(value, of, AX.X, ALU.max))
        st.then(pick(out, of, over(value, e), ALU.is_equal))
        st.then(pick(out, out, across(rank, NT), ALU.mult))
        st.then(dve.tensor_reduce(total, out, AX.X, ALU.max))
        st.then(pick(out, out, over(total, e), ALU.is_equal))

    best(scores, one, m1)
    st.then(dve.scalar_tensor_tensor(rest, one, -BIG, scores, ALU.mult, ALU.add))
    best(rest, two, m2)
    pick(exp, m2, m1, ALU.subtract).then_inc(asked, 1)
    dve.wait_ge(answered, 1)
    st.then(dve.tensor_scalar_add(total, exp, 1.0))
    st.then(dve.reciprocal(total, total))
    st.then(pick(exp, exp, total, ALU.mult))
    if gates is not None:
        st.then(pick(one, one, over(total, e), ALU.mult))
        st.then(pick(two, two, over(exp, e), ALU.mult))
        st.then(pick(gates, one, two, ALU.add))


def best_two_places(a, e):
    return (a.take(e, rows=P), a.take(NT, e, rows=P), a.take(NT, e, rows=P), a.take(NT, e, rows=P),
            a.take(NT, rows=P), a.take(NT, rows=P), a.take(NT, rows=P), a.take(NT, rows=P))


def router(nc, name, c, a, src_t, w_dram, b_dram, scores, gates=None, softmax=False, picks=None):
    e = scores.shape[2]
    ks = src_t.shape[1]
    w = a.take(ks, e)
    b = a.take(e, rows=P)
    top, total = a.take(NT, rows=P), a.take(NT, rows=P)
    tmp = picks or (best_two_places(a, e) if gates is not None else None)
    with Phase(nc, name) as ph:
        loaded = ph.sem("loaded")
        multiplied = ph.sem("multiplied")
        step = ph.sem("dve_step")
        soft = ph.sem("softmax_asked")
        soft_done = ph.sem("softmax_done")
        asked = ph.sem("exp_asked")
        answered = ph.sem("exp_done")
        ps = ph.psum("scores", [LANES, 512])
        view = ps[0:P, 0:NT * e].rearrange("p (t e) -> p t e", e=e)
        block = ph.block()

        @block.sync
        def _(sp):
            with nc.allow_non_contiguous_dma(reason="few scores: short rows"):
                sp.dma_start(w, w_dram.rearrange("(k p) e -> p k e", p=LANES)).then_inc(loaded, 16)
            sp.dma_start(b, b_dram.unsqueeze(0).to_broadcast([P, e])).then_inc(loaded, 16)

        @block.tensor
        def _(pe):
            pe.wait_ge(loaded, 32)
            for t in range(NT):
                for k in range(ks):
                    last = pe.matmul(view[:, t, :], src_t[:, k, t * P:(t + 1) * P], w[:, k, :],
                                     start=(k == 0), stop=(k == ks - 1))
            last.then_inc(multiplied, 1)

        @block.vector
        def _(dve):
            st = Steps(dve, step)
            dve.wait_ge(loaded, 32)
            dve.wait_ge(multiplied, 1)
            st.then(dve.tensor_tensor(scores, across(b, NT), view, ALU.add))
            if softmax:
                st.then(dve.tensor_reduce(top, scores, AX.X, ALU.max))
                dve.tensor_tensor(scores, scores, over(top, e), ALU.subtract).then_inc(soft, 1)
                dve.wait_ge(soft_done, 1)
                st.then(dve.tensor_reduce(total, scores, AX.X, ALU.add))
                st.then(dve.reciprocal(total, total))
                st.then(dve.tensor_tensor(scores, scores, over(total, e), ALU.mult))
            if tmp is not None:
                best_two(dve, st, c, scores, gates, tmp, asked, answered)

        @block.scalar
        def _(act):
            if softmax:
                act.wait_ge(soft, 1)
                act.activation(scores, scores, ACT.Exp).then_inc(soft_done, 1)
            if tmp is not None:
                act.wait_ge(asked, 1)
                act.activation(tmp[6], tmp[6], ACT.Exp).then_inc(answered, 1)


def choose_half(nc, name, c, a, scores, gate, row_dram, chosen):
    row = a.take(N, rows=P)
    spare = a.take(N, rows=P)
    part = a.take(4, NT, rows=P)
    rank = a.take(NT, rows=P)
    with Phase(nc, name) as ph:
        moved = ph.sem("row_moved")
        step = ph.sem("dve_step")
        block = ph.block()

        @block.sync
        def _(sp):
            with nc.allow_non_contiguous_dma(reason="one word of each partition"):
                sp.dma_start(row_dram.rearrange("(t p) -> p t", p=P), scores).then_inc(moved, 16)
            sp.wait_ge(moved, 16)
            sp.dma_start(row, row_dram.unsqueeze(0).to_broadcast([P, N])).then_inc(moved, 16)
            sp.wait_ge(moved, 32)

        @block.vector
        def _(dve):
            st = Steps(dve, step)
            st.then(dve.memset(part, 0.0))
            dve.wait_ge(moved, 32)
            for t in range(NT):
                own, lo, hi = scores[:, t:t + 1], t * P, (t + 1) * P
                if t > 0:
                    st.then(dve.tensor_scalar(spare[:, 0:lo], row[:, 0:lo], own, None, ALU.is_ge, ALU.add,
                                              accum_out=part[:, 0, t:t + 1]))
                st.then(dve.tensor_scalar(spare[:, lo:N], row[:, lo:N], own, None, ALU.is_gt, ALU.add,
                                          accum_out=part[:, 1, t:t + 1]))
                st.then(dve.scalar_tensor_tensor(spare[:, lo:hi], row[:, lo:hi], own, c["after"][0:P, 0:P],
                                                 ALU.is_equal, ALU.mult, accum_out=part[:, 2, t:t + 1]))
            st.then(dve.tensor_tensor(rank, part[:, 0, :], part[:, 1, :], ALU.add))
            st.then(dve.tensor_tensor(rank, rank, part[:, 2, :], ALU.add))
            st.then(dve.scalar_tensor_tensor(gate, rank, float(chosen), scores, ALU.is_lt, ALU.mult))


ACCS = 4
HEADS = 4
GE = 4
ROW = HEADS * GE + HEADS
SRC_ROW = 24
DST_ROW = 8


def attention_scores(nc, name, c, arena, src_t, rec, places, w, scores_out, gates, src_table):
    a = Arena(arena, Y_AT, LATER_AT)
    node = a.take(NT, SRC_ROW, rows=P)
    bests = a.take(ACCS, NT, ROW, rows=P)
    best = bests[:, 0, :, :]
    target = a.take(NT, ROW, rows=P)
    all_sums = a.take(ACCS, NT, ROW, rows=P)
    sums = all_sums[:, 0, :, :]
    att = a.take(2, HEADS * GE, rows=P)
    w_sb = a.take(DK, HEADS * GE)
    prod = a.take(NT, HEADS * GE, rows=P)
    self_e = a.take(NT, HEADS, rows=P)
    zero_b = a.take(HEADS * GE, rows=P)
    z_at = a.at
    b = Arena(arena, TMP_AT, REC_AT)
    edge = b.take(T_GAT, ROW)
    edge_dst = b.take(T_GAT, DST_ROW)
    weight = b.take(T_GAT, HEADS)
    ring = b.take(RING, GROUP, SRC_ROW)
    idx = b.take(RING, GROUP, dtype=I32)
    hot = b.take(RING, GROUP, P)
    head = lambda v: v.rearrange("p t (h g) -> p t h g", h=HEADS)

    def node_terms():
        with Phase(nc, name + "_terms") as ph:
            loaded, multiplied, step, stored = (ph.sem(x) for x in ("loaded", "multiplied", "dve_step", "stored"))
            ready = ph.sem("node_ready")
            ps = ph.psum("h", [LANES, 512])
            view = ps[0:P, 0:NT * HEADS * GE].rearrange("p (t e) -> p t e", e=HEADS * GE)
            block = ph.block()

            @block.sync
            def _(sp):
                sp.dma_start(w_sb, w["W_gat"].rearrange("(k p) e -> p k e", p=LANES)).then_inc(loaded, 16)
                for i, n in enumerate(("att_src", "att_dst")):
                    sp.dma_start(att[:, i, :], w[n].rearrange("h g -> (h g)").unsqueeze(0)
                                 .to_broadcast([P, HEADS * GE])).then_inc(loaded, 16)
                sp.wait_ge(ready, 1)
                sp.dma_start(src_table.rearrange("(t p) d -> p t d", p=P), node).then_inc(stored, 16)
                sp.wait_ge(stored, 16)

            @block.tensor
            def _(pe):
                pe.wait_ge(loaded, 48)
                for t in range(NT):
                    for k in range(DK):
                        last = pe.matmul(view[:, t, :], src_t[:, k, t * P:(t + 1) * P], w_sb[:, k, :],
                                         start=(k == 0), stop=(k == DK - 1))
                last.then_inc(multiplied, 1)

            @block.vector
            def _(dve):
                st = Steps(dve, step)
                dve.wait_ge(loaded, 48)
                dve.wait_ge(multiplied, 1)
                st.then(dve.tensor_copy(node[:, :, 0:16], view))
                for i in range(2):
                    st.then(dve.tensor_tensor(prod, node[:, :, 0:16], across(att[:, i, :], NT), ALU.mult))
                    st.then(dve.tensor_reduce(node[:, :, 16 + HEADS * i:16 + HEADS * (i + 1)], head(prod),
                                              AX.X, ALU.add))
                for x in range(ACCS):
                    st.then(dve.tensor_copy(bests[:, x, :, 0:HEADS], node[:, :, 16:20]))
                dve.sem_inc(ready, 1)

    def maxima():
        z = Arena(arena, z_at, YT_AT)
        quad = GROUP // 2
        miss = z.take(2, GROUP, P)
        masked = z.take(2, quad, HEADS * P)
        new = z.take(2, quad, HEADS, rows=P)
        bodies = T_GAT // (RING * GROUP)
        units = 2 * RING
        by_act = 2
        with Phase(nc, name + "_max") as ph:
            turns = ph.sem("pool_turns")
            idx_ready = [ph.sem(f"idx_ready{h}") for h in range(RING)]
            gathered = c["pool_dma"]
            kept = ph.sem("groups_kept")
            step = ph.sem("dve_step")
            missed = ph.sem("miss_ready")
            act_masked = ph.sem("act_masked")
            dve_masked = ph.sem("dve_masked")
            turned = ph.sem("quads_turned")
            reduced = ph.sem("quads_reduced")
            ps = ph.psum("t", [LANES, 2, quad, 512])
            block = ph.block()

            @block.gpsimd
            def _(pool):
                with pool.Fori(0, bodies) as i:
                    for h in range(RING):
                        pool.wait_ge(idx_ready[h], i + 1)
                        pool.sem_inc(turns, 1)
                        for j in range(GROUP):
                            pool.indirect_dma_start(
                                ring[:, h, j, :], None, src_table,
                                bass.IndirectOffsetOnAxis(ap=idx[:, h, j:j + 1].bitcast(U32), axis=0))\
                                .then_inc(gathered.sems[h], 16)

            @block.scalar
            def _(act):
                def index(g, h):
                    act.copy(idx[:, h, :], rec[:, bass.ds(g * GROUP, GROUP), 0].bitcast(I32))\
                       .then_inc(idx_ready[h], 1)

                act.sem_inc(act_masked, units)
                for h in range(RING):
                    index(h, h)

                def group(i, h, more):
                    g = i * RING + h
                    gathered.wait(act, h, i * GROUP + GROUP)
                    act.copy(edge[:, bass.ds(g * GROUP, GROUP), :], ring[:, h, :, 0:ROW]).then_inc(kept, 1)
                    act.wait_ge(missed, g + 1)
                    for q in range(2):
                        u = 2 * h + q
                        act.wait_ge(turned, i * units + (units + u - 1))
                        for x in range(by_act):
                            for j in range(quad):
                                last = act.activation(masked[:, q, j, x * P:(x + 1) * P],
                                                      miss[:, h % 2, quad * q + j, :], ACT.Identity, scale=-BIG,
                                                      bias=ring[:, h, quad * q + j, 16 + x:17 + x])
                        last.then_inc(act_masked, 1)
                    act.wait_ge(kept, g + 1)
                    if more:
                        act.wait_ge(dve_masked, i * units + (2 * h + 2))
                        act.wait_ge(act_masked, i * units + (units + 2 * h + 2))
                        index(g + RING, h)

                with act.Fori(0, bodies - 1) as i:
                    for h in range(RING):
                        group(i, h, True)
                for h in range(RING):
                    group(bodies - 1, h, False)

            @block.vector
            def _(dve):
                st = Steps(dve, step)

                def mark(i, h):
                    if h >= 2:
                        dve.wait_ge(act_masked, i * units + (units + 2 * h - 2))
                    of = rec[:, bass.ds((i * RING + h) * GROUP, GROUP), 1]
                    dve.tensor_tensor(miss[:, h % 2, :, :], over(of, P), across(c["lane"][:, 0:P], GROUP),
                                      ALU.not_equal).then_inc(missed, 1)

                def mask(i, h, q):
                    u = 2 * h + q
                    dve.wait_ge(missed, i * RING + (h + 1))
                    gathered.wait(dve, h, i * GROUP + GROUP)
                    dve.wait_ge(turned, i * units + (units + u - 1))
                    of = slice(quad * q, quad * (q + 1))
                    for x in range(by_act, HEADS):
                        last = dve.scalar_tensor_tensor(
                            masked[:, q, :, x * P:(x + 1) * P], miss[:, h % 2, of, :], -BIG,
                            over(ring[:, h, of, 16 + x], P), ALU.mult, ALU.add)
                    last.then_inc(dve_masked, 1)

                def reduce(i, h, q):
                    u = 2 * h + q
                    _, place = nc.values_load_multi_w_load_instructions(
                        places[0:1, bass.ds((i * RING + h) * GROUP + quad * q, quad)],
                        engines=(mybir.EngineType.DVE,), min_val=0, max_val=(NT - 1) * ROW)
                    dve.wait_ge(turned, i * units + (units + u + 1))
                    st.then(dve.tensor_reduce(new[:, q, :, :], ps[0:P, q, :, :].rearrange("p g (x e) -> p g x e", x=HEADS),
                                              AX.X, ALU.max))
                    dve.sem_inc(reduced, 1)
                    for j in range(quad):
                        to = flat(bests[:, j % ACCS, :, :])[:, bass.ds(place[j], HEADS)]
                        st.lag(dve.tensor_tensor(to, to, new[:, q, j, :], ALU.max), ACCS - 1)

                dve.sem_inc(reduced, 2)
                st.ahead(ACCS)
                with dve.Fori(0, bodies) as i:
                    st.enter(i, units * (1 + quad))
                    dve.wait_ge(act_masked, i * units + units)
                    mark(i, 0)
                    mask(i, 0, 0)
                    for u in range(units):
                        if u % 2 == 0 and u + 2 < units:
                            mark(i, u // 2 + 1)
                        if u + 1 < units:
                            mask(i, (u + 1) // 2, (u + 1) % 2)
                        reduce(i, u // 2, u % 2)
                st.leave(bodies)

            @block.tensor
            def _(pe):
                pe.sem_inc(turned, units)
                with pe.Fori(0, bodies) as i:
                    for u in range(units):
                        pe.wait_ge(act_masked, i * units + (units + u + 1))
                        pe.wait_ge(dve_masked, i * units + (u + 1))
                        pe.wait_ge(reduced, i * units + (u + 1))
                        for j in range(quad):
                            for x in range(HEADS):
                                last = pe.transpose(ps[0:P, u % 2, j, x * LANES:(x + 1) * LANES],
                                                    masked[:, u % 2, j, x * P:(x + 1) * P], c["ident"])
                        last.then_inc(turned, 1)

            for h in range(RING):
                gathered.finished(h, GROUP * bodies)

    def target_terms():
        with Phase(nc, name + "_targets") as ph:
            step, asked, answered = (ph.sem(x) for x in ("dve_step", "exp_asked", "exp_done"))
            block = ph.block()

            @block.vector
            def _(dve):
                st = Steps(dve, step)
                tt = dve.tensor_tensor
                for x in range(1, ACCS):
                    st.then(tt(best[:, :, 0:HEADS], best[:, :, 0:HEADS], bests[:, x, :, 0:HEADS], ALU.max))
                    st.done(dve.memset(flat(all_sums[:, x, :, :]), 0.0))
                a_dst, a_src, m = node[:, :, 20:24], node[:, :, 16:20], target[:, :, HEADS:2 * HEADS]
                st.then(dve.tensor_copy(target[:, :, 0:HEADS], a_dst))
                st.then(tt(m, best[:, :, 0:HEADS], a_dst, ALU.add))
                st.then(dve.scalar_tensor_tensor(m, m, 0.2, m, ALU.mult, ALU.max))
                st.then(tt(self_e, a_src, a_dst, ALU.add))
                st.then(dve.scalar_tensor_tensor(self_e, self_e, 0.2, self_e, ALU.mult, ALU.max))
                st.then(tt(self_e, self_e, m, ALU.subtract))
                dve.sem_inc(asked, 1)
                dve.wait_ge(answered, 1)
                st.then(dve.tensor_copy(sums[:, :, 16:20], self_e))
                for h in range(HEADS):
                    st.then(tt(sums[:, :, GE * h:GE * (h + 1)], node[:, :, GE * h:GE * (h + 1)],
                               over(self_e[:, :, h], GE), ALU.mult))

            @block.scalar
            def _(act):
                act.wait_ge(asked, 1)
                act.activation(self_e, self_e, ACT.Exp).then_inc(answered, 1)

    def target_rows():
        z = Arena(arena, z_at, YT_AT)
        hot_t = z.take(2, GROUP, LANES, rows=P)
        bodies = T_GAT // (RING * GROUP)
        with Phase(nc, name + "_rows") as ph:
            hot_ready = ph.sem("hot_ready")
            turned = ph.sem("groups_turned")
            copied = ph.sem("groups_copied")
            multiplied = ph.sem("groups_multiplied")
            taken = ph.sem("groups_taken")
            ps_t = ph.psum("t", [LANES, 2, GROUP // 4, 4, LANES])
            ps = ph.psum("rows", [LANES, 2, 512])
            block = ph.block()

            @block.vector
            def _(dve):
                def one_hot(i, h):
                    dve.wait_ge(turned, i * RING + (h + 1))
                    dve.tensor_tensor(hot[:, h, :, :], over(rec[:, bass.ds((i * RING + h) * GROUP, GROUP), 1], P),
                                      across(c["lane"][:, 0:P], GROUP), ALU.is_equal).then_inc(hot_ready, 1)

                def take(i, h):
                    g = i * RING + h
                    dve.wait_ge(multiplied, g + 1)
                    dve.tensor_copy(edge_dst[:, bass.ds(g * GROUP, GROUP), :],
                                    ps[:, h % 2, 0:GROUP * DST_ROW].rearrange("p (g w) -> p g w", g=GROUP))\
                       .then_inc(taken, 1)

                dve.sem_inc(taken, 2)
                for h in range(RING):
                    one_hot(0, h)
                with dve.Fori(0, bodies - 1) as i:
                    for h in range(RING):
                        take(i, h)
                        one_hot(i + 1, h)
                for h in range(RING):
                    take(bodies - 1, h)

            @block.scalar
            def _(act):
                with act.Fori(0, bodies) as i:
                    for h in range(RING):
                        g = i * RING + h
                        act.wait_ge(turned, g + (RING + 1))
                        for x in range(GROUP // 4):
                            last = act.copy(hot_t[:, h % 2, 4 * x:4 * x + 4, :], ps_t[0:P, h % 2, x, :, :])
                        last.then_inc(copied, 1)

            @block.tensor
            def _(pe):
                pe.sem_inc(turned, RING)

                def turn(g, h):
                    pe.wait_ge(hot_ready, g + 1)
                    for j in range(GROUP):
                        last = pe.transpose(ps_t[0:P, h % 2, j // 4, j % 4, :], hot[:, h, j, :], c["ident"])
                    last.then_inc(turned, 1)

                def multiply(g, h):
                    _, place = nc.values_load_multi_w_load_instructions(
                        places[0:1, bass.ds(g * GROUP, GROUP)], engines=(mybir.EngineType.PE,),
                        min_val=0, max_val=(NT - 1) * ROW)
                    pe.wait_ge(copied, g + 1)
                    pe.wait_ge(taken, g + 1)
                    for j in range(GROUP):
                        last = pe.matmul(ps[:, h % 2, j * DST_ROW:(j + 1) * DST_ROW], hot_t[:, h % 2, j, :],
                                         flat(target)[:, bass.ds(place[j], DST_ROW)], start=True, stop=True)
                    last.then_inc(multiplied, 1)

                turn(0, 0)
                with pe.Fori(0, bodies - 1) as i:
                    for h in range(RING):
                        turn(i * RING + (h + 1), (h + 1) % RING)
                        multiply(i * RING + h, h)
                last = (bodies - 1) * RING
                for h in range(RING):
                    if h + 1 < RING:
                        turn(last + h + 1, h + 1)
                    multiply(last + h, h)

    def edge_weights():
        with Phase(nc, name + "_edges") as ph:
            step, asked, answered = (ph.sem(x) for x in ("dve_step", "exp_asked", "exp_done"))
            block = ph.block()

            @block.vector
            def _(dve):
                st = Steps(dve, step)
                tt = dve.tensor_tensor
                st.then(tt(weight, edge[:, :, 16:20], edge_dst[:, :, 0:HEADS], ALU.add))
                st.then(dve.scalar_tensor_tensor(weight, weight, 0.2, weight, ALU.mult, ALU.max))
                st.then(tt(weight, weight, edge_dst[:, :, HEADS:2 * HEADS], ALU.subtract))
                st.then(dve.tensor_scalar_min(weight, weight, 0.0))
                dve.sem_inc(asked, 1)
                dve.wait_ge(answered, 1)
                for h in range(HEADS):
                    st.then(tt(edge[:, :, GE * h:GE * (h + 1)], edge[:, :, GE * h:GE * (h + 1)],
                               over(weight[:, :, h], GE), ALU.mult))
                st.then(dve.tensor_copy(edge[:, :, 16:20], weight))

            @block.scalar
            def _(act):
                act.wait_ge(asked, 1)
                act.activation(weight, weight, ACT.Exp).then_inc(answered, 1)

    def edge_sums():
        with Phase(nc, name + "_sum") as ph:
            step = ph.sem("dve_step")
            hot_ready = ph.sem("hot_ready")
            summed = ph.sem("groups_summed")
            ps = ph.psum("sum", [LANES, RING, 512])
            bodies = T_GAT // (RING * GROUP)
            block = ph.block()

            @block.vector
            def _(dve):
                st = Steps(dve, step)
                st.ahead(ACCS)

                def one_hot(i, h):
                    dve.wait_ge(summed, i * RING + (h + 1))
                    of = rec[:, bass.ds((i * RING + h) * GROUP, GROUP), :]
                    dve.tensor_tensor(hot[:, h, :, :], over(of[:, :, 1], P), across(c["lane"][:, 0:P], GROUP),
                                      ALU.is_equal).then_inc(hot_ready, 1)

                def add_group(i, h):
                    _, place = nc.values_load_multi_w_load_instructions(
                        places[0:1, bass.ds((i * RING + h) * GROUP, GROUP)],
                        engines=(mybir.EngineType.DVE,), min_val=0, max_val=(NT - 1) * ROW)
                    dve.wait_ge(summed, i * RING + (RING + h + 1))
                    for j in range(GROUP):
                        to = flat(all_sums[:, j % ACCS, :, :])[:, bass.ds(place[j], ROW)]
                        st.lag(dve.tensor_tensor(to, to, ps[0:P, h, j * ROW:(j + 1) * ROW], ALU.add), ACCS - 1)
                    st.all()

                for h in range(RING):
                    one_hot(0, h)
                with dve.Fori(0, bodies - 1) as i:
                    st.enter(i, RING * GROUP)
                    for h in range(RING):
                        add_group(i, h)
                        one_hot(i + 1, h)
                st.leave(bodies - 1)
                for h in range(RING):
                    add_group(bodies - 1, h)

            @block.tensor
            def _(pe):
                pe.sem_inc(summed, RING)
                with pe.Fori(0, bodies) as i:
                    for h in range(RING):
                        pe.wait_ge(hot_ready, i * RING + (h + 1))
                        for j in range(GROUP):
                            last = pe.matmul(ps[0:P, h, j * ROW:(j + 1) * ROW], hot[:, h, j, :],
                                             edge[:, bass.ds((i * RING + h) * GROUP + j, 1), :]
                                             .rearrange("p a b -> p (a b)"), start=True, stop=True)
                        last.then_inc(summed, 1)

    def finish():
        k = HEADS * GE
        f = Arena(arena, TMP_AT, REC_AT)
        agg = f.take(NT, k, rows=P)
        sq = f.take(NT, k, rows=P)
        mean = f.take(NT, rows=P)
        root = f.take(NT, rows=P)
        par = f.take(3, k, rows=P)
        tmp = best_two_places(f, GE)
        with Phase(nc, name + "_norm") as ph:
            loaded, step, asked, rooted, e_asked, e_done = (
                ph.sem(x) for x in ("loaded", "dve_step", "root_asked", "root_ready", "exp_asked", "exp_done"))
            block = ph.block()

            @block.sync
            def _(sp):
                for i, n in enumerate(("b_gat", "ln_gamma", "ln_beta")):
                    sp.dma_start(par[:, i, :], w[n].unsqueeze(0).to_broadcast([P, k])).then_inc(loaded, 16)

            @block.vector
            def _(dve):
                st = Steps(dve, step)
                tt = dve.tensor_tensor
                for x in range(1, ACCS):
                    st.then(tt(sums, sums, all_sums[:, x, :, :], ALU.add))
                st.then(dve.tensor_scalar_add(self_e, sums[:, :, 16:20], 1e-16))
                st.then(dve.reciprocal(self_e, self_e))
                for h in range(HEADS):
                    st.then(tt(agg[:, :, GE * h:GE * (h + 1)], sums[:, :, GE * h:GE * (h + 1)],
                               over(self_e[:, :, h], GE), ALU.mult))
                dve.wait_ge(loaded, 48)
                st.then(tt(agg, agg, across(par[:, 0, :], NT), ALU.add))
                st.then(dve.tensor_reduce(mean, agg, AX.X, ALU.add))
                st.then(dve.tensor_scalar_mul(mean, mean, 1.0 / k))
                st.then(tt(agg, agg, over(mean, k), ALU.subtract))
                st.then(tt(sq, agg, agg, ALU.mult))
                st.then(dve.tensor_reduce(root, sq, AX.X, ALU.add))
                st.then(dve.tensor_scalar(root, root, 1.0 / k, EPS, ALU.mult, ALU.add))
                dve.sem_inc(asked, 1)
                dve.wait_ge(rooted, 1)
                st.then(dve.reciprocal(root, root))
                st.then(tt(agg, agg, over(root, k), ALU.mult))
                st.then(tt(agg, agg, across(par[:, 1, :], NT), ALU.mult))
                st.then(tt(agg, agg, across(par[:, 2, :], NT), ALU.add))
                st.then(dve.tensor_reduce(scores_out, agg.rearrange("p t (h g) -> p t g h", h=HEADS), AX.X, ALU.add))
                st.then(dve.tensor_scalar_mul(flat(scores_out), flat(scores_out), 1.0 / HEADS))
                best_two(dve, st, c, scores_out, gates, tmp, e_asked, e_done)

            @block.scalar
            def _(act):
                act.wait_ge(asked, 1)
                act.activation(root, root, ACT.Sqrt).then_inc(rooted, 1)
                act.wait_ge(e_asked, 1)
                act.activation(tmp[6], tmp[6], ACT.Exp).then_inc(e_done, 1)

    node_terms()
    maxima()
    target_terms()
    target_rows()
    edge_weights()
    edge_sums()
    finish()


def last_norm(nc, name, a, x, y, gamma, beta, out):
    stats = a.take(NT, 6, rows=P)
    mean, root, spare = (a.take(NT, rows=P) for _ in range(3))
    g = a.take(D, rows=P)
    b = a.take(D, rows=P)
    with Phase(nc, name) as ph:
        loaded, step, asked, rooted, ready, stored = (
            ph.sem(s) for s in ("loaded", "dve_step", "root_asked", "root_ready", "quad_ready", "stored"))
        block = ph.block()

        @block.sync
        def _(sp):
            sp.dma_start(g, gamma.unsqueeze(0).to_broadcast([P, D])).then_inc(loaded, 16)
            sp.dma_start(b, beta.unsqueeze(0).to_broadcast([P, D])).then_inc(loaded, 16)
            rows = out.rearrange("(t p) d -> p t d", p=P)
            for q, (t, n) in enumerate(quads()):
                sp.wait_ge(ready, q + 1)
                sp.dma_start(rows[:, t:t + n, :], x[:, t:t + n, :]).then_inc(stored, 16)
            sp.wait_ge(stored, 16 * len(quads()))

        @block.vector
        def _(dve):
            st = Steps(dve, step)
            row_statistics(dve, st, y, stats, mean, root, spare).then_inc(asked, 1)
            dve.wait_ge(rooted, 1)
            st.then(dve.reciprocal(root, root))
            dve.wait_ge(loaded, 32)
            for t, n in quads():
                part, xs = y[:, t:t + n, :], x[:, t:t + n, :]
                st.then(dve.tensor_tensor(part, part, over(mean[:, t:t + n], D), ALU.subtract))
                st.then(dve.tensor_tensor(part, part, over(root[:, t:t + n], D), ALU.mult))
                st.then(dve.tensor_tensor(part, part, across(g, n), ALU.mult))
                st.then(dve.tensor_tensor(part, part, across(b, n), ALU.add))
                dve.tensor_tensor(xs, xs, part, ALU.add).then_inc(ready, 1)

        @block.scalar
        def _(act):
            act.wait_ge(asked, 1)
            act.activation(root, root, ACT.Sqrt).then_inc(rooted, 1)


def residual_layers(nc, w, out):
    Phase.cleared = []
    dram = lambda name, shape, dt=F32: nc.dram_tensor(name, shape, dt, kind="Internal").ap()
    by_dst = dram("edges_by_dst", (T_MAIN * LANES, 4))
    by_src = dram("edges_by_src", (T_MAIN * LANES, 4))
    by_gat = dram("gat_edges_by_dst", (T_GAT * LANES, 4))
    rows = [dram(f"rows{i}", (N, D)) for i in range(5)]
    src_table = dram("gat_src_rows", (N, SRC_ROW))
    pair_rows = dram("rows_by_expert", (PAIR_ROWS, D))
    pair_results = dram("results_by_expert", (PAIR_ROWS, D))
    score_row = dram("score_row", (N,))

    with ExitStack() as ctx:
        arena = ctx.enter_context(nc.sbuf_tensor("arena", [LANES, ARENA], F32))[:, :]
        sb = lambda name, shape, dt=F32: ctx.enter_context(nc.sbuf_tensor(name, shape, dt))[:, :]
        c = constants(nc, ctx, arena)
        clear_table(nc, ctx, c, arena, pair_rows)
        at_dst = sb("places_by_dst", [1, T_MAIN], I32)
        at_src = sb("places_by_src", [1, T_MAIN], I32)
        at_gat = sb("places_gat", [1, T_GAT], I32)
        degree = sb("degree", [P, NT])

        n_main, n_gat = E_MAIN // P, E_GAT // LANES
        a = Arena(arena, ACC_AT)
        scatter_dst = Scatter(c, a, P, n_main, by_dst)
        scatter_gat = Scatter(c, a, LANES, n_gat, by_gat)
        scatter_src = Scatter(c, Arena(arena, LATER_AT, WEIGHTS_AT), P, n_main, by_src)
        gat_spill = dram("gat_records", (LANES, 4 * n_gat)), dram("gat_slots", (LANES, n_gat), I32)
        bucket_sort(nc, "sort_dst", c, arena, w["dst"], w["src"], None, P, T_MAIN, D, scatter_dst, at_dst)
        bucket_sort(nc, "sort_src", c, arena, w["src"], w["dst"], w["edge_weight"], P, T_MAIN, D, scatter_src, at_src,
                    beside=(scatter_dst, 4))
        e = w["L2_ffn_edge_index"]
        bucket_sort(nc, "sort_gat", c, arena, e[1, :], e[0, :], None, LANES, T_GAT, ROW, scatter_gat, at_gat,
                    spill=gat_spill, beside=(scatter_dst, 4))

        def node(at, rows=P):
            return arena[0:rows, at:at + NT * D].rearrange("p (t d) -> p t d", d=D)

        x, y, acc = node(X_AT), node(Y_AT), node(ACC_AT)
        yt = arena[:, YT_AT:YT_AT + DK * N].rearrange("p (k n) -> p k n", k=DK)
        rec = Arena(arena, REC_AT)
        rec_dst, rec_src, rec_gat = rec.take(T_MAIN, 4), rec.take(T_MAIN, 4), rec.take(T_GAT, 4)
        tmp = lambda: Arena(arena, TMP_AT, REC_AT)

        x_view = w["x"].rearrange("(t p) d -> p t d", p=P)
        eps1 = sb("one_plus_eps", [P, 1])
        layer_norm(nc, "L0g_norm", c, arena, x, y, yt, rows[0],
                   loads=[(x, x_view), (eps1, w["L0_gnn_eps"].unsqueeze(0).to_broadcast([P, 1]))],
                   beside=(scatter_dst, 3))
        degrees(nc, "degrees", c, Arena(arena, TMP_AT, EARLY_AT), scatter_dst, degree, (scatter_dst, None))
        load_records(nc, "load_dst", [(rec_dst, by_dst)])
        graph_sum(nc, "L0g_sum", c, arena, rows[0], rec_dst, at_dst, flat(acc), T_MAIN, False)

        def mix(dve, st, quad_ready, asked, rooted):
            st.then(dve.tensor_scalar_add(eps1, eps1, 1.0))
            for t, n in quads():
                dve.scalar_tensor_tensor(y[:, t:t + n, :], y[:, t:t + n, :], eps1, acc[:, t:t + n, :],
                                         ALU.mult, ALU.add).then_inc(quad_ready, 1)

        to_features(nc, "L0g_mix", c, arena, y, yt, mix)
        wide = lambda at, m: arena[:, at:at + m * N].rearrange("p (m n) -> p m n", m=m)
        weight = lambda at, k, f: arena[:, at:at + k * f].rearrange("p (k f) -> p k f", k=k)
        small = sb("column_bias", [LANES, 8])
        stats = sb("batch_stats", [LANES, 8 * 6 * len(CHUNKS)]).rearrange("p (m s) -> p m s", m=8)
        h1, h2, h3 = wide(Y_AT, 4), wide(X_AT, 8), wide(Y_AT, 4)
        w1, w2, w3, w4 = (weight(WEIGHTS_AT, k, f) for k, f in ((2, 512), (4, 1024), (8, 512), (4, 256)))
        turns = {1: (2, 1), 2: (8, 3), 3: (8, 1)}
        for i, (src, h, ws) in enumerate(((yt, h1, w1), (h1, h2, w2), (h2, h3, w3)), 1):
            m = h.shape[1]
            dense(nc, f"L0g_mlp{i}", [(src, ws, w[f"L0_gnn_W{i}"])], (small[:, 0:m], w[f"L0_gnn_b{i}"]), h,
                  ACT.Identity, stats[:, 0:m, :], beside=(scatter_src, turns[i][0]))
            batch_norm_elu(nc, f"L0g_bn{i}", Arena(arena, X_AT if i != 2 else Y_AT), h, stats[:, 0:m, :],
                           w[f"L0_gnn_g{i}"], w[f"L0_gnn_beta{i}"], beside=(scatter_src, turns[i][1]))
        row_bias = sb("row_bias", [P, D])
        project(nc, "L0g_out", h3, w4, w["L0_gnn_W4"], x, (row_bias, w["L0_gnn_b4"]), add=True, loads=[(x, x_view)],
                beside=(scatter_src, None))
        load_records(nc, "load_more", [(rec_dst, by_dst), (rec_src, by_src)])
        scatter_gat.place(Arena(arena, LATER_AT, WEIGHTS_AT))
        with Phase(nc, "load_gat_records") as ph:
            back = ph.sem("loaded")
            block = ph.block()

            @block.sync
            def _(sp):
                for of, to in zip(gat_spill, (flat(scatter_gat.rec), scatter_gat.slot)):
                    sp.dma_start(to, of).then_inc(back, 16)
                sp.wait_ge(back, 32)

        layer_norm(nc, "L0f_norm", c, arena, x, y, yt)
        a = tmp()
        rh = a.take(1, N)
        wr = a.take(2, LANES)
        dense(nc, "L0f_hidden", [(yt, wr, w["L0_ffn_router_w1"])], (small[:, 0:1], w["L0_ffn_router_b1"]), rh, ACT.Relu)
        spare = Arena(arena, WEIGHTS_AT, YT_AT)
        scores, gates = spare.take(NT, 6, rows=P), spare.take(NT, 6, rows=P)
        router(nc, "L0f_router", c, spare, rh, w["L0_ffn_router_w2"], w["L0_ffn_router_b2"], scores, gates, softmax=True)
        experts(nc, "L0f", c, tmp(), yt, x, [(w["L0_ffn_expert_w1"], w["L0_ffn_expert_b1"]),
                                          (w["L0_ffn_expert_w2"], w["L0_ffn_expert_b2"])],
                w["L0_ffn_expert_w3"], gates, gates, w["L0_ffn_expert_b3"], 6, ACT.Relu,
                beside=(scatter_gat, None))
        load_records(nc, "load_gat", [(rec_gat, by_gat)])

        layer_norm(nc, "L1g_norm", c, arena, x, y, yt)
        wk = tmp().take(2, D)
        project(nc, "L1g_rows", yt, wk, w["L1_gnn_kernel"], acc, table=rows[1])
        graph_sum(nc, "L1g_sum", c, arena, rows[1], rec_src, at_src, flat(acc), T_MAIN, True)
        add_scaled(nc, "L1g_add", x, acc, bias=(row_bias, w["L1_gnn_bias"]))

        layer_norm(nc, "L1f_norm", c, arena, x, y, yt)
        a = tmp()
        scores, gate2, gate1 = a.take(NT, 1, rows=P), a.take(NT, 2, rows=P), a.take(NT, 1, rows=P)
        at = a.at
        router(nc, "L1f_router", c, a, yt, w["L1_ffn_wr"], w["L1_ffn_br"], scores)
        a.at = at
        choose_half(nc, "L1f_choose", c, a, flat(scores), flat(gate1), score_row, max(1, int(0.5 * N)) - 1)
        add_gates(nc, "L1f_gates", x, y, gate1, gate2)
        a.at = at
        hidden_w, hidden_b, out_w = w["L1_ffn_w1"], w["L1_ffn_b1"], w["L1_ffn_w2"]
        experts(nc, "L1f", c, a, yt, x, [(hidden_w, hidden_b)], out_w, gate2, gate1, w["L1_ffn_b2"].unsqueeze(0), 2,
                ACT.Gelu_apprx_tanh)

        layer_norm(nc, "L2g_norm", c, arena, x, y, yt, rows[2])
        graph_sum(nc, "L2g_sum1", c, arena, rows[2], rec_dst, at_dst, flat(acc), T_MAIN, False)
        inv = sb("inverse_degree", [P, NT])
        inverse(nc, "L2g_inverse", degree, inv, lambda dve: dve.tensor_scalar_max(inv, degree, 1.0))
        agg_t = arena[:, Y_AT:Y_AT + DK * N].rearrange("p (k n) -> p k n", k=DK)

        def mean(dve, st, quad_ready, asked, rooted):
            for t, n in quads():
                dve.tensor_tensor(acc[:, t:t + n, :], acc[:, t:t + n, :], over(inv[:, t:t + n], D),
                                  ALU.mult).then_inc(quad_ready, 1)

        to_features(nc, "L2g_mean", c, arena, acc, agg_t, mean)
        a = tmp()
        ht = a.take(4, N)
        a = Arena(arena, LATER_AT, YT_AT)
        w1l, w1r, w2l, w2r = a.take(2, 512), a.take(2, 512), a.take(4, D), a.take(4, D)
        dense(nc, "L2g_hidden", [(agg_t, w1l, w["L2_gnn_W1l"]), (yt, w1r, w["L2_gnn_W1r"])],
              (small[:, 0:4], w["L2_gnn_b1"]), ht, ACT.Relu)
        project(nc, "L2g_rows", ht, w2l, w["L2_gnn_W2l"], acc, table=rows[3])
        project(nc, "L2g_own", ht, w2r, w["L2_gnn_W2r"], x, (row_bias, w["L2_gnn_b2"]), add=True)
        graph_sum(nc, "L2g_sum2", c, arena, rows[3], rec_dst, at_dst, flat(acc), T_MAIN, False)
        add_scaled(nc, "L2g_add", x, acc, scale=inv)

        layer_norm(nc, "L2f_norm", c, arena, x, y, yt)
        scores4 = sb("gat_scores", [P, NT * GE]).rearrange("p (t e) -> p t e", e=GE)
        gates4 = sb("gat_gates", [P, NT * GE]).rearrange("p (t e) -> p t e", e=GE)
        attention_scores(nc, "L2f_gat", c, arena, yt, rec_gat, at_gat,
                         {n: w["L2_ffn_" + n] for n in ("W_gat", "att_src", "att_dst", "b_gat", "ln_gamma", "ln_beta")},
                         scores4, gates4, src_table)
        experts(nc, "L2f", c, tmp(), yt, x, [(w["L2_ffn_W1"], w["L2_ffn_b1"])], w["L2_ffn_W2"], gates4, gates4,
                w["L2_ffn_b2"], 4, ACT.Gelu)

        layer_norm(nc, "L3g_norm", c, arena, x, y, yt)
        wk = tmp().take(2, D)
        project(nc, "L3g_rows", yt, wk, w["L3_gnn_W"], acc, (row_bias, w["L3_gnn_b"]), table=rows[4])
        graph_sum(nc, "L3g_sum", c, arena, rows[4], rec_dst, at_dst, flat(acc), T_MAIN, False)
        inverse(nc, "L3g_inverse", degree, inv, lambda dve: dve.tensor_scalar_add(inv, degree, 1.0))
        add_scaled(nc, "L3g_add", x, acc, scale=inv)

        layer_norm(nc, "L3f_norm", c, arena, x, y, yt)
        a = tmp()
        picks = best_two_places(a, 16)
        _, one, two, _, _, _, w_two, w_one = picks
        at = a.at
        scores = a.take(NT, 16, rows=P)
        router(nc, "L3f_router", c, a, yt, w["L3_ffn_gate_w"], w["L3_ffn_gate_b"], scores, picks=picks)
        spare = Arena(arena, LATER_AT, YT_AT)
        slots = spare.take(2, NT, rows=P, dtype=I32)
        expert_of = spare.take(pair_tiles(16), rows=1, dtype=I32)
        send_to_experts(nc, "L3f_send", c, spare, y, one, two, slots, expert_of, pair_rows)
        a.at = at
        run_experts(nc, "L3f", c, a, pair_rows, expert_of, w["L3_ffn_w1"], w["L3_ffn_b1"], w["L3_ffn_w2"],
                    w["L3_ffn_b2"], pair_results, ACT.Relu)
        combine(nc, "L3f_combine", c, Arena(arena, WEIGHTS_AT, YT_AT), pair_results, slots, w_one, w_two, y)
        last_norm(nc, "L3f_last", tmp(), x, y, w["L3_ffn_gamma"], w["L3_ffn_beta"], out)


def add_gates(nc, name, x, y, gate, gates):
    with Phase(nc, name) as ph:
        block = ph.block()

        @block.vector
        def _(dve):
            dve.tensor_tensor(x, x, y, ALU.add)
            dve.tensor_copy(gates[:, :, 0:1], gate)
            dve.tensor_copy(gates[:, :, 1:2], gate)


def inverse(nc, name, degree, inv, first):
    with Phase(nc, name) as ph:
        step = ph.sem("dve_step")
        block = ph.block()

        @block.vector
        def _(dve):
            st = Steps(dve, step)
            st.then(first(dve))
            dve.reciprocal(inv, inv)


def kernel(**inputs):
    import concourse.bacc as bacc
    from concourse.bass_utils import run_bass_kernel_spmd

    arrays = {k: np.asarray(v) for k, v in inputs.items()}
    arrays["L0_gnn_eps"] = arrays["L0_gnn_eps"].reshape(1)
    for name in ("L2_gnn_W1l", "L2_gnn_W1r", "L2_gnn_W2l", "L2_gnn_W2r", "L3_gnn_W"):
        arrays[name] = arrays[name].T
    w1, b1, w2 = arrays["L1_ffn_w1"], arrays["L1_ffn_b1"], arrays["L1_ffn_w2"]
    arrays["L1_ffn_w1"] = w1.reshape(D, 2, -1).transpose(1, 0, 2)
    arrays["L1_ffn_b1"] = b1.reshape(2, -1)
    arrays["L1_ffn_w2"] = w2.reshape(2, -1, D)
    del arrays["L1_ffn_attention_mask"]
    arrays = {k: np.ascontiguousarray(v) for k, v in arrays.items()}

    nc = bacc.Bacc("TRN2", target_bir_lowering=False, num_devices=1)
    aps = {k: nc.dram_tensor("in_" + k, v.shape, mybir.dt.from_np(v.dtype), kind="ExternalInput").ap()
           for k, v in arrays.items()}
    out = nc.dram_tensor("out", (N, D), F32, kind="ExternalOutput").ap()
    residual_layers(nc, aps, out)
    r = run_bass_kernel_spmd(nc, [{"in_" + k: v for k, v in arrays.items()}], core_ids=[0])
    return r.results[0]["out"]
```

```python
from contextlib import ExitStack

import numpy as np
import concourse.bass as bass
import concourse.mybir as mybir

F32 = mybir.dt.float32
I32 = mybir.dt.int32
U32 = mybir.dt.uint32
ALU = mybir.AluOpType
ACT = mybir.ActivationFunctionType
AX = mybir.AxisListType

N = 3125
P = 125
NT = N // P
D = 256
DK = D // 128
LANES = 128
GROUP = 8
STEP = 2 * GROUP
RING = 4
QUADS = 2 * RING
E_MAIN = 50000
E_GAT = 32768
CHUNK = 4 * P
FULL = N // CHUNK
CHUNKS = [(c * CHUNK, min(CHUNK, N - c * CHUNK)) for c in range(FULL + 1)]
ZEROS = 1280
ROUND = 12582912.0
EPS = 1e-5
BIG = 1e30


def edge_tiles(edges):
    most = (edges + NT * (LANES - 1)) // LANES
    return -(-most // (RING * GROUP)) * (RING * GROUP)


T_MAIN = edge_tiles(E_MAIN)
T_GAT = edge_tiles(E_GAT)

Y_AT = 0
ACC_AT = Y_AT + NT * D
LATER_AT = ACC_AT + NT * D
WEIGHTS_AT = LATER_AT + 2304
YT_AT = WEIGHTS_AT + 4096
X_AT = YT_AT + DK * N
TMP_AT = X_AT + NT * D
ARENA = X_AT + 8 * N
REC_MAIN = 4 * T_MAIN
REC_GAT = 4 * T_GAT
REC_AT = ARENA - 2 * REC_MAIN - REC_GAT
EARLY_AT = REC_AT - (LANES + T_MAIN)


class Steps:

    def __init__(self, eng, sem):
        self.eng, self.sem, self.n, self.turn = eng, sem, 0, 0

    def done(self, ins):
        ins.then_inc(self.sem, 1)
        self.n += 1

    def then(self, ins):
        self.done(ins)
        self.eng.wait_ge(self.sem, self.turn + self.n)

    def ahead(self, n):
        self.eng.sem_inc(self.sem, n)
        self.n += n

    def lag(self, ins, behind):
        self.done(ins)
        self.eng.wait_ge(self.sem, self.turn + self.n - behind)

    def all(self):
        self.eng.wait_ge(self.sem, self.turn + self.n)

    def enter(self, i, each):
        self.first, self.each, self.turn = self.n, each, i * each

    def leave(self, turns):
        assert self.n == self.first + self.each, (self.n - self.first, self.each)
        self.n, self.turn = self.first + self.each * turns, 0


class PoolDma:

    def __init__(self, nc, ctx):
        self.sems = [ctx.enter_context(nc.semaphore(f"pool_dma{h}")) for h in range(RING)]
        self.base = [0] * RING

    def wait(self, eng, h, dmas):
        eng.wait_ge(self.sems[h], dmas * 16 + self.base[h])

    def finished(self, h, dmas):
        self.base[h] += 16 * dmas


class Phase:

    cleared = []

    def __init__(self, nc, name):
        self.nc, self.name, self.ctx = nc, name, ExitStack()

        self.sems = []

    def __enter__(self):
        self.ctx.__enter__()
        return self

    def __exit__(self, *e):
        self.ctx.__exit__(*e)
        if e[0] is None:
            for s in Phase.cleared:
                self.nc.release_semaphore(s)
            for s in self.sems:
                self.nc.gpsimd.sem_clear(s)
            Phase.cleared = self.sems

    def sem(self, name):
        self.sems.append(self.nc.alloc_semaphore(f"{self.name}_{name}"))
        return self.sems[-1]

    def psum(self, name, shape, dtype=F32):
        return self.ctx.enter_context(self.nc.psum_tensor(f"{self.name}_{name}", shape, dtype))

    def block(self):
        return self.ctx.enter_context(self.nc.Block())


class Arena:

    def __init__(self, tensor, at, end=ARENA):
        self.t, self.at, self.end = tensor, at, end

    def take(self, *shape, rows=LANES, dtype=None):
        words = int(np.prod(shape))
        assert self.at + words <= self.end, (self.at, words, self.end)
        v = self.t[0:rows, self.at:self.at + words]
        self.at += words
        if dtype is not None:
            v = v.bitcast(dtype)
        if len(shape) == 2:
            v = v.rearrange("p (a b) -> p a b", a=shape[0])
        elif len(shape) == 3:
            v = v.rearrange("p (a b c) -> p a b c", a=shape[0], b=shape[1])
        return v


def over(ap, n):
    return ap.unsqueeze(2).to_broadcast([ap.shape[0], ap.shape[1], n])


def across(ap, n):
    return ap.unsqueeze(1).to_broadcast([ap.shape[0], n, ap.shape[1]])


def constants(nc, ctx, arena):
    def sb(name, shape):
        return ctx.enter_context(nc.sbuf_tensor(name, shape, F32))[:, :]

    a, early = Arena(arena, 0), Arena(arena, EARLY_AT)
    c = {
        "ident": sb("ident", [LANES, LANES]),
        "ones": sb("ones", [LANES, LANES]),
        "before": early.take(LANES),
        "after": sb("after", [LANES, LANES]),
        "zeros": arena[:, YT_AT:YT_AT + ZEROS],
        "lane": sb("lane", [LANES, LANES]),
        "tile": early.take(T_MAIN),
        "pool_dma": PoolDma(nc, ctx),
        "lane_i": a.take(LANES, dtype=I32),
        "tile_i": a.take(T_MAIN, dtype=I32),
    }
    with Phase(nc, "const") as ph:
        s = ph.sem("set")
        block = ph.block()

        @block.gpsimd
        def _(pool):
            st = Steps(pool, s)
            pool.memset(c["ident"], 0.0).then_inc(s, 1)
            pool.memset(c["ones"], 1.0).then_inc(s, 1)
            pool.memset(c["before"], 0.0).then_inc(s, 1)
            pool.iota(c["lane_i"], pattern=[[1, LANES]], base=0, channel_multiplier=0).then_inc(s, 1)
            pool.iota(c["tile_i"], pattern=[[1, T_MAIN]], base=0, channel_multiplier=0).then_inc(s, 1)
            st.n = 5
            pool.wait_ge(s, 5)
            st.done(pool.affine_select(out=c["ident"], in_=c["ident"], compare_op=ALU.not_equal, fill=1.0,
                                       base=0, pattern=[[-1, LANES]], channel_multiplier=1))
            st.done(pool.affine_select(out=c["before"], in_=c["before"], compare_op=ALU.is_ge, fill=1.0,
                                       base=0, pattern=[[-1, LANES]], channel_multiplier=1))
            st.done(pool.affine_select(out=c["after"], in_=c["ones"], compare_op=ALU.is_ge, fill=0.0,
                                       base=-1, pattern=[[-1, LANES]], channel_multiplier=1))
            pool.wait_ge(s, 8)

        @block.vector
        def _(dve):
            dve.wait_ge(s, 5)
            dve.tensor_copy(c["lane"], c["lane_i"])
            dve.tensor_copy(c["tile"], c["tile_i"])
            dve.memset(c["zeros"], 0.0)
    return c


class Scatter:

    def __init__(self, c, a, parts, n_each, table):
        self.dma, self.table, self.parts, self.n_each = c["pool_dma"], table, parts, n_each
        self.turns, self.at = n_each // STEP, 0
        assert self.turns * STEP == n_each
        self.place(a)

    def place(self, a):
        self.rec = a.take(self.n_each, 4, rows=self.parts)
        self.slot = a.take(self.n_each, rows=self.parts, dtype=I32)
        self.rec_ring = a.take(2, GROUP, 4, rows=self.parts)
        self.slot_ring = a.take(2, GROUP, rows=self.parts, dtype=I32)

    def run(self, ph, pool, turns=None):
        turns = self.turns - self.at if turns is None else turns
        copied = ph.sem("ring_copied")
        counts = ph.sem("ring_turns")

        def turn(i, at, first=False):
            for h in range(2):
                if not first:
                    self.dma.wait(pool, h, at * GROUP)
                of = (at * 2 + h) * GROUP
                pool.tensor_copy(self.rec_ring[:, h, :, :], self.rec[:, bass.ds(of, GROUP), :])
                pool.tensor_copy(self.slot_ring[:, h, :], self.slot[:, bass.ds(of, GROUP)]).then_inc(copied, 1)
                pool.wait_ge(copied, i * 2 + (h + 1))
                pool.sem_inc(counts, 1)
                for j in range(GROUP):
                    pool.indirect_dma_start(
                        self.table,
                        bass.IndirectOffsetOnAxis(ap=self.slot_ring[:, h, j:j + 1].bitcast(U32), axis=0),
                        self.rec_ring[:, h, j, :], None).then_inc(self.dma.sems[h], 16)

        first = 0
        if self.at == 0:
            turn(0, 0, first=True)
            first = 1
        if turns > first:
            with pool.Fori(first, turns) as i:
                turn(i, i + self.at)
        self.at += turns
        if self.at == self.turns:
            for h in range(2):
                self.dma.wait(pool, h, self.turns * GROUP)
                self.dma.finished(h, self.turns * GROUP)


def beside_work(ph, block, job):
    if job is not None:
        @block.gpsimd
        def _(pool):
            job[0].run(ph, pool, job[1])


def bucket_sort(nc, name, c, arena, key, other, weight, parts, tiles, place_scale, scatter, places, spill=None, beside=None,
                clear=None, turns=0):
    n_each = key.shape[0] // parts
    table, rec, slot_i = scatter.table, scatter.rec, scatter.slot
    a = Arena(arena, X_AT, EARLY_AT)
    key_i = a.take(n_each, rows=parts, dtype=I32)
    oth_i = a.take(n_each, rows=parts, dtype=I32)
    wgt = a.take(n_each, rows=parts)
    key_f = a.take(n_each, rows=parts)
    bucket = a.take(n_each, rows=parts)
    slot_f = a.take(n_each, rows=parts)
    shared = a.take(NT * max(n_each, tiles))
    hot = shared[0:parts, 0:NT * n_each].rearrange("p (b i) -> p b i", b=NT)
    run = a.take(3, n_each, rows=parts)
    pads = a.take(tiles, 4)
    total = a.take(NT, rows=parts)
    count = a.take(NT)
    tiles_of = a.take(NT)
    upto = a.take(NT)
    first = a.take(NT)
    cmp = shared[0:1, 0:NT * tiles].rearrange("p (t b) -> p t b", b=NT)
    place_f = a.take(tiles, rows=1)

    with Phase(nc, name) as ph:
        loaded = ph.sem("edges_loaded")
        step = ph.sem("dve_step")
        counted = ph.sem("counted")
        padded = ph.sem("pads_set")
        table_clear = ph.sem("table_clear")
        slots_ready = ph.sem("slots_ready")
        cleared = ph.sem("clear_done")
        spilled = ph.sem("spilled")
        ps = ph.psum("sums", [LANES, 2, 512])
        block = ph.block()

        @block.sync
        def _(sp):
            view = lambda v: v.rearrange("(p i) -> p i", p=parts)
            sp.dma_start(key_i, view(key)).then_inc(loaded, 16)
            sp.dma_start(oth_i, view(other)).then_inc(loaded, 16)
            if weight is not None:
                sp.dma_start(wgt, view(weight)).then_inc(loaded, 16)
            sp.wait_ge(padded, 1)
            sp.dma_start(table.rearrange("(p t) c -> p (t c)", p=LANES),
                         pads.rearrange("p t c -> p (t c)")).then_inc(table_clear, 16)
            sp.wait_ge(table_clear, 16)
            if clear is not None:
                words = clear.shape[0] * D // LANES
                view = clear.rearrange("(p r) d -> p (r d)", p=LANES)
                for i in range(words // ZEROS):
                    sp.dma_start(view[:, i * ZEROS:(i + 1) * ZEROS], c["zeros"]).then_inc(cleared, 16)
                    sp.wait_ge(cleared, 16 * i + 16)

        @block.vector
        def _(dve):
            st = Steps(dve, step)
            dve.memset(pads, 0.0).then_inc(step, 1)
            st.n = 1
            dve.wait_ge(step, 1)
            dve.memset(pads[:, :, 1], -1.0).then_inc(padded, 1)
            dve.wait_ge(loaded, 32 if weight is None else 48)
            st.then(dve.tensor_copy(key_f, key_i))
            st.then(dve.tensor_scalar(bucket, key_f, -float(P // 2), 1.0 / P, ALU.add, ALU.mult))
            st.then(dve.tensor_scalar_add(bucket, bucket, ROUND))
            st.then(dve.tensor_scalar_add(bucket, bucket, -ROUND))
            st.done(dve.tensor_copy(rec[:, :, 0].bitcast(I32), oth_i))
            st.done(dve.tensor_copy(rec[:, :, 3].bitcast(I32), key_i))
            if weight is None:
                st.done(dve.memset(rec[:, :, 2], 0.0))
            else:
                st.done(dve.tensor_copy(rec[:, :, 2], wgt))
            st.done(dve.scalar_tensor_tensor(rec[:, :, 1], bucket, -float(P), key_f, ALU.mult, ALU.add))
            for b in range(NT):
                st.done(dve.tensor_scalar(hot[:, b, :], bucket, c["lane"][0:parts, b:b + 1], None,
                                          ALU.is_equal, ALU.add, accum_out=total[:, b:b + 1]))
            dve.wait_ge(counted, 1)
            st.then(dve.tensor_copy(count, ps[:, 0, 0:NT]))
            st.then(dve.tensor_scalar(tiles_of, count, LANES / 2 - 0.5, 1.0 / LANES, ALU.add, ALU.mult))
            st.then(dve.tensor_scalar_add(tiles_of, tiles_of, ROUND))
            st.then(dve.tensor_scalar_add(tiles_of, tiles_of, -ROUND))
            st.then(dve.tensor_tensor_scan(upto, c["ones"][:, 0:NT], tiles_of, 0.0, ALU.mult, ALU.add))
            st.then(dve.tensor_tensor(first, upto, tiles_of, ALU.subtract))
            st.then(dve.tensor_scalar(first, first, float(LANES), -1.0, ALU.mult, ALU.add))
            st.then(dve.tensor_tensor(first[0:parts], first[0:parts], ps[0:parts, 1, 0:NT], ALU.add))
            numbered, kept = {}, {}

            def number(b):
                if b >= 3:
                    dve.wait_ge(step, kept[b - 3])
                st.done(dve.tensor_tensor_scan(run[:, b % 3, :], c["ones"][0:parts, 0:1].to_broadcast([parts, n_each]),
                                               hot[:, b, :], first[0:parts, b:b + 1], ALU.mult, ALU.add))
                numbered[b] = st.n

            number(0)
            for b in range(NT):
                if b + 1 < NT:
                    number(b + 1)
                dve.wait_ge(step, numbered[b])
                st.done(dve.tensor_tensor(hot[:, b, :], hot[:, b, :], run[:, b % 3, :], ALU.mult))
                kept[b] = st.n
            st.all()
            st.then(dve.tensor_reduce(slot_f, hot.rearrange("p b i -> p i b"), AX.X, ALU.add))
            dve.tensor_copy(slot_i, slot_f).then_inc(slots_ready, 1)
            st.then(dve.tensor_tensor(cmp, across(upto[0:1], tiles), over(c["tile"][0:1, 0:tiles], NT), ALU.is_le))
            st.then(dve.tensor_reduce(place_f, cmp, AX.X, ALU.add))
            st.then(dve.tensor_scalar(places, place_f, float(NT - 1), float(place_scale), ALU.min, ALU.mult))

        @block.tensor
        def _(pe):
            pe.wait_ge(step, 1 + 8 + NT)
            pe.matmul(ps[:, 0, 0:NT], c["ones"][0:parts, :], total, start=True, stop=True)
            pe.matmul(ps[:, 1, 0:NT], c["before"][0:parts, :], total, start=True, stop=True).then_inc(counted, 1)

        beside_work(ph, block, beside)
        if turns:
            @block.gpsimd
            def _(pool):
                pool.wait_ge(table_clear, 16)
                pool.wait_ge(slots_ready, 1)
                scatter.run(ph, pool, turns)

        if spill is None:
            return

        @block.scalar
        def _(act):
            act.wait_ge(slots_ready, 1)
            for to, of in zip(spill, (flat(rec), slot_i)):
                act.dma_start(to, of).then_inc(spilled, 16)
            act.wait_ge(spilled, 32)


def degrees(nc, name, c, a, scatter, degree, beside):
    parts, n_each = scatter.parts, scatter.n_each
    bf16 = mybir.dt.bfloat16
    key = a.take(n_each, rows=parts)
    bucket = a.take(n_each, rows=parts)
    by_target = a.take(2, GROUP * P // 2, rows=parts).bitcast(bf16).rearrange("p h (g c) -> p h g c", g=GROUP)
    by_bucket = a.take(2, GROUP * 13, rows=parts).bitcast(bf16).rearrange("p h (g c) -> p h g c", g=GROUP)
    with Phase(nc, name) as ph:
        step, ready, used = (ph.sem(x) for x in ("dve_step", "group_ready", "group_used"))
        ps = ph.psum("deg", [LANES, 512])
        block = ph.block()
        beside_work(ph, block, beside)

        @block.vector
        def _(dve):
            st = Steps(dve, step)
            st.then(dve.tensor_copy(key, scatter.rec[:, :, 3].bitcast(I32)))
            st.then(dve.tensor_tensor(bucket, key, scatter.rec[:, :, 1], ALU.subtract))
            st.then(dve.tensor_scalar_mul(bucket, bucket, 1.0 / P))
            st.then(dve.tensor_scalar_add(bucket, bucket, ROUND))
            st.then(dve.tensor_scalar_add(bucket, bucket, -ROUND))
            with dve.Fori(0, scatter.turns) as i:
                for h in range(2):
                    dve.wait_ge(used, i * 2 + (h + 1))
                    at = (i * 2 + h) * GROUP
                    dve.tensor_tensor(by_target[:, h, :, :], over(scatter.rec[:, bass.ds(at, GROUP), 1], P),
                                      across(c["lane"][0:parts, 0:P], GROUP), ALU.is_equal)
                    dve.tensor_tensor(by_bucket[:, h, :, 0:NT], over(bucket[:, bass.ds(at, GROUP)], NT),
                                      across(c["lane"][0:parts, 0:NT], GROUP), ALU.is_equal).then_inc(ready, 1)
            dve.wait_ge(used, 2 * scatter.turns + 2)
            st.then(dve.tensor_copy(degree, ps[0:P, 0:NT]))

        @block.tensor
        def _(pe):
            pe.sem_inc(used, 2)

            def turn(i, first=False, final=False):
                for h in range(2):
                    pe.wait_ge(ready, i * 2 + (h + 1))
                    for j in range(GROUP):
                        last = pe.matmul(ps[0:P, 0:NT], by_target[:, h, j, :], by_bucket[:, h, j, 0:NT],
                                         start=(first and h == 0 and j == 0), stop=(final and h == 1 and j == GROUP - 1))
                    last.then_inc(used, 1)

            turn(0, first=True)
            with pe.Fori(1, scatter.turns - 1) as i:
                turn(i)
            turn(scatter.turns - 1, final=True)


def records(view, table):
    return view, table.rearrange("(t p) c -> p t c", p=LANES)


def graph_sum(nc, name, c, arena, rows, rec, places, acc, tiles, weighted, bias=None, arrived=(), table=None):
    a = Arena(arena, TMP_AT, REC_AT)
    msg = a.take(RING, GROUP, D)
    hot = a.take(RING, GROUP, P)
    own = a.take(RING, GROUP, 4)
    bodies = tiles // (RING * GROUP)
    with Phase(nc, name) as ph:
        turns = ph.sem("pool_turns")
        idx_ready = [ph.sem(f"idx_ready{h}") for h in range(RING)]
        gathered = c["pool_dma"]
        hot_ready = [ph.sem(f"hot_ready{h}") for h in range(RING)]
        summed = ph.sem("quads_summed")
        freed = ph.sem("psum_freed")
        step = ph.sem("dve_step")
        ps = ph.psum("sum", [LANES, 2, 4, D])
        bias_loaded = ph.sem("bias_loaded")
        loaded = ph.sem("records_loaded")
        block = ph.block()

        @block.sync
        def _(sp):
            if bias is not None:
                sp.dma_start(bias[0], bias[1].unsqueeze(0).to_broadcast([P, D])).then_inc(bias_loaded, 16)
            for s, dmas in arrived:
                sp.wait_ge(s, 16 * dmas)
            if table is not None:
                to, of = records(rec, table)
                for i in range(bodies):
                    turn = slice(i * RING * GROUP, (i + 1) * RING * GROUP)
                    sp.dma_start(to[:, turn, :], of[:, turn, :]).then_inc(loaded, 16)
                    sp.wait_ge(loaded, 16 * i + 16)

        @block.scalar
        def _(act):
            with act.Fori(0, bodies) as i:
                if table is not None:
                    act.wait_ge(loaded, i * 16 + 16)
                for h in range(RING):
                    act.wait_ge(summed, i * QUADS + (2 * h + 2))
                    act.copy(own[:, h, :, :], rec[:, bass.ds((i * RING + h) * GROUP, GROUP), :])\
                       .then_inc(idx_ready[h], 1)


        @block.gpsimd
        def _(pool):
            with pool.Fori(0, bodies) as i:
                for h in range(RING):
                    pool.wait_ge(idx_ready[h], i + 1)
                    pool.sem_inc(turns, 1)
                    for j in range(GROUP):
                        pool.indirect_dma_start(
                            msg[:, h, j, :], None, rows,
                            bass.IndirectOffsetOnAxis(ap=own[:, h, j, 0:1].bitcast(U32), axis=0))\
                            .then_inc(gathered.sems[h], 16)

        @block.tensor
        def _(pe):
            pe.sem_inc(summed, QUADS)
            with pe.Fori(0, bodies) as i:
                for h in range(RING):
                    pe.wait_ge(hot_ready[h], i + 1)
                    gathered.wait(pe, h, i * GROUP + GROUP)
                    for q in range(2):
                        pe.wait_ge(freed, i * QUADS + (2 * h + q + 1))
                        for j in range(4):
                            t = 4 * q + j
                            last = pe.matmul(ps[0:P, q, j, :], hot[:, h, t, :], msg[:, h, t, :],
                                             start=True, stop=True)
                        last.then_inc(summed, 1)

        for h in range(RING):
            gathered.finished(h, GROUP * bodies)

        @block.vector
        def _(dve):
            st = Steps(dve, step)
            dve.sem_inc(freed, 2)
            if bias is None:
                st.then(dve.memset(acc, 0.0))
            else:
                dve.wait_ge(bias_loaded, 16)
                st.then(dve.tensor_copy(acc.rearrange("p (t d) -> p t d", d=D), across(bias[0], NT)))

            def one_hot(i, h):
                dve.wait_ge(summed, i * QUADS + (2 * h + 2))
                dve.wait_ge(idx_ready[h], i + 1)
                if weighted:
                    for j in range(GROUP):
                        hit = dve.tensor_scalar(hot[:, h, j, :], c["lane"][:, 0:P], own[:, h, j, 1:2], own[:, h, j, 2:3],
                                                ALU.is_equal, ALU.mult)
                else:
                    hit = dve.tensor_tensor(hot[:, h, :, :], over(own[:, h, :, 1], P), across(c["lane"][:, 0:P], GROUP),
                                            ALU.is_equal)
                hit.then_inc(hot_ready[h], 1)

            def add_group(i, h):
                _, place = nc.values_load_multi_w_load_instructions(
                    places[0:1, bass.ds((i * RING + h) * GROUP, GROUP)], engines=(mybir.EngineType.DVE,),
                    min_val=0, max_val=(NT - 1) * D)
                for q in range(2):
                    dve.wait_ge(summed, i * QUADS + (QUADS + 2 * h + q + 1))
                    for j in range(4):
                        to = acc[:, bass.ds(place[4 * q + j], D)]
                        st.then(dve.tensor_tensor(to, to, ps[0:P, q, j, :], ALU.add))
                    dve.sem_inc(freed, 1)

            for h in range(RING):
                one_hot(0, h)
            with dve.Fori(0, bodies - 1) as i:
                st.enter(i, RING * GROUP)
                for h in range(RING):
                    add_group(i, h)
                    one_hot(i + 1, h)
            st.leave(bodies - 1)
            for h in range(RING):
                add_group(bodies - 1, h)


OUT_BANKS = 4


def quads():
    return [(t, min(4, NT - t)) for t in range(0, NT, 4)]


def flat(ap):
    return ap.rearrange("p a b -> p (a b)")


def to_features(nc, name, c, arena, y, yt, prepare, table=None, loads=(), roots=None, beside=None, later=(), arrived=(),
                combine=None, product=None):
    with Phase(nc, name) as ph:
        loaded = ph.sem("loaded")
        step = ph.sem("dve_step")
        quad_ready = ph.sem("quad_ready")
        transposed = ph.sem("transposed")
        copied = ph.sem("copied")
        stored = ph.sem("stored")
        asked = ph.sem("root_asked")
        rooted = ph.sem("root_ready")
        weights, multiplied, taken = (ph.sem(s) for s in ("weights_loaded", "multiplied", "products_taken"))
        ps = ph.psum("t", [LANES, 8, 512])
        banks = 8 if product is None else 4
        block = ph.block()

        beside_work(ph, block, beside)
        if combine is not None:
            combine.begin(ph, block)

        @block.sync
        def _(sp):
            for to, of in loads:
                sp.dma_start(to, of).then_inc(loaded, 16)
            if product is not None:
                w, w_dram, bias, out, out_table = product
                sp.dma_start(w, w_dram.rearrange("(k p) f -> p k f", p=LANES)).then_inc(weights, 16)
                if bias is not None:
                    sp.dma_start(bias[0], bias[1].unsqueeze(0).to_broadcast([P, D])).then_inc(weights, 16)
            for s, to, of in later:
                sp.dma_start(to, of).then_inc(s, 16)
            for s, dmas in arrived:
                sp.wait_ge(s, 16 * dmas)
            if table is not None:
                rows = table.rearrange("(t p) d -> p t d", p=P)
                for q, (t, n) in enumerate(quads()):
                    sp.wait_ge(quad_ready, q + 1)
                    sp.dma_start(rows[:, t:t + n, :], y[:, t:t + n, :]).then_inc(stored, 16)
                sp.wait_ge(stored, 16 * len(quads()))

            if product is not None:
                rows = out_table.rearrange("(t p) d -> p t d", p=P)
                for t, n in quads():
                    sp.wait_ge(taken, t + n)
                    sp.dma_start(rows[:, t:t + n, :], out[:, t:t + n, :]).then_inc(stored, 16)
                sp.wait_ge(stored, 16 * len(quads()))

        @block.vector
        def _(dve):
            st = Steps(dve, step)
            if loads:
                dve.wait_ge(loaded, 16 * len(loads))
            if product is None:
                prepare(dve, st, quad_ready, asked, rooted)
                return
            _, _, bias, out, _ = product
            dve.wait_ge(weights, 16 + 16 * (bias is not None))

            def take(first, n):
                for t in range(first, first + n):
                    dve.wait_ge(multiplied, t + 1)
                    of = ps[0:P, 4 + t % 4, 0:D]
                    if bias is None:
                        dve.tensor_copy(out[:, t, :], of).then_inc(taken, 1)
                    else:
                        dve.tensor_tensor(out[:, t, :], bias[0], of, ALU.add).then_inc(taken, 1)

            prepare(dve, st, quad_ready, asked, rooted, take)

        @block.tensor
        def _(pe):
            if yt is None:
                return

            def turn(q, t, n):
                pe.wait_ge(quad_ready, q + 1)
                for k in range(DK):
                    u = DK * q + k
                    if u >= banks:
                        pe.wait_ge(copied, u + 1 - banks)
                    for j in range(n):
                        last = pe.transpose(ps[:, u % banks, j * P:(j + 1) * P],
                                            y[:, t + j, k * LANES:(k + 1) * LANES], c["ident"][0:P, 0:P])
                    last.then_inc(transposed, 1)

            def multiply(q, first, n):
                w = product[0]
                pe.wait_ge(copied, DK * q + DK)
                for t in range(first, first + n):
                    if t >= 4:
                        pe.wait_ge(taken, t - 3)
                    for k in range(DK):
                        last = pe.matmul(ps[0:P, 4 + t % 4, 0:D], yt[:, k, t * P:(t + 1) * P], w[:, k, :],
                                         start=(k == 0), stop=(k == DK - 1))
                    last.then_inc(multiplied, 1)

            if product is not None:
                pe.wait_ge(weights, 16 + 16 * (product[2] is not None))
            for q, (t, n) in enumerate(quads()):
                turn(q, t, n)
                if product is not None:
                    multiply(q, t, n)

        @block.scalar
        def _(act):
            def root(t, n):
                act.activation(roots[:, t:t + n], roots[:, t:t + n], ACT.Sqrt).then_inc(rooted, 1)

            def copy(q, t, n):
                for k in range(DK):
                    u = DK * q + k
                    act.wait_ge(transposed, u + 1)
                    act.copy(yt[:, k, t * P:(t + n) * P], ps[:, u % banks, 0:n * P]).then_inc(copied, 1)

            if roots is not None and combine is None:
                act.wait_ge(asked, 1)
                root(0, NT)
            if yt is None:
                return
            for q, (t, n) in enumerate(quads()):
                if combine is not None:
                    act.wait_ge(asked, q + 1)
                    root(t, n)
                    if q:
                        copy(q - 1, *quads()[q - 1])
                else:
                    copy(q, t, n)
            if combine is not None:
                copy(q, t, n)

        if combine is not None:
            combine.finished()


def row_statistics(dve, st, x, stats, mean, root, spare, tiles=range(NT), before=None):
    for t in tiles:
        if before is not None:
            before(t)
        st.done(dve.bn_stats(stats[:, t, :], x[:, t, :]))
    st.all()
    half = D // 2
    lo, hi = tiles[0], tiles[-1] + 1
    stats, mean, root, spare = stats[:, lo:hi, :], mean[:, lo:hi], root[:, lo:hi], spare[:, lo:hi]
    st.then(dve.tensor_tensor(mean, stats[:, :, 1], stats[:, :, 4], ALU.add))
    st.then(dve.tensor_scalar_mul(mean, mean, 0.5))
    st.then(dve.tensor_tensor(spare, stats[:, :, 1], mean, ALU.subtract))
    st.then(dve.tensor_tensor(spare, spare, spare, ALU.mult))
    st.then(dve.tensor_tensor(root, stats[:, :, 2], stats[:, :, 5], ALU.add))
    st.then(dve.scalar_tensor_tensor(root, root, 1.0 / (2 * half), spare, ALU.mult, ALU.add))
    return dve.tensor_scalar_add(root, root, EPS)


def layer_norm(nc, name, c, arena, x, y, yt, table=None, loads=(), beside=None, plus=None, later=(), arrived=(),
               combine=None, a=None, product=None):
    a = a or Arena(arena, TMP_AT)
    stats = a.take(NT, 6, rows=P)
    mean, root, spare = (a.take(NT, rows=P) for _ in range(3))

    def prepare(dve, st, quad_ready, asked, rooted, take=None):
        def add(t):
            xt, acc = x[:, t, :], plus[0][:, t, :]
            if plus[1] is None:
                st.then(dve.tensor_tensor(xt, xt, acc, ALU.add))
            else:
                st.then(dve.scalar_tensor_tensor(xt, acc, plus[1][:, t:t + 1], xt, ALU.mult, ALU.add))

        def normalize(first, n):
            for t in range(first, first + n):
                last = dve.tensor_scalar(y[:, t, :], x[:, t, :], mean[:, t:t + 1], root[:, t:t + 1],
                                         ALU.subtract, ALU.mult)
            last.then_inc(quad_ready, 1)

        if combine is None:
            row_statistics(dve, st, x, stats, mean, root, spare, before=plus and add).then_inc(asked, 1)
            dve.wait_ge(rooted, 1)
            st.then(dve.reciprocal(root, root))
            for first, n in quads():
                normalize(first, n)
            return

        def later(q, first, n):
            dve.wait_ge(rooted, q + 1)
            st.then(dve.reciprocal(root[:, first:first + n], root[:, first:first + n]))
            normalize(first, n)

        for q, (first, n) in enumerate(quads()):
            row_statistics(dve, st, x, stats, mean, root, spare, range(first, first + n),
                           lambda t: combine.add(dve, t)).then_inc(asked, 1)
            if q:
                later(q - 1, *quads()[q - 1])
            if take is not None and q >= 2:
                take(*quads()[q - 2])
        later(q, *quads()[q])
        if take is not None:
            take(*quads()[q - 1])
            take(*quads()[q])

    to_features(nc, name, c, arena, y, yt, prepare, table, loads, roots=root, beside=beside,
                later=later, arrived=arrived, combine=combine, product=product)


def dense(nc, name, products, bias, out, func, stats=None, beside=None):
    m = out.shape[1]
    with Phase(nc, name) as ph:
        loaded = ph.sem("weights_loaded")
        multiplied = ph.sem("multiplied")
        free = ph.sem("psum_free")
        ps = ph.psum("out", [LANES, m, 512])
        block = ph.block()
        beside_work(ph, block, beside)

        @block.sync
        def _(sp):
            for _, w, w_dram in products:
                sp.dma_start(w, w_dram.rearrange("(k p) f -> p k f", p=LANES)).then_inc(loaded, 16)

        @block.tensor
        def _(pe):
            pe.wait_ge(loaded, 16 * len(products) + 16)

            def chunk(n, at, cols):
                for fo in range(m):
                    pe.wait_ge(free, n * m + (fo + 1))
                    parts = [(rhs, w, k) for rhs, w, _ in products for k in range(w.shape[1])]
                    for i, (rhs, w, k) in enumerate(parts):
                        last = pe.matmul(ps[:, fo, 0:cols], w[:, k, fo * LANES:(fo + 1) * LANES],
                                         rhs[:, k, bass.ds(at, cols)], start=(i == 0), stop=(i == len(parts) - 1))
                    last.then_inc(multiplied, 1)

            with pe.Fori(0, FULL) as n:
                chunk(n, n * CHUNK, CHUNK)
            chunk(FULL, FULL * CHUNK, N - FULL * CHUNK)

        @block.scalar
        def _(act):
            with nc.allow_non_contiguous_dma(reason="a column of biases"):
                act.dma_start(bias[0], bias[1].rearrange("(m p) -> p m", p=LANES)).then_inc(loaded, 16)
            act.wait_ge(loaded, 16 * len(products) + 16)
            act.sem_inc(free, m)

            def chunk(n, at, cols):
                for fo in range(m):
                    act.wait_ge(multiplied, n * m + (fo + 1))
                    act.activation(out[:, fo, bass.ds(at, cols)], ps[:, fo, 0:cols], func,
                                   bias=bias[0][:, fo:fo + 1]).then_inc(free, 1)

            with act.Fori(0, FULL) as n:
                chunk(n, n * CHUNK, CHUNK)
            chunk(FULL, FULL * CHUNK, N - FULL * CHUNK)

        @block.vector
        def _(dve):
            if stats is None:
                return

            def chunk(n, at, cols):
                for fo in range(m):
                    dve.wait_ge(free, n * m + (m + fo + 1))
                    dve.bn_stats(stats[:, fo, bass.ds(n * 6, 6)], out[:, fo, bass.ds(at, cols)])

            with dve.Fori(0, FULL) as n:
                chunk(n, n * CHUNK, CHUNK)
            chunk(FULL, FULL * CHUNK, N - FULL * CHUNK)


def batch_norm_elu(nc, name, a, h, stats, gamma, beta, beside=None, later=()):
    m = h.shape[1]
    mv = a.take(m, 2)
    g, b, scale, shift = (a.take(m) for _ in range(4))
    e = a.take(2, N)
    with Phase(nc, name) as ph:
        loaded = ph.sem("loaded")
        step = ph.sem("dve_step")
        asked = ph.sem("root_asked")
        rooted = ph.sem("root_ready")
        scaled = ph.sem("scale_ready")
        act_step = ph.sem("act_step")
        split = ph.sem("split_ready")
        freed = ph.sem("exp_freed")
        block = ph.block()
        beside_work(ph, block, beside)

        @block.sync
        def _(sp):
            with nc.allow_non_contiguous_dma(reason="a column of parameters"):
                sp.dma_start(g, gamma.rearrange("(m p) -> p m", p=LANES)).then_inc(loaded, 16)
                sp.dma_start(b, beta.rearrange("(m p) -> p m", p=LANES)).then_inc(loaded, 16)
            for s, to, of in later:
                sp.dma_start(to, of).then_inc(s, 16)

        @block.vector
        def _(dve):
            st = Steps(dve, step)
            for f in range(m):
                st.done(dve.bn_aggr(mv[:, f, :], stats[:, f, :]))
            dve.wait_ge(step, m)
            dve.tensor_scalar_add(scale, mv[:, :, 1], EPS).then_inc(asked, 1)
            dve.wait_ge(rooted, 1)
            st.then(dve.reciprocal(scale, scale))
            dve.wait_ge(loaded, 32)
            st.then(dve.tensor_tensor(scale, scale, g, ALU.mult))
            st.then(dve.tensor_tensor(shift, mv[:, :, 0], scale, ALU.mult))
            dve.tensor_tensor(shift, b, shift, ALU.subtract).then_inc(scaled, 1)
            for f in range(m):
                dve.wait_ge(split, f + 1)
                st.then(dve.tensor_scalar(e[:, f % 2, :], e[:, f % 2, :], 1.0, -1.0, ALU.min, ALU.add))
                dve.tensor_tensor(h[:, f, :], h[:, f, :], e[:, f % 2, :], ALU.add).then_inc(freed, 1)

        @block.scalar
        def _(act):
            act.wait_ge(asked, 1)
            act.activation(scale, scale, ACT.Sqrt).then_inc(rooted, 1)
            act.wait_ge(scaled, 1)
            for f in range(m):
                if f >= 2:
                    act.wait_ge(freed, f - 1)
                act.activation(e[:, f % 2, :], h[:, f, :], ACT.Exp, bias=shift[:, f:f + 1],
                               scale=scale[:, f:f + 1]).then_inc(act_step, 1)
                act.wait_ge(act_step, f + 1)
                act.activation(h[:, f, :], h[:, f, :], ACT.Relu, bias=shift[:, f:f + 1],
                               scale=scale[:, f:f + 1]).then_inc(split, 1)


def project(nc, name, ht, w, w_dram, out, bias=None, add=False, table=None, arrives={}, later=()):
    with Phase(nc, name) as ph:
        loaded = ph.sem("loaded")
        multiplied = ph.sem("multiplied")
        added = ph.sem("added")
        step = ph.sem("dve_step")
        stored = ph.sem("stored")
        ps = ph.psum("out", [LANES, 8, 512])
        block = ph.block()
        ks = w.shape[1]
        n_loads = 1 + (bias is not None)

        @block.sync
        def _(sp):
            sp.dma_start(w, w_dram.rearrange("(k p) f -> p k f", p=LANES)).then_inc(loaded, 16)
            if bias is not None:
                sp.dma_start(bias[0], bias[1].unsqueeze(0).to_broadcast([P, D])).then_inc(loaded, 16)
            for s, to, of in later:
                sp.dma_start(to, of).then_inc(s, 16)
            if table is not None:
                rows = table.rearrange("(t p) d -> p t d", p=P)
                for t, n in quads():
                    sp.wait_ge(added, t + n)
                    sp.dma_start(rows[:, t:t + n, :], out[:, t:t + n, :]).then_inc(stored, 16)
                sp.wait_ge(stored, 16 * len(quads()))

        @block.tensor
        def _(pe):
            pe.wait_ge(loaded, 16 * n_loads)
            for t in range(NT):
                if t >= 8:
                    pe.wait_ge(added, t - 7)
                for k in range(ks):
                    last = pe.matmul(ps[0:P, t % 8, 0:D], ht[:, k, t * P:(t + 1) * P], w[:, k, :],
                                     start=(k == 0), stop=(k == ks - 1))
                last.then_inc(multiplied, 1)

        @block.vector
        def _(dve):
            st = Steps(dve, step)
            dve.wait_ge(loaded, 16 * n_loads)
            for t in range(NT):
                if add and bias is not None and t % 4 == 0:
                    if t in arrives:
                        dve.wait_ge(arrives[t], 16)
                    n = min(4, NT - t)
                    st.then(dve.tensor_tensor(out[:, t:t + n, :], out[:, t:t + n, :], across(bias[0], n), ALU.add))
                dve.wait_ge(multiplied, t + 1)
                if add:
                    dve.tensor_tensor(out[:, t, :], out[:, t, :], ps[0:P, t % 8, 0:D], ALU.add).then_inc(added, 1)
                elif bias is not None:
                    dve.tensor_tensor(out[:, t, :], bias[0], ps[0:P, t % 8, 0:D], ALU.add).then_inc(added, 1)
                else:
                    dve.tensor_copy(out[:, t, :], ps[0:P, t % 8, 0:D]).then_inc(added, 1)


def experts(nc, name, c, a, yt, target, hidden, last_w, gates, bias_gates, last_b, count, func, beside=None):
    widths = [w.shape[2] for w, _ in hidden]
    ins = [D] + widths
    w_sb = [a.take(2, ins[i] // LANES * widths[i]).rearrange("p h (k f) -> p h k f", f=widths[i])
            for i in range(len(hidden))]
    b_sb = [a.take(2, widths[i] // LANES) for i in range(len(hidden))]
    wl_sb = a.take(2, widths[-1] // LANES * D).rearrange("p h (k f) -> p h k f", f=D)
    h_sb = [a.take(2, widths[i] // LANES * CHUNK).rearrange("p h (k f) -> p h k f", f=CHUNK)
            for i in range(len(hidden))]
    gate = a.take(2, NT, rows=P)
    n_bias = bias_gates.shape[2]
    gates_t = a.take(N, rows=n_bias)
    lb_sb = a.take(D, rows=n_bias)
    turns = count // 2
    assert turns * 2 == count
    n_w = 2 * len(hidden) + 1
    stages = len(hidden) + 1
    n_ch = len(CHUNKS)
    units = [w // LANES for w in widths]

    def order():
        for at in range(n_ch + stages - 1):
            for s in range(stages):
                if 0 <= at - s < n_ch:
                    yield s, at - s

    with Phase(nc, name) as ph:
        loaded = [ph.sem(f"weights_loaded{h}") for h in range(2)]
        small_loaded = ph.sem("last_bias_loaded")
        multiplied = [ph.sem(f"multiplied{s}") for s in range(stages)]
        written = [ph.sem(f"written{s}") for s in range(stages - 1)]
        added = ph.sem("added")
        gate_ready = ph.sem("gate_ready")
        g_t = ph.sem("gates_transposed")
        g_c = ph.sem("gates_copied")
        b_m = ph.sem("bias_multiplied")
        step = ph.sem("dve_step")
        ps_h = ph.psum("hidden", [LANES, 4, 512])
        ps_o = ph.psum("out", [LANES, OUT_BANKS, 2, D])
        banks = [list(range(4))] if stages == 2 else [[0, 1], [2, 3]]
        block = ph.block()
        beside_work(ph, block, beside)

        def hid(i, h, n, s):
            return i * (2 * n_ch * units[s]) + (h * n_ch + n) * units[s]

        pairs = [(t, min(2, NT - t)) for t in range(0, NT, 2)]
        per_turn = 2 * len(pairs)

        def last_use(u):
            return max(v for v in range(-per_turn, u) if v % per_turn % OUT_BANKS == u % OUT_BANKS) + 1 + per_turn

        @block.sync
        def _(sp):
            sp.dma_start(lb_sb, last_b).then_inc(small_loaded, 16)
            with sp.Fori(0, turns) as i:
                for h in range(2):
                    e = i * 2 + h
                    sp.wait_ge(multiplied[-1], i * per_turn + (h + 1) * len(pairs))
                    for j, (w, b) in enumerate(hidden):
                        sp.dma_start(w_sb[j][:, h, :, :],
                                     w[bass.ds(e, 1), :, :].rearrange("e (k p) f -> p (e k) f", p=LANES))\
                            .then_inc(loaded[h], 16)
                        with nc.allow_non_contiguous_dma(reason="a column of biases"):
                            sp.dma_start(b_sb[j][:, h, :], b[bass.ds(e, 1), :].rearrange("e (m p) -> p (e m)", p=LANES))\
                                .then_inc(loaded[h], 16)
                    sp.dma_start(wl_sb[:, h, :, :],
                                 last_w[bass.ds(e, 1), :, :].rearrange("e (k p) f -> p (e k) f", p=LANES))\
                        .then_inc(loaded[h], 16)

        @block.tensor
        def _(pe):
            for q, (t, n) in enumerate(quads()):
                if q >= 4:
                    pe.wait_ge(g_c, q - 3)
                for j in range(n):
                    last = pe.transpose(ps_h[0:n_bias, q % 4, j * P:(j + 1) * P], bias_gates[:, t + j, :],
                                        c["ident"][0:P, 0:P])
                last.then_inc(g_t, 1)
            pe.wait_ge(small_loaded, 16)
            for t in range(NT):
                if t % 4 == 0:
                    pe.wait_ge(g_c, t // 4 + 1)
                if t >= OUT_BANKS:
                    pe.wait_ge(step, t - OUT_BANKS + 1)
                pe.matmul(ps_o[0:P, t % OUT_BANKS, 0, :], gates_t[:, t * P:(t + 1) * P], lb_sb, start=True, stop=True)\
                    .then_inc(b_m, 1)
            pe.wait_ge(step, NT)
            pe.sem_inc(multiplied[-1], per_turn)
            with pe.Fori(0, turns) as i:
                for h in range(2):
                    pe.wait_ge(loaded[h], i * (16 * n_w) + 16 * n_w)
                    for s, n in order():
                        at, cols = CHUNKS[n]
                        if s < stages - 1:
                            if s > 0:
                                pe.wait_ge(written[s - 1], hid(i, h, n + 1, s - 1) + len(banks[s - 1]))
                            for m in range(units[s]):
                                pe.wait_ge(written[s], hid(i, h, n, s) + (m + 1))
                                ks = ins[s] // LANES
                                bank = banks[s][m % len(banks[s])]
                                for k in range(ks):
                                    rhs = yt[:, k, at:at + cols] if s == 0 else h_sb[s - 1][:, n % 2, k, 0:cols]
                                    last = pe.matmul(ps_h[:, bank, 0:cols],
                                                     w_sb[s][:, h, k, m * LANES:(m + 1) * LANES], rhs,
                                                     start=(k == 0), stop=(k == ks - 1))
                                last.then_inc(multiplied[s], 1)
                        else:
                            pe.wait_ge(written[s - 1], hid(i, h, n + 1, s - 1) + len(banks[s - 1]))
                            ks = widths[-1] // LANES
                            for u, (t, tiles) in enumerate(pairs):
                                if not 4 * n <= t < 4 * n + 4:
                                    continue
                                v = h * len(pairs) + u
                                pe.wait_ge(added, i * per_turn + last_use(v))
                                for j in range(tiles):
                                    col = (t + j - 4 * n) * P
                                    for k in range(ks):
                                        last = pe.matmul(ps_o[0:P, v % OUT_BANKS, j, :],
                                                         h_sb[s - 1][:, n % 2, k, col:col + P], wl_sb[:, h, k, :],
                                                         start=(k == 0), stop=(k == ks - 1))
                                last.then_inc(multiplied[s], 1)

        @block.scalar
        def _(act):
            for q, (t, n) in enumerate(quads()):
                act.wait_ge(g_t, q + 1)
                act.copy(gates_t[:, t * P:(t + n) * P], ps_h[0:n_bias, q % 4, 0:n * P]).then_inc(g_c, 1)
            for s in range(stages - 1):
                act.sem_inc(written[s], len(banks[s]))
            with act.Fori(0, turns) as i:
                for h in range(2):
                    act.wait_ge(loaded[h], i * (16 * n_w) + 16 * n_w)
                    for s, n in order():
                        if s == stages - 1:
                            continue
                        at, cols = CHUNKS[n]
                        for m in range(units[s]):
                            act.wait_ge(multiplied[s], hid(i, h, n, s) + (m + 1))
                            act.activation(h_sb[s][:, n % 2, m, 0:cols],
                                           ps_h[:, banks[s][m % len(banks[s])], 0:cols], func,
                                           bias=b_sb[s][:, h, m:m + 1]).then_inc(written[s], 1)

        @block.vector
        def _(dve):
            st = Steps(dve, step)
            for t in range(NT):
                dve.wait_ge(b_m, t + 1)
                st.done(dve.tensor_tensor(target[:, t, :], target[:, t, :], ps_o[0:P, t % OUT_BANKS, 0, :], ALU.add))
            dve.wait_ge(step, NT)
            dve.sem_inc(added, per_turn)
            with dve.Fori(0, turns) as i:
                dve.wait_ge(added, i * per_turn + per_turn)
                for h in range(2):
                    dve.tensor_copy(gate[:, h, :], gates[:, :, bass.ds(i * 2 + h, 1)].rearrange("p t e -> p (t e)"))\
                       .then_inc(gate_ready, 1)
                for h in range(2):
                    dve.wait_ge(gate_ready, i * 2 + 2)
                    for u, (t, tiles) in enumerate(pairs):
                        v = h * len(pairs) + u
                        dve.wait_ge(multiplied[-1], i * per_turn + (per_turn + v + 1))
                        for j in range(tiles):
                            last = dve.scalar_tensor_tensor(target[:, t + j, :], ps_o[0:P, v % OUT_BANKS, j, :],
                                                            gate[:, h, t + j:t + j + 1], target[:, t + j, :],
                                                            ALU.mult, ALU.add)
                        last.then_inc(added, 1)


PAIR_TILE = 256


def pair_tiles(experts_n):
    most = (2 * N + experts_n * (PAIR_TILE - 1)) // PAIR_TILE
    return most + most % 2


PAIR_ROWS = pair_tiles(16) * PAIR_TILE
assert PAIR_ROWS * D // LANES % ZEROS == 0


def send_to_experts(nc, name, c, a, y, one, two, slots, expert_of, table):
    e = one.shape[2]
    tiles = pair_tiles(e)
    both = a.take(NT, e, rows=P)
    run = a.take(NT, e, rows=P)
    total = a.take(e, rows=P)
    tiles_of, upto, first = a.take(e), a.take(e), a.take(e)
    cmp = a.take(tiles, e, rows=1)
    exp_f = a.take(tiles, rows=1)
    slot_f = a.take(NT, rows=P)
    index = a.take(tiles, rows=1)
    index_i = a.take(tiles, rows=1, dtype=I32)
    before = a.take(LANES)
    with Phase(nc, name) as ph:
        step, counted, ready, set_ = (ph.sem(x) for x in ("dve_step", "counted", "slots_ready", "constants_set"))
        totals = ph.sem("totals_ready")
        sent = c["pool_dma"]
        ps = ph.psum("sums", [LANES, 2, 512])
        block = ph.block()

        @block.vector
        def _(dve):
            st = Steps(dve, step)
            tt = dve.tensor_tensor
            st.then(tt(both, one, two, ALU.add))
            tt_total = dve.tensor_reduce(total, both.rearrange("p t e -> p e t"), AX.X, ALU.add)
            tt_total.then_inc(totals, 1)
            dve.wait_ge(counted, 1)
            st.then(dve.tensor_scalar(tiles_of, ps[:, 0, 0:e], PAIR_TILE / 2 - 0.5, 1.0 / PAIR_TILE, ALU.add, ALU.mult))
            st.then(dve.tensor_scalar_add(tiles_of, tiles_of, ROUND))
            st.then(dve.tensor_scalar_add(tiles_of, tiles_of, -ROUND))
            st.then(dve.tensor_tensor_scan(upto, c["ones"][:, 0:e], tiles_of, 0.0, ALU.mult, ALU.add))
            st.then(tt(first, upto, tiles_of, ALU.subtract))
            st.then(dve.tensor_scalar(first, first, float(PAIR_TILE), -1.0, ALU.mult, ALU.add))
            st.then(tt(first[0:P], first[0:P], ps[0:P, 1, 0:e], ALU.add))
            for x in range(e):
                st.done(dve.tensor_tensor_scan(run[:, :, x], c["ones"][0:P, 0:NT], both[:, :, x], first[0:P, x:x + 1],
                                               ALU.mult, ALU.add))
            st.all()
            for i, pick in enumerate((one, two)):
                st.then(tt(both, pick, run, ALU.mult))
                st.then(dve.tensor_reduce(slot_f, both, AX.X, ALU.add))
                st.then(dve.tensor_copy(slots[:, i, :], slot_f))
            dve.sem_inc(ready, 1)
            dve.wait_ge(set_, 4)
            st.then(dve.tensor_copy(index, index_i))
            st.then(tt(cmp, across(upto[0:1], tiles), over(index, e), ALU.is_le))
            st.then(dve.tensor_reduce(exp_f, cmp, AX.X, ALU.add))
            st.then(dve.tensor_scalar(expert_of, exp_f, float(e - 1), 1.0, ALU.min, ALU.mult))

        @block.tensor
        def _(pe):
            pe.wait_ge(totals, 1)
            pe.wait_ge(set_, 4)
            pe.matmul(ps[:, 0, 0:e], c["ones"][0:P, :], total, start=True, stop=True)
            pe.matmul(ps[:, 1, 0:e], before[0:P, :], total, start=True, stop=True).then_inc(counted, 1)

        @block.gpsimd
        def _(pool):
            pool.iota(index_i, pattern=[[1, tiles]], base=0, channel_multiplier=0).then_inc(set_, 1)
            pool.memset(before, 0.0).then_inc(set_, 1)
            pool.wait_ge(set_, 2)
            pool.affine_select(out=before, in_=before, compare_op=ALU.is_ge, fill=1.0, base=0,
                               pattern=[[-1, LANES]], channel_multiplier=1).then_inc(set_, 2)
            pool.wait_ge(ready, 1)
            for t in range(NT):
                for i in range(2):
                    pool.indirect_dma_start(
                        table, bass.IndirectOffsetOnAxis(ap=slots[:, i, t:t + 1].bitcast(U32), axis=0),
                        y[:, t, :], None).then_inc(sent.sems[0], 16)
            sent.wait(pool, 0, 2 * NT)
            sent.finished(0, 2 * NT)


def run_experts(nc, name, c, a, table, expert_of, hidden, last, out_table, func):
    e, _, f = hidden[0][0].shape
    tiles = pair_tiles(e)
    assert tiles * PAIR_TILE <= PAIR_ROWS
    units = f // LANES
    layers = range(len(hidden))
    ins = [DK] + [units] * len(hidden)
    w_sb = [[a.take(ins[s], f) for _ in range(2)] for s in layers]
    b_sb = [[a.take(units) for _ in range(2)] for s in layers]
    wl_sb = [a.take(units, D) for _ in range(2)]
    bl_sb = [a.take(D) for _ in range(2)]
    xs = [a.take(2, D) for _ in range(2)]
    xt = [a.take(DK, PAIR_TILE) for _ in range(2)]
    hid = [[a.take(units, PAIR_TILE) for _ in range(2)] for s in layers]
    res = [a.take(2, D) for _ in range(2)]
    rows_in = table[0:tiles * PAIR_TILE, :].rearrange("(t s p) d -> t p s d", p=LANES, s=2)
    rows_out = out_table[0:tiles * PAIR_TILE, :].rearrange("(t s p) d -> t p s d", p=LANES, s=2)
    with Phase(nc, name) as ph:
        weights = [[ph.sem(f"weights{s}_loaded{h}") for h in range(2)] for s in layers]
        last_weights = [ph.sem(f"last_weights_loaded{h}") for h in range(2)]
        rows = [ph.sem(f"rows_loaded{h}") for h in range(2)]
        turned = ph.sem("rows_turned")
        turned_copied = ph.sem("rows_copied")
        multiplied = [ph.sem(f"multiplied{s}") for s in layers]
        hidden_written = [ph.sem(f"hidden_written{s}") for s in layers]
        last_done = ph.sem("last_products")
        written = ph.sem("results_written")
        stored = c["pool_dma"]
        counts = ph.sem("pool_turns")
        ps_t = ph.psum("t", [LANES, DK, PAIR_TILE])
        ps_h = [ph.psum(f"h{s}", [LANES, units, 512]) for s in layers]
        ps_o = ph.psum("o", [LANES, 2, 2, D])
        turns = tiles // 2
        block = ph.block()

        @block.sync
        def _(sp):
            def load_rows(t, h):
                sp.dma_start(xs[h], rows_in[bass.ds(t, 1)].rearrange("t p s d -> p (t s) d")).then_inc(rows[h], 16)

            def load_tile(t, h, more=True):
                ex = sp.value_load(expert_of[0:1, bass.ds(t, 1)], min_val=0, max_val=e - 1)
                for s in layers:
                    sp.wait_ge(multiplied[s], t * units + units)
                    sp.wait_ge(hidden_written[s], t * units + units)
                    w, b = hidden[s]
                    sp.dma_start(w_sb[s][h], w[bass.ds(ex, 1), :, :].rearrange("e (k p) f -> p (e k) f", p=LANES))\
                      .then_inc(weights[s][h], 16)
                    with nc.allow_non_contiguous_dma(reason="a column of biases"):
                        sp.dma_start(b_sb[s][h], b[bass.ds(ex, 1), :].rearrange("e (m p) -> p (e m)", p=LANES))\
                          .then_inc(weights[s][h], 16)
                if more:
                    sp.wait_ge(turned, t + 1)
                    load_rows(t + 1, 1 - h)
                sp.wait_ge(last_done, t + 1)
                sp.wait_ge(written, t + 1)
                sp.dma_start(wl_sb[h], last[0][bass.ds(ex, 1), :, :].rearrange("e (k p) f -> p (e k) f", p=LANES))\
                  .then_inc(last_weights[h], 16)
                sp.dma_start(bl_sb[h], last[1][bass.ds(ex, 1), :].to_broadcast([LANES, D]))\
                  .then_inc(last_weights[h], 16)

            load_rows(0, 0)
            with sp.Fori(0, turns - 1) as i:
                for h in range(2):
                    load_tile(i * 2 + h, h)
            load_tile(tiles - 2, 0)
            load_tile(tiles - 1, 1, more=False)

        @block.tensor
        def _(pe):
            def turn(t, h):
                pe.wait_ge(rows[h], (t - h) * 8 + 16)
                for s in range(2):
                    for k in range(DK):
                        done = pe.transpose(ps_t[:, k, s * LANES:(s + 1) * LANES], xs[h][:, s, k * LANES:(k + 1) * LANES],
                                            c["ident"])
                done.then_inc(turned, 1)

            def layer(s, t, h):
                pe.wait_ge(weights[s][h], (t - h) * 16 + 32)
                if s == 0:
                    pe.wait_ge(turned_copied, t + 1)
                    of = xt[h]
                else:
                    pe.wait_ge(hidden_written[s - 1], t * units + 3 * units)
                    of = hid[s - 1][h]
                for m in range(units):
                    pe.wait_ge(hidden_written[s], t * units + (units + m + 1))
                    for k in range(ins[s]):
                        done = pe.matmul(ps_h[s][:, m, 0:PAIR_TILE], w_sb[s][h][:, k, m * LANES:(m + 1) * LANES],
                                         of[:, k, :], start=(k == 0), stop=(k == ins[s] - 1))
                    done.then_inc(multiplied[s], 1)

            def output(t, h):
                pe.wait_ge(last_weights[h], (t - h) * 16 + 32)
                pe.wait_ge(hidden_written[-1], t * units + 3 * units)
                pe.wait_ge(written, t + 1)
                for s in range(2):
                    for m in range(units):
                        done = pe.matmul(ps_o[:, h, s, :], hid[-1][h][:, m, s * LANES:(s + 1) * LANES], wl_sb[h][:, m, :],
                                         start=(m == 0), stop=(m == units - 1))
                done.then_inc(last_done, 1)

            def step(t, h, before=True, more=True):
                layer(0, t, h)
                if more:
                    turn(t + 1, 1 - h)
                if before:
                    output(t - 1, 1 - h)
                for s in layers[1:]:
                    layer(s, t, h)

            for s in layers:
                pe.sem_inc(multiplied[s], 2 * units)
            pe.sem_inc(last_done, 2)
            pe.sem_inc(turned, 1)
            turn(0, 0)
            step(0, 0, before=False)
            step(1, 1)
            with pe.Fori(1, turns - 1) as i:
                for h in range(2):
                    step(i * 2 + h, h)
            step(tiles - 2, 0)
            step(tiles - 1, 1, more=False)
            output(tiles - 1, 1)

        @block.scalar
        def _(act):
            for s in layers:
                act.sem_inc(hidden_written[s], 2 * units)

            def copy_turned(t, h):
                act.wait_ge(turned, t + 2)
                act.copy(xt[h], ps_t[:, :, :]).then_inc(turned_copied, 1)

            def apply(s, t, h):
                act.wait_ge(weights[s][h], (t - h) * 16 + 32)
                for m in range(units):
                    act.wait_ge(multiplied[s], t * units + (2 * units + m + 1))
                    act.activation(hid[s][h][:, m, :], ps_h[s][:, m, 0:PAIR_TILE], func, bias=b_sb[s][h][:, m:m + 1])\
                       .then_inc(hidden_written[s], 1)

            def step(t, h, more=True):
                apply(0, t, h)
                if more:
                    copy_turned(t + 1, 1 - h)
                for s in layers[1:]:
                    apply(s, t, h)

            copy_turned(0, 0)
            with act.Fori(0, turns - 1) as i:
                for h in range(2):
                    step(i * 2 + h, h)
            step(tiles - 2, 0)
            step(tiles - 1, 1, more=False)

        @block.vector
        def _(dve):
            dve.sem_inc(written, 2)
            with dve.Fori(0, turns) as i:
                for h in range(2):
                    t = i * 2 + h
                    dve.wait_ge(last_weights[h], i * 32 + 32)
                    dve.wait_ge(last_done, t + 3)
                    dve.wait_ge(counts, t + 1)
                    dve.tensor_tensor(res[h], ps_o[:, h, :, :], across(bl_sb[h], 2), ALU.add).then_inc(written, 1)

        @block.gpsimd
        def _(pool):
            pool.sem_inc(counts, 2)

            def store(t, h):
                pool.wait_ge(written, t + 3)
                pool.dma_start(rows_out[bass.ds(t, 1)].rearrange("t p s d -> p (t s) d"), res[h])\
                    .then_inc(stored.sems[h], 16)

            store(0, 0)
            store(1, 1)
            with pool.Fori(1, turns) as i:
                for h in range(2):
                    stored.wait(pool, h, i)
                    pool.sem_inc(counts, 1)
                    store(i * 2 + h, h)
            for h in range(2):
                stored.wait(pool, h, turns)
                stored.finished(h, turns)


class Combine:

    def __init__(self, c, a, table, slots, w_one, w_two, target):
        self.fetched, self.table, self.slots = c["pool_dma"], table, slots
        self.weights, self.target = (w_one, w_two), target
        self.rows = a.take(RING, 2, D, rows=P)

    def begin(self, ph, block):
        added = self.added = ph.sem("rows_added")

        @block.gpsimd
        def _(pool):
            for t in range(NT):
                if t >= RING:
                    pool.wait_ge(added, 2 * (t - RING) + 2)
                for i in range(2):
                    pool.indirect_dma_start(
                        self.rows[:, t % RING, i, :], None, self.table,
                        bass.IndirectOffsetOnAxis(ap=self.slots[:, i, t:t + 1].bitcast(U32), axis=0))\
                        .then_inc(self.fetched.sems[t % RING], 16)

    def add(self, dve, t):
        self.fetched.wait(dve, t % RING, 2 * (t // RING) + 2)
        for i, w in enumerate(self.weights):
            if i:
                dve.wait_ge(self.added, 2 * t + 1)
            dve.scalar_tensor_tensor(self.target[:, t, :], self.rows[:, t % RING, i, :], w[:, t:t + 1],
                                     self.target[:, t, :], ALU.mult, ALU.add).then_inc(self.added, 1)
        dve.wait_ge(self.added, 2 * t + 2)

    def finished(self):
        for h in range(RING):
            self.fetched.finished(h, 2 * len(range(h, NT, RING)))


def last_norm(nc, name, a, combine, x, y, gamma, beta, out):
    stats = a.take(NT, 6, rows=P)
    mean, root, spare = (a.take(NT, rows=P) for _ in range(3))
    g, b = a.take(D, rows=P), a.take(D, rows=P)
    with Phase(nc, name) as ph:
        loaded, step, asked, rooted, ready, stored = (
            ph.sem(s) for s in ("loaded", "dve_step", "root_asked", "root_ready", "quad_ready", "stored"))
        block = ph.block()
        combine.begin(ph, block)

        @block.vector
        def _(dve):
            st = Steps(dve, step)
            dve.wait_ge(loaded, 32)
            st.then(dve.tensor_tensor(x, x, across(b, NT), ALU.add))

            def normalize(q, first, n):
                part, rows = y[:, first:first + n, :], x[:, first:first + n, :]
                dve.wait_ge(rooted, q + 1)
                st.then(dve.reciprocal(root[:, first:first + n], root[:, first:first + n]))
                for t in range(first, first + n):
                    st.done(dve.tensor_scalar(y[:, t, :], y[:, t, :], mean[:, t:t + 1], root[:, t:t + 1],
                                              ALU.subtract, ALU.mult))
                st.all()
                st.then(dve.tensor_tensor(part, part, across(g, n), ALU.mult))
                dve.tensor_tensor(rows, rows, part, ALU.add).then_inc(ready, 1)

            for q, (first, n) in enumerate(quads()):
                row_statistics(dve, st, y, stats, mean, root, spare, range(first, first + n),
                               lambda t: combine.add(dve, t)).then_inc(asked, 1)
                if q:
                    normalize(q - 1, *quads()[q - 1])
            normalize(q, *quads()[q])

        @block.scalar
        def _(act):
            for q, (t, n) in enumerate(quads()):
                act.wait_ge(asked, q + 1)
                act.activation(root[:, t:t + n], root[:, t:t + n], ACT.Sqrt).then_inc(rooted, 1)

        @block.sync
        def _(sp):
            sp.dma_start(g, gamma.unsqueeze(0).to_broadcast([P, D])).then_inc(loaded, 16)
            sp.dma_start(b, beta.unsqueeze(0).to_broadcast([P, D])).then_inc(loaded, 16)
            rows = out.rearrange("(t p) d -> p t d", p=P)
            for q, (t, n) in enumerate(quads()):
                sp.wait_ge(ready, q + 1)
                sp.dma_start(rows[:, t:t + n, :], x[:, t:t + n, :]).then_inc(stored, 16)
            sp.wait_ge(stored, 16 * len(quads()))

        combine.finished()


def best_two(dve, st, c, scores, tmp, asked, answered):
    e = scores.shape[2]
    rank, one, two, rest, m1, m2, exp, total = tmp
    pick = dve.tensor_tensor
    st.then(dve.tensor_scalar(rank, c["lane"][0:P, 0:e], -1.0, float(e), ALU.mult, ALU.add))

    def best(of, out, value):
        st.then(dve.tensor_reduce(value, of, AX.X, ALU.max))
        st.then(pick(out, of, over(value, e), ALU.is_equal))
        st.then(pick(out, out, across(rank, NT), ALU.mult))
        st.then(dve.tensor_reduce(total, out, AX.X, ALU.max))
        st.then(pick(out, out, over(total, e), ALU.is_equal))

    best(scores, one, m1)
    st.then(dve.scalar_tensor_tensor(rest, one, -BIG, scores, ALU.mult, ALU.add))
    best(rest, two, m2)
    pick(exp, m2, m1, ALU.subtract).then_inc(asked, 1)
    dve.wait_ge(answered, 1)
    st.then(dve.tensor_scalar_add(total, exp, 1.0))
    st.then(dve.reciprocal(total, total))
    st.then(pick(exp, exp, total, ALU.mult))


def best_two_places(a, e):
    return (a.take(e, rows=P), a.take(NT, e, rows=P), a.take(NT, e, rows=P), a.take(NT, e, rows=P),
            a.take(NT, rows=P), a.take(NT, rows=P), a.take(NT, rows=P), a.take(NT, rows=P))


def router(nc, name, c, a, src_t, w_dram, b_dram, scores, softmax=False, picks=None, plus=None):
    e = scores.shape[2]
    ks = src_t.shape[1]
    w = a.take(ks, e)
    b = a.take(e, rows=P)
    top, total = a.take(NT, rows=P), a.take(NT, rows=P)
    with Phase(nc, name) as ph:
        loaded = ph.sem("loaded")
        multiplied = ph.sem("multiplied")
        step = ph.sem("dve_step")
        soft = ph.sem("softmax_asked")
        soft_done = ph.sem("softmax_done")
        asked = ph.sem("exp_asked")
        answered = ph.sem("exp_done")
        ps = ph.psum("scores", [LANES, 512])
        view = ps[0:P, 0:NT * e].rearrange("p (t e) -> p t e", e=e)
        block = ph.block()

        @block.sync
        def _(sp):
            with nc.allow_non_contiguous_dma(reason="few scores: short rows"):
                sp.dma_start(w, w_dram.rearrange("(k p) e -> p k e", p=LANES)).then_inc(loaded, 16)
            sp.dma_start(b, b_dram.unsqueeze(0).to_broadcast([P, e])).then_inc(loaded, 16)

        @block.tensor
        def _(pe):
            pe.wait_ge(loaded, 32)
            for t in range(NT):
                for k in range(ks):
                    last = pe.matmul(view[:, t, :], src_t[:, k, t * P:(t + 1) * P], w[:, k, :],
                                     start=(k == 0), stop=(k == ks - 1))
            last.then_inc(multiplied, 1)

        @block.vector
        def _(dve):
            st = Steps(dve, step)
            if plus is not None:
                st.done(dve.tensor_tensor(plus[0], plus[0], plus[1], ALU.add))
            dve.wait_ge(loaded, 32)
            dve.wait_ge(multiplied, 1)
            st.then(dve.tensor_tensor(scores, across(b, NT), view, ALU.add))
            if softmax:
                st.then(dve.tensor_reduce(top, scores, AX.X, ALU.max))
                dve.tensor_tensor(scores, scores, over(top, e), ALU.subtract).then_inc(soft, 1)
                dve.wait_ge(soft_done, 1)
                st.then(dve.tensor_reduce(total, scores, AX.X, ALU.add))
                st.then(dve.reciprocal(total, total))
                st.then(dve.tensor_tensor(scores, scores, over(total, e), ALU.mult))
            if picks is not None:
                best_two(dve, st, c, scores, picks, asked, answered)

        @block.scalar
        def _(act):
            if softmax:
                act.wait_ge(soft, 1)
                act.activation(scores, scores, ACT.Exp).then_inc(soft_done, 1)
            if picks is not None:
                act.wait_ge(asked, 1)
                act.activation(picks[6], picks[6], ACT.Exp).then_inc(answered, 1)


def choose_half(nc, name, c, a, scores, gates, chosen, beside=None):
    each = a.take(NT, P, rows=P)
    row = a.take(N, rows=P)
    spare = a.take(N, rows=P)
    part = a.take(4, NT, rows=P)
    rank = a.take(NT, rows=P)
    with Phase(nc, name) as ph:
        repeated = ph.sem("scores_repeated")
        turned = ph.sem("quads_turned")
        copied = ph.sem("quads_copied")
        step = ph.sem("dve_step")
        ps = ph.psum("row", [LANES, len(quads()), 512])
        block = ph.block()
        beside_work(ph, block, beside)

        @block.tensor
        def _(pe):
            pe.wait_ge(repeated, 1)
            for q, (t, n) in enumerate(quads()):
                for j in range(n):
                    last = pe.transpose(ps[0:P, q, j * P:(j + 1) * P], each[:, t + j, :], c["ident"][0:P, 0:P])
                last.then_inc(turned, 1)

        @block.scalar
        def _(act):
            for q, (t, n) in enumerate(quads()):
                act.wait_ge(turned, q + 1)
                act.copy(row[:, t * P:(t + n) * P], ps[0:P, q, 0:n * P]).then_inc(copied, 1)

        @block.vector
        def _(dve):
            st = Steps(dve, step)
            dve.tensor_copy(each, over(scores, P)).then_inc(repeated, 1)
            st.then(dve.memset(part, 0.0))
            dve.wait_ge(copied, len(quads()))
            for t in range(NT):
                own, lo, hi = scores[:, t:t + 1], t * P, (t + 1) * P
                if t > 0:
                    st.then(dve.tensor_scalar(spare[:, 0:lo], row[:, 0:lo], own, None, ALU.is_ge, ALU.add,
                                              accum_out=part[:, 0, t:t + 1]))
                st.then(dve.tensor_scalar(spare[:, lo:N], row[:, lo:N], own, None, ALU.is_gt, ALU.add,
                                          accum_out=part[:, 1, t:t + 1]))
                st.then(dve.scalar_tensor_tensor(spare[:, lo:hi], row[:, lo:hi], own, c["after"][0:P, 0:P],
                                                 ALU.is_equal, ALU.mult, accum_out=part[:, 2, t:t + 1]))
            st.then(dve.tensor_tensor(rank, part[:, 0, :], part[:, 1, :], ALU.add))
            st.then(dve.tensor_tensor(rank, rank, part[:, 2, :], ALU.add))
            for gate in gates:
                st.then(dve.scalar_tensor_tensor(gate, rank, float(chosen), scores, ALU.is_lt, ALU.mult))


ACCS = 4
MASKS = 4
HEADS = 4
GE = 4
ROW = HEADS * GE + HEADS
SRC_ROW = 24
DST_ROW = 8
PARTS = 3
STRIDE = PARTS * DST_ROW
BF16 = mybir.dt.bfloat16


def attention_scores(nc, name, c, arena, src_t, rec, places, w, picks, src_table):
    a = Arena(arena, ACC_AT, YT_AT)
    node = a.take(NT, SRC_ROW, rows=P)
    bests = a.take(ACCS, NT, STRIDE, rows=P)
    best = bests[:, 0, :, :]
    att = a.take(2, HEADS * GE, rows=P)
    w_sb = a.take(DK, HEADS * GE)
    prod = a.take(NT, HEADS * GE, rows=P)
    self_e = a.take(NT, HEADS, rows=P)
    masked_at = a.at
    target = a.take(NT, DST_ROW, rows=P)
    target_parts = a.take(NT * STRIDE // 2, rows=P).bitcast(BF16).rearrange("p (t w) -> p t w", t=NT)
    ident_b = a.take(LANES // 2).bitcast(BF16)
    all_sums = a.take(2 * ACCS, NT, STRIDE, rows=P)
    sums = all_sums[:, 0, :, 0:ROW]
    hot_t_at = a.at
    b = Arena(arena, TMP_AT, REC_AT)
    edge = b.take(T_GAT, ROW)
    edge_dst = b.take(T_GAT, DST_ROW)
    weight = b.take(T_GAT, HEADS)
    ring = b.take(RING, GROUP, SRC_ROW)
    idx = b.take(RING, GROUP, dtype=I32)
    hot = b.take(RING, GROUP, P)
    head = lambda v: v.rearrange("p t (h g) -> p t h g", h=HEADS)

    def node_terms():
        with Phase(nc, name + "_terms") as ph:
            loaded, multiplied, step, stored = (ph.sem(x) for x in ("loaded", "multiplied", "dve_step", "stored"))
            ready = ph.sem("node_ready")
            ps = ph.psum("h", [LANES, 512])
            view = ps[0:P, 0:NT * HEADS * GE].rearrange("p (t e) -> p t e", e=HEADS * GE)
            block = ph.block()

            @block.sync
            def _(sp):
                sp.dma_start(w_sb, w["W_gat"].rearrange("(k p) e -> p k e", p=LANES)).then_inc(loaded, 16)
                for i, n in enumerate(("att_src", "att_dst")):
                    sp.dma_start(att[:, i, :], w[n].rearrange("h g -> (h g)").unsqueeze(0)
                                 .to_broadcast([P, HEADS * GE])).then_inc(loaded, 16)
                sp.wait_ge(ready, 1)
                sp.dma_start(src_table.rearrange("(t p) d -> p t d", p=P), node).then_inc(stored, 16)
                sp.wait_ge(stored, 16)

            @block.tensor
            def _(pe):
                pe.wait_ge(loaded, 48)
                for t in range(NT):
                    for k in range(DK):
                        last = pe.matmul(view[:, t, :], src_t[:, k, t * P:(t + 1) * P], w_sb[:, k, :],
                                         start=(k == 0), stop=(k == DK - 1))
                last.then_inc(multiplied, 1)

            @block.vector
            def _(dve):
                st = Steps(dve, step)
                dve.wait_ge(loaded, 48)
                dve.wait_ge(multiplied, 1)
                st.then(dve.tensor_copy(node[:, :, 0:16], view))
                for i in range(2):
                    st.then(dve.tensor_tensor(prod, node[:, :, 0:16], across(att[:, i, :], NT), ALU.mult))
                    st.then(dve.tensor_reduce(node[:, :, 16 + HEADS * i:16 + HEADS * (i + 1)], head(prod),
                                              AX.X, ALU.add))
                for x in range(ACCS):
                    st.then(dve.tensor_copy(bests[:, x, :, 0:HEADS], node[:, :, 16:20]))
                dve.sem_inc(ready, 1)

    def maxima():
        z = Arena(arena, masked_at, YT_AT)
        quad = GROUP // 2
        miss = hot
        masked = z.take(MASKS, quad, HEADS * P)
        new = z.take(2, quad, HEADS, rows=P)
        bodies = T_GAT // (RING * GROUP)
        units = 2 * RING
        by_act = 3
        with Phase(nc, name + "_max") as ph:
            turns = ph.sem("pool_turns")
            idx_ready = [ph.sem(f"idx_ready{h}") for h in range(RING)]
            gathered = c["pool_dma"]
            kept = ph.sem("groups_kept")
            step = ph.sem("dve_step")
            missed = ph.sem("miss_ready")
            act_masked = ph.sem("act_masked")
            dve_masked = ph.sem("dve_masked")
            turned = ph.sem("quads_turned")
            reduced = ph.sem("quads_reduced")
            ps = ph.psum("t", [LANES, 2, quad, 512])
            block = ph.block()

            @block.gpsimd
            def _(pool):
                with pool.Fori(0, bodies) as i:
                    for h in range(RING):
                        pool.wait_ge(idx_ready[h], i + 1)
                        pool.sem_inc(turns, 1)
                        for j in range(GROUP):
                            pool.indirect_dma_start(
                                ring[:, h, j, :], None, src_table,
                                bass.IndirectOffsetOnAxis(ap=idx[:, h, j:j + 1].bitcast(U32), axis=0))\
                                .then_inc(gathered.sems[h], 16)

            @block.scalar
            def _(act):
                def index(g, h):
                    act.copy(idx[:, h, :], rec[:, bass.ds(g * GROUP, GROUP), 0].bitcast(I32))\
                       .then_inc(idx_ready[h], 1)

                act.sem_inc(act_masked, units)
                for h in range(RING):
                    index(h, h)

                def group(i, h, more):
                    g = i * RING + h
                    gathered.wait(act, h, i * GROUP + GROUP)
                    act.copy(edge[:, bass.ds(g * GROUP, GROUP), :], ring[:, h, :, 0:ROW]).then_inc(kept, 1)
                    act.wait_ge(missed, g + 1)
                    for q in range(2):
                        u = 2 * h + q
                        act.wait_ge(turned, i * units + (units + u + 1 - MASKS))
                        for x in range(by_act):
                            for j in range(quad):
                                last = act.activation(masked[:, u % MASKS, j, x * P:(x + 1) * P],
                                                      miss[:, h, quad * q + j, :], ACT.Identity, scale=-BIG,
                                                      bias=ring[:, h, quad * q + j, 16 + x:17 + x])
                        last.then_inc(act_masked, 1)
                    act.wait_ge(kept, g + 1)
                    if more:
                        act.wait_ge(dve_masked, i * units + (2 * h + 2))
                        act.wait_ge(act_masked, i * units + (units + 2 * h + 2))
                        index(g + RING, h)

                with act.Fori(0, bodies - 1) as i:
                    for h in range(RING):
                        group(i, h, True)
                for h in range(RING):
                    group(bodies - 1, h, False)

            @block.vector
            def _(dve):
                st = Steps(dve, step)

                def mark(i, h):
                    dve.wait_ge(act_masked, i * units + (2 * h + 2))
                    of = rec[:, bass.ds((i * RING + h) * GROUP, GROUP), 1]
                    dve.tensor_tensor(miss[:, h, :, :], over(of, P), across(c["lane"][:, 0:P], GROUP),
                                      ALU.not_equal).then_inc(missed, 1)

                def mask(i, h, q):
                    u = 2 * h + q
                    dve.wait_ge(missed, i * RING + (h + 1))
                    gathered.wait(dve, h, i * GROUP + GROUP)
                    dve.wait_ge(turned, i * units + (units + u + 1 - MASKS))
                    of = slice(quad * q, quad * (q + 1))
                    for x in range(by_act, HEADS):
                        last = dve.scalar_tensor_tensor(
                            masked[:, u % MASKS, :, x * P:(x + 1) * P], miss[:, h, of, :], -BIG,
                            over(ring[:, h, of, 16 + x], P), ALU.mult, ALU.add)
                    last.then_inc(dve_masked, 1)

                def reduce(i, h, q):
                    u = 2 * h + q
                    dve.wait_ge(turned, i * units + (units + u + 1))
                    st.done(dve.tensor_reduce(new[:, q, :, :], ps[0:P, q, :, :].rearrange("p g (x e) -> p g x e", x=HEADS),
                                              AX.X, ALU.max))
                    _, place = nc.values_load_multi_w_load_instructions(
                        places[0:1, bass.ds((i * RING + h) * GROUP + quad * q, quad)],
                        engines=(mybir.EngineType.DVE,), min_val=0, max_val=(NT - 1) * STRIDE)
                    st.all()
                    dve.sem_inc(reduced, 1)
                    for j in range(quad):
                        to = flat(bests[:, j % ACCS, :, :])[:, bass.ds(place[j], HEADS)]
                        st.lag(dve.tensor_tensor(to, to, new[:, q, j, :], ALU.max), ACCS - 1)

                dve.sem_inc(reduced, 2)
                st.ahead(ACCS)
                def turn(i, more):
                    for u in range(units):
                        if u % 2 == 0:
                            if u + 4 < units:
                                mark(i, u // 2 + 2)
                            elif more:
                                mark(i + 1, u // 2 + 2 - RING)
                        if u + 2 < units:
                            mask(i, (u + 2) // 2, u % 2)
                        elif more:
                            mask(i + 1, 0, u % 2)
                        reduce(i, u // 2, u % 2)

                mark(0, 0)
                mark(0, 1)
                mask(0, 0, 0)
                mask(0, 0, 1)
                with dve.Fori(0, bodies - 1) as i:
                    st.enter(i, units * (1 + quad))
                    turn(i, True)
                st.leave(bodies - 1)
                turn(bodies - 1, False)

            @block.tensor
            def _(pe):
                pe.sem_inc(turned, units)
                with pe.Fori(0, bodies) as i:
                    for u in range(units):
                        pe.wait_ge(act_masked, i * units + (units + u + 1))
                        pe.wait_ge(dve_masked, i * units + (u + 1))
                        pe.wait_ge(reduced, i * units + (u + 1))
                        for j in range(quad):
                            for x in range(HEADS):
                                last = pe.transpose(ps[0:P, u % 2, j, x * LANES:(x + 1) * LANES],
                                                    masked[:, u % MASKS, j, x * P:(x + 1) * P], c["ident"])
                        last.then_inc(turned, 1)

            for h in range(RING):
                gathered.finished(h, GROUP * bodies)

    def target_terms():
        rest = Arena(arena, a.at, YT_AT).take(NT, DST_ROW, rows=P)
        with Phase(nc, name + "_targets") as ph:
            step, asked, answered = (ph.sem(x) for x in ("dve_step", "exp_asked", "exp_done"))
            block = ph.block()

            @block.vector
            def _(dve):
                st = Steps(dve, step)
                tt = dve.tensor_tensor
                for x in range(1, ACCS):
                    st.then(tt(best[:, :, 0:HEADS], best[:, :, 0:HEADS], bests[:, x, :, 0:HEADS], ALU.max))
                st.done(dve.memset(all_sums[:, 1:2 * ACCS, :, :].rearrange("p x t w -> p (x t w)"), 0.0))
                a_dst, a_src, m = node[:, :, 20:24], node[:, :, 16:20], target[:, :, HEADS:2 * HEADS]
                st.then(dve.tensor_copy(target[:, :, 0:HEADS], a_dst))
                st.then(tt(m, best[:, :, 0:HEADS], a_dst, ALU.add))
                st.then(dve.scalar_tensor_tensor(m, m, 0.2, m, ALU.mult, ALU.max))
                st.then(dve.tensor_copy(rest, target))
                for x in range(PARTS):
                    part = target_parts[:, :, x * DST_ROW:(x + 1) * DST_ROW]
                    st.then(dve.tensor_copy(part, rest))
                    st.then(tt(rest, rest, part, ALU.subtract))
                st.done(dve.tensor_copy(ident_b, c["ident"]))
                st.then(tt(self_e, a_src, a_dst, ALU.add))
                st.then(dve.scalar_tensor_tensor(self_e, self_e, 0.2, self_e, ALU.mult, ALU.max))
                st.then(tt(self_e, self_e, m, ALU.subtract))
                dve.sem_inc(asked, 1)
                dve.wait_ge(answered, 1)
                st.then(dve.tensor_copy(sums[:, :, 16:20], self_e))
                for h in range(HEADS):
                    st.then(tt(sums[:, :, GE * h:GE * (h + 1)], node[:, :, GE * h:GE * (h + 1)],
                               over(self_e[:, :, h], GE), ALU.mult))

            @block.scalar
            def _(act):
                act.wait_ge(asked, 1)
                act.activation(self_e, self_e, ACT.Exp).then_inc(answered, 1)

    def target_rows():
        z = Arena(arena, hot_t_at, YT_AT)
        bf16 = lambda v, shape: v.bitcast(BF16).rearrange("p (a b c) -> p a b c", a=shape[0], b=shape[1])
        hot_t = bf16(z.take(GROUP * LANES, rows=P), (2, GROUP))
        hot_b = bf16(hot.rearrange("p a b c -> p (a b c)")[:, 0:RING * GROUP * P // 2], (RING, GROUP))
        bodies = T_GAT // (RING * GROUP)
        with Phase(nc, name + "_rows") as ph:
            hot_ready = ph.sem("hot_ready")
            turned = ph.sem("groups_turned")
            copied = ph.sem("groups_copied")
            multiplied = ph.sem("groups_multiplied")
            taken = ph.sem("groups_taken")
            ps_t = ph.psum("t", [LANES, 2, GROUP, LANES], BF16)
            ps = ph.psum("rows", [LANES, 2, 512])
            block = ph.block()

            @block.vector
            def _(dve):
                def one_hot(i, h):
                    dve.wait_ge(turned, i * RING + (h + 1))
                    dve.tensor_tensor(hot_b[:, h, :, :], over(rec[:, bass.ds((i * RING + h) * GROUP, GROUP), 1], P),
                                      across(c["lane"][:, 0:P], GROUP), ALU.is_equal).then_inc(hot_ready, 1)

                def take(i, h):
                    g = i * RING + h
                    dve.wait_ge(multiplied, g + 1)
                    dve.tensor_reduce(edge_dst[:, bass.ds(g * GROUP, GROUP), :],
                                      ps[:, h % 2, 0:GROUP * STRIDE].rearrange("p (g x w) -> p g w x", g=GROUP, x=PARTS),
                                      AX.X, ALU.add).then_inc(taken, 1)

                dve.sem_inc(taken, 2)
                for h in range(RING):
                    one_hot(0, h)
                with dve.Fori(0, bodies - 1) as i:
                    for h in range(RING):
                        take(i, h)
                        one_hot(i + 1, h)
                for h in range(RING):
                    take(bodies - 1, h)

            @block.scalar
            def _(act):
                with act.Fori(0, bodies) as i:
                    for h in range(RING):
                        g = i * RING + h
                        act.wait_ge(turned, g + (RING + 1))
                        act.copy(hot_t[:, h % 2, :, :], ps_t[0:P, h % 2, :, :]).then_inc(copied, 1)

            @block.tensor
            def _(pe):
                pe.sem_inc(turned, RING)

                def turn(g, h):
                    pe.wait_ge(hot_ready, g + 1)
                    for j in range(GROUP):
                        last = pe.transpose(ps_t[0:P, h % 2, j, :], hot_b[:, h, j, :], ident_b)
                    last.then_inc(turned, 1)

                def multiply(g, h):
                    _, place = nc.values_load_multi_w_load_instructions(
                        places[0:1, bass.ds(g * GROUP, GROUP)], engines=(mybir.EngineType.PE,),
                        min_val=0, max_val=(NT - 1) * STRIDE)
                    pe.wait_ge(copied, g + 1)
                    pe.wait_ge(taken, g + 1)
                    for j in range(GROUP):
                        last = pe.matmul(ps[:, h % 2, j * STRIDE:(j + 1) * STRIDE], hot_t[:, h % 2, j, :],
                                         flat(target_parts)[:, bass.ds(place[j], STRIDE)], start=True, stop=True)
                    last.then_inc(multiplied, 1)

                turn(0, 0)
                with pe.Fori(0, bodies - 1) as i:
                    for h in range(RING):
                        turn(i * RING + (h + 1), (h + 1) % RING)
                        multiply(i * RING + h, h)
                last = (bodies - 1) * RING
                for h in range(RING):
                    if h + 1 < RING:
                        turn(last + h + 1, h + 1)
                    multiply(last + h, h)

    def edge_weights():
        with Phase(nc, name + "_edges") as ph:
            step, asked, answered = (ph.sem(x) for x in ("dve_step", "exp_asked", "exp_done"))
            block = ph.block()

            @block.vector
            def _(dve):
                st = Steps(dve, step)
                tt = dve.tensor_tensor
                st.then(tt(weight, edge[:, :, 16:20], edge_dst[:, :, 0:HEADS], ALU.add))
                st.then(dve.scalar_tensor_tensor(weight, weight, 0.2, weight, ALU.mult, ALU.max))
                st.then(tt(weight, weight, edge_dst[:, :, HEADS:2 * HEADS], ALU.subtract))
                st.then(dve.tensor_scalar_min(weight, weight, 0.0))
                dve.sem_inc(asked, 1)
                dve.wait_ge(answered, 1)
                for h in range(HEADS):
                    st.then(tt(edge[:, :, GE * h:GE * (h + 1)], edge[:, :, GE * h:GE * (h + 1)],
                               over(weight[:, :, h], GE), ALU.mult))
                st.then(dve.tensor_copy(edge[:, :, 16:20], weight))

            @block.scalar
            def _(act):
                act.wait_ge(asked, 1)
                act.activation(weight, weight, ACT.Exp).then_inc(answered, 1)

    def edge_sums():
        odd = Arena(arena, hot_t_at, YT_AT).take(2, GROUP * ROW, rows=P)
        with Phase(nc, name + "_sum") as ph:
            step = ph.sem("dve_step")
            hot_ready = ph.sem("hot_ready")
            summed = ph.sem("groups_summed")
            moved = ph.sem("odd_groups_moved")
            dve_added, pool_added = ph.sem("even_groups_added"), ph.sem("odd_groups_added")
            pool_step = ph.sem("pool_step")
            ps = ph.psum("sum", [LANES, RING, 512])
            bodies = T_GAT // (RING * GROUP)
            block = ph.block()

            def load_places(eng, i, h):
                return nc.values_load_multi_w_load_instructions(
                    places[0:1, bass.ds((i * RING + h) * GROUP, GROUP)],
                    engines=(eng,), min_val=0, max_val=(NT - 1) * STRIDE)[1]

            def add_group(eng, st, added, of, place, accs):
                for j in range(GROUP):
                    to = flat(all_sums[:, accs + j % ACCS, :, :])[:, bass.ds(place[j], ROW)]
                    st.lag(eng.tensor_tensor(to, to, of[:, j * ROW:(j + 1) * ROW], ALU.add), ACCS - 1)
                st.all()
                eng.sem_inc(added, 1)

            @block.vector
            def _(dve):
                st = Steps(dve, step)
                st.ahead(ACCS)
                dve.sem_inc(dve_added, 2)

                def one_hot(i, h):
                    dve.wait_ge(summed, i * RING + (h + 1))
                    of = rec[:, bass.ds((i * RING + h) * GROUP, GROUP), :]
                    dve.tensor_tensor(hot[:, h, :, :], over(of[:, :, 1], P), across(c["lane"][:, 0:P], GROUP),
                                      ALU.is_equal).then_inc(hot_ready, 1)

                def even(i, h):
                    place = load_places(mybir.EngineType.DVE, i, h)
                    dve.wait_ge(summed, i * RING + (RING + h + 1))
                    add_group(dve, st, dve_added, ps[0:P, h, 0:GROUP * ROW], place, 0)

                for h in range(RING):
                    one_hot(0, h)
                with dve.Fori(0, bodies - 1) as i:
                    st.enter(i, 2 * GROUP)
                    for h in range(0, RING, 2):
                        even(i, h)
                        one_hot(i + 1, h)
                        one_hot(i + 1, h + 1)
                st.leave(bodies - 1)
                for h in range(0, RING, 2):
                    even(bodies - 1, h)

            @block.gpsimd
            def _(pool):
                st = Steps(pool, pool_step)
                st.ahead(ACCS)
                pool.sem_inc(pool_added, 2)
                with pool.Fori(0, bodies) as i:
                    st.enter(i, 2 * GROUP)
                    for h in range(1, RING, 2):
                        place = load_places(mybir.EngineType.Pool, i, h)
                        pool.wait_ge(moved, i * 2 + (h // 2 + 3))
                        add_group(pool, st, pool_added, odd[:, h // 2, :], place, ACCS)
                st.leave(bodies)

            @block.scalar
            def _(act):
                act.sem_inc(moved, 2)
                with act.Fori(0, bodies) as i:
                    for h in range(1, RING, 2):
                        act.wait_ge(summed, i * RING + (RING + h + 1))
                        act.wait_ge(pool_added, i * 2 + (h // 2 + 1))
                        act.copy(odd[:, h // 2, :], ps[0:P, h, 0:GROUP * ROW]).then_inc(moved, 1)

            @block.tensor
            def _(pe):
                pe.sem_inc(summed, RING)
                with pe.Fori(0, bodies) as i:
                    for h in range(RING):
                        pe.wait_ge(hot_ready, i * RING + (h + 1))
                        pe.wait_ge((dve_added, moved)[h % 2], i * 2 + (h // 2 + 1))
                        for j in range(GROUP):
                            last = pe.matmul(ps[0:P, h, j * ROW:(j + 1) * ROW], hot[:, h, j, :],
                                             edge[:, bass.ds((i * RING + h) * GROUP + j, 1), :]
                                             .rearrange("p a b -> p (a b)"), start=True, stop=True)
                        last.then_inc(summed, 1)

    def finish():
        k = HEADS * GE
        f = Arena(arena, TMP_AT, REC_AT)
        agg = f.take(NT, k, rows=P)
        sq = f.take(NT, k, rows=P)
        mean = f.take(NT, rows=P)
        root = f.take(NT, rows=P)
        par = f.take(3, k, rows=P)
        scores = f.take(NT, GE, rows=P)
        with Phase(nc, name + "_norm") as ph:
            loaded, step, asked, rooted, e_asked, e_done = (
                ph.sem(x) for x in ("loaded", "dve_step", "root_asked", "root_ready", "exp_asked", "exp_done"))
            block = ph.block()

            @block.sync
            def _(sp):
                for i, n in enumerate(("b_gat", "ln_gamma", "ln_beta")):
                    sp.dma_start(par[:, i, :], w[n].unsqueeze(0).to_broadcast([P, k])).then_inc(loaded, 16)

            @block.vector
            def _(dve):
                st = Steps(dve, step)
                tt = dve.tensor_tensor
                for x in range(1, 2 * ACCS):
                    st.then(tt(sums, sums, all_sums[:, x, :, 0:ROW], ALU.add))
                st.then(dve.tensor_scalar_add(self_e, sums[:, :, 16:20], 1e-16))
                st.then(dve.reciprocal(self_e, self_e))
                for h in range(HEADS):
                    st.then(tt(agg[:, :, GE * h:GE * (h + 1)], sums[:, :, GE * h:GE * (h + 1)],
                               over(self_e[:, :, h], GE), ALU.mult))
                dve.wait_ge(loaded, 48)
                st.then(tt(agg, agg, across(par[:, 0, :], NT), ALU.add))
                st.then(dve.tensor_reduce(mean, agg, AX.X, ALU.add))
                st.then(dve.tensor_scalar_mul(mean, mean, 1.0 / k))
                st.then(tt(agg, agg, over(mean, k), ALU.subtract))
                st.then(tt(sq, agg, agg, ALU.mult))
                st.then(dve.tensor_reduce(root, sq, AX.X, ALU.add))
                st.then(dve.tensor_scalar(root, root, 1.0 / k, EPS, ALU.mult, ALU.add))
                dve.sem_inc(asked, 1)
                dve.wait_ge(rooted, 1)
                st.then(dve.reciprocal(root, root))
                st.then(tt(agg, agg, over(root, k), ALU.mult))
                st.then(tt(agg, agg, across(par[:, 1, :], NT), ALU.mult))
                st.then(tt(agg, agg, across(par[:, 2, :], NT), ALU.add))
                st.then(dve.tensor_reduce(scores, agg.rearrange("p t (h g) -> p t g h", h=HEADS), AX.X, ALU.add))
                st.then(dve.tensor_scalar_mul(flat(scores), flat(scores), 1.0 / HEADS))
                best_two(dve, st, c, scores, picks, e_asked, e_done)

            @block.scalar
            def _(act):
                act.wait_ge(asked, 1)
                act.activation(root, root, ACT.Sqrt).then_inc(rooted, 1)
                act.wait_ge(e_asked, 1)
                act.activation(picks[6], picks[6], ACT.Exp).then_inc(e_done, 1)

    node_terms()
    maxima()
    target_terms()
    target_rows()
    edge_weights()
    edge_sums()
    finish()


def residual_layers(nc, w, out):
    Phase.cleared = []
    dram = lambda name, shape, dt=F32: nc.dram_tensor(name, shape, dt, kind="Internal").ap()
    by_dst = dram("edges_by_dst", (T_MAIN * LANES, 4))
    by_src = dram("edges_by_src", (T_MAIN * LANES, 4))
    by_gat = dram("gat_edges_by_dst", (T_GAT * LANES, 4))
    rows = [dram(f"rows{i}", (N, D)) for i in range(5)]
    src_table = dram("gat_src_rows", (N, SRC_ROW))
    pair_rows = dram("rows_by_expert", (PAIR_ROWS, D))
    pair_results = dram("results_by_expert", (PAIR_ROWS, D))

    with ExitStack() as ctx:
        arena = ctx.enter_context(nc.sbuf_tensor("arena", [LANES, ARENA], F32))[:, :]
        sb = lambda name, shape, dt=F32: ctx.enter_context(nc.sbuf_tensor(name, shape, dt))[:, :]
        c = constants(nc, ctx, arena)
        at_dst = sb("places_by_dst", [1, T_MAIN], I32)
        at_src = sb("places_by_src", [1, T_MAIN], I32)
        at_gat = sb("places_gat", [1, T_GAT], I32)
        degree = sb("degree", [P, NT])

        n_main, n_gat = E_MAIN // P, E_GAT // LANES
        a = Arena(arena, ACC_AT)
        scatter_dst = Scatter(c, a, P, n_main, by_dst)
        scatter_gat = Scatter(c, a, LANES, n_gat, by_gat)
        scatter_src = Scatter(c, Arena(arena, LATER_AT, WEIGHTS_AT), P, n_main, by_src)
        gat_spill = dram("gat_records", (LANES, 4 * n_gat)), dram("gat_slots", (LANES, n_gat), I32)
        bucket_sort(nc, "sort_dst", c, arena, w["dst"], w["src"], None, P, T_MAIN, D, scatter_dst, at_dst,
                    turns=1)
        bucket_sort(nc, "sort_src", c, arena, w["src"], w["dst"], w["edge_weight"], P, T_MAIN, D, scatter_src, at_src,
                    beside=(scatter_dst, 7))
        e = w["L2_ffn_edge_index"]
        bucket_sort(nc, "sort_gat", c, arena, e[1, :], e[0, :], None, LANES, T_GAT, STRIDE, scatter_gat, at_gat,
                    spill=gat_spill, beside=(scatter_dst, 6), clear=pair_rows)

        def node(at, rows=P):
            return arena[0:rows, at:at + NT * D].rearrange("p (t d) -> p t d", d=D)

        x, y, acc = node(X_AT), node(Y_AT), node(ACC_AT)
        yt = arena[:, YT_AT:YT_AT + DK * N].rearrange("p (k n) -> p k n", k=DK)
        rec = Arena(arena, REC_AT)
        rec_dst, rec_src, rec_gat = rec.take(T_MAIN, 4), rec.take(T_MAIN, 4), rec.take(T_GAT, 4)
        tmp = lambda: Arena(arena, TMP_AT, REC_AT)

        x_view = w["x"].rearrange("(t p) d -> p t d", p=P)
        eps1 = sb("one_plus_eps", [P, 1])
        layer_norm(nc, "L0g_norm", c, arena, x, y, None, rows[0],
                   loads=[(x, x_view), (eps1, w["L0_gnn_eps"].unsqueeze(0).to_broadcast([P, 1]))],
                   beside=(scatter_dst, 4))
        degrees(nc, "degrees", c, Arena(arena, TMP_AT, EARLY_AT), scatter_dst, degree, (scatter_dst, None))
        graph_sum(nc, "L0g_sum", c, arena, rows[0], rec_dst, at_dst, flat(acc), T_MAIN, False,
                  table=by_dst)

        def mix(dve, st, quad_ready, *_):
            st.then(dve.tensor_scalar_add(eps1, eps1, 1.0))
            for t, n in quads():
                dve.scalar_tensor_tensor(y[:, t:t + n, :], y[:, t:t + n, :], eps1, acc[:, t:t + n, :],
                                         ALU.mult, ALU.add).then_inc(quad_ready, 1)

        to_features(nc, "L0g_mix", c, arena, y, yt, mix)
        wide = lambda at, m: arena[:, at:at + m * N].rearrange("p (m n) -> p m n", m=m)
        weight = lambda at, k, f: arena[:, at:at + k * f].rearrange("p (k f) -> p k f", k=k)
        small = sb("column_bias", [LANES, 8])
        stats = sb("batch_stats", [LANES, 8 * 6 * len(CHUNKS)]).rearrange("p (m s) -> p m s", m=8)
        records_loaded, gat_loaded, rec_gat_loaded = (
            ctx.enter_context(nc.semaphore(s)) for s in ("records_loaded", "gat_edges_loaded", "gat_records_loaded"))
        x_parts = [(t, end, ctx.enter_context(nc.semaphore(f"residual_loaded{t}")))
                   for t, end in ((0, 8), (8, 16), (16, NT))]
        h1, h2, h3 = wide(Y_AT, 4), wide(X_AT, 8), wide(Y_AT, 4)
        w1, w2, w3, w4 = (weight(WEIGHTS_AT, k, f) for k, f in ((2, 512), (4, 1024), (8, 512), (4, 256)))
        turns = {1: (2, 1), 2: (9, 3), 3: (9, 1)}
        for i, (src, h, ws) in enumerate(((yt, h1, w1), (h1, h2, w2), (h2, h3, w3)), 1):
            m = h.shape[1]
            dense(nc, f"L0g_mlp{i}", [(src, ws, w[f"L0_gnn_W{i}"])], (small[:, 0:m], w[f"L0_gnn_b{i}"]), h,
                  ACT.Identity, stats[:, 0:m, :], beside=(scatter_src, turns[i][0]))
            batch_norm_elu(nc, f"L0g_bn{i}", Arena(arena, {1: X_AT, 2: Y_AT, 3: TMP_AT}[i]), h, stats[:, 0:m, :],
                           w[f"L0_gnn_g{i}"], w[f"L0_gnn_beta{i}"], beside=(scatter_src, turns[i][1]),
                           later=[(s, x[:, t:end, :], x_view[:, t:end, :]) for t, end, s in x_parts] if i == 3 else ())
        row_bias = sb("row_bias", [P, D])
        scatter_gat.place(Arena(arena, LATER_AT, WEIGHTS_AT))
        project(nc, "L0g_out", h3, w4, w["L0_gnn_W4"], x, (row_bias, w["L0_gnn_b4"]), add=True,
                arrives={t: s for t, _, s in x_parts},
                later=[(records_loaded, *records(rec_dst, by_dst)), (records_loaded, *records(rec_src, by_src)),
                       (gat_loaded, flat(scatter_gat.rec), gat_spill[0]), (gat_loaded, scatter_gat.slot, gat_spill[1])])

        def sparse_experts(name, e, a, spare, one, two, w_one, w_two, target, hidden, last_layer, func):
            slots = spare.take(2, NT, rows=P, dtype=I32)
            expert_of = spare.take(pair_tiles(e), rows=1, dtype=I32)
            send_to_experts(nc, name + "_send", c, spare, y, one, two, slots, expert_of, pair_rows)
            at = a.at
            run_experts(nc, name, c, a, pair_rows, expert_of, hidden, last_layer, pair_results, func)
            a.at = at
            return Combine(c, a, pair_results[0:pair_tiles(e) * PAIR_TILE, :], slots, w_one, w_two, target)

        layer_norm(nc, "L0f_norm", c, arena, x, y, yt, arrived=[(records_loaded, 2), (gat_loaded, 2)])
        a = tmp()
        picks = best_two_places(a, 6)
        _, one, two, _, _, _, w_two, w_one = picks
        at = a.at
        scores = a.take(NT, 6, rows=P)
        rh = a.take(1, N)
        wr = a.take(2, LANES)
        dense(nc, "L0f_hidden", [(yt, wr, w["L0_ffn_router_w1"])], (small[:, 0:1], w["L0_ffn_router_b1"]), rh, ACT.Relu)
        spare = Arena(arena, WEIGHTS_AT, YT_AT)
        router(nc, "L0f_router", c, spare, rh, w["L0_ffn_router_w2"], w["L0_ffn_router_b2"], scores, softmax=True,
               picks=picks)
        a.at = at
        combine = sparse_experts(
            "L0f", 6, a, Arena(arena, WEIGHTS_AT, YT_AT), one, two, w_one, w_two, x,
            [(w["L0_ffn_expert_w1"], w["L0_ffn_expert_b1"]), (w["L0_ffn_expert_w2"], w["L0_ffn_expert_b2"])],
            (w["L0_ffn_expert_w3"], w["L0_ffn_expert_b3"]), ACT.Relu)

        wk = a.take(2, D)
        layer_norm(nc, "L1g_norm", c, arena, x, y, yt, combine=combine, a=a,
                   product=(wk, w["L1_gnn_kernel"], None, acc, rows[1]))
        graph_sum(nc, "L1g_sum", c, arena, rows[1], rec_src, at_src, flat(acc), T_MAIN, True,
                  bias=(row_bias, w["L1_gnn_bias"]))

        layer_norm(nc, "L1f_norm", c, arena, x, y, yt, plus=(acc, None))
        a = tmp()
        scores, gate2, gate1 = a.take(NT, 1, rows=P), a.take(NT, 2, rows=P), a.take(NT, 1, rows=P)
        at = a.at
        router(nc, "L1f_router", c, a, yt, w["L1_ffn_wr"], w["L1_ffn_br"], scores,
               plus=(x, y))
        a.at = at
        choose_half(nc, "L1f_choose", c, a, flat(scores), [gate1[:, :, 0], gate2[:, :, 0], gate2[:, :, 1]],
                    max(1, int(0.5 * N)) - 1, beside=(scatter_gat, 5))
        a.at = at
        hidden_w, hidden_b, out_w = w["L1_ffn_w1"], w["L1_ffn_b1"], w["L1_ffn_w2"]
        experts(nc, "L1f", c, a, yt, x, [(hidden_w, hidden_b)], out_w, gate2, gate1, w["L1_ffn_b2"].unsqueeze(0), 2,
                ACT.Gelu_apprx_tanh, beside=(scatter_gat, None))

        layer_norm(nc, "L2g_norm", c, arena, x, y, yt, rows[2], later=[(rec_gat_loaded, *records(rec_gat, by_gat))])
        graph_sum(nc, "L2g_sum1", c, arena, rows[2], rec_dst, at_dst, flat(acc), T_MAIN, False,
                  arrived=[(rec_gat_loaded, 1)])
        inv = sb("inverse_degree", [P, NT])
        inverse(nc, "L2g_inverse", degree, inv, lambda dve: dve.tensor_scalar_max(inv, degree, 1.0))
        agg_t = arena[:, Y_AT:Y_AT + DK * N].rearrange("p (k n) -> p k n", k=DK)

        def mean(dve, st, quad_ready, *_):
            for t, n in quads():
                dve.tensor_tensor(acc[:, t:t + n, :], acc[:, t:t + n, :], over(inv[:, t:t + n], D),
                                  ALU.mult).then_inc(quad_ready, 1)

        to_features(nc, "L2g_mean", c, arena, acc, agg_t, mean)
        a = tmp()
        ht = a.take(4, N)
        a = Arena(arena, LATER_AT, YT_AT)
        w1l, w1r, w2l, w2r = a.take(2, 512), a.take(2, 512), a.take(4, D), a.take(4, D)
        dense(nc, "L2g_hidden", [(agg_t, w1l, w["L2_gnn_W1l"]), (yt, w1r, w["L2_gnn_W1r"])],
              (small[:, 0:4], w["L2_gnn_b1"]), ht, ACT.Relu)
        project(nc, "L2g_rows", ht, w2l, w["L2_gnn_W2l"], acc, table=rows[3])
        project(nc, "L2g_own", ht, w2r, w["L2_gnn_W2r"], x, (row_bias, w["L2_gnn_b2"]), add=True)
        graph_sum(nc, "L2g_sum2", c, arena, rows[3], rec_dst, at_dst, flat(acc), T_MAIN, False)

        layer_norm(nc, "L2f_norm", c, arena, x, y, yt, plus=(acc, inv))
        picks_at = sb("gat_picks", [P, GE + 3 * NT * GE + 4 * NT])
        picks = best_two_places(Arena(picks_at, 0, picks_at.shape[1]), GE)
        _, one, two, _, _, _, w_two, w_one = picks
        attention_scores(nc, "L2f_gat", c, arena, yt, rec_gat, at_gat,
                         {n: w["L2_ffn_" + n] for n in ("W_gat", "att_src", "att_dst", "b_gat", "ln_gamma", "ln_beta")},
                         picks, src_table)
        a = tmp()
        combine = sparse_experts("L2f", GE, a, Arena(arena, LATER_AT, YT_AT), one, two, w_one, w_two, x,
                                 [(w["L2_ffn_W1"], w["L2_ffn_b1"])], (w["L2_ffn_W2"], w["L2_ffn_b2"]), ACT.Gelu)

        wk = a.take(2, D)
        layer_norm(nc, "L3g_norm", c, arena, x, y, yt, combine=combine, a=a,
                   product=(wk, w["L3_gnn_W"], (row_bias, w["L3_gnn_b"]), acc, rows[4]))
        graph_sum(nc, "L3g_sum", c, arena, rows[4], rec_dst, at_dst, flat(acc), T_MAIN, False)
        inverse(nc, "L3g_inverse", degree, inv, lambda dve: dve.tensor_scalar_add(inv, degree, 1.0))

        layer_norm(nc, "L3f_norm", c, arena, x, y, yt, plus=(acc, inv))
        a = tmp()
        picks = best_two_places(a, 16)
        _, one, two, _, _, _, w_two, w_one = picks
        at = a.at
        scores = a.take(NT, 16, rows=P)
        router(nc, "L3f_router", c, a, yt, w["L3_ffn_gate_w"], w["L3_ffn_gate_b"], scores, picks=picks)
        a.at = at
        combine = sparse_experts("L3f", 16, a, Arena(arena, LATER_AT, YT_AT), one, two, w_one, w_two, y,
                                 [(w["L3_ffn_w1"], w["L3_ffn_b1"])], (w["L3_ffn_w2"], w["L3_ffn_b2"]), ACT.Relu)
        last_norm(nc, "L3f_last", a, combine, x, y, w["L3_ffn_gamma"], w["L3_ffn_beta"], out)


def inverse(nc, name, degree, inv, first):
    with Phase(nc, name) as ph:
        step = ph.sem("dve_step")
        block = ph.block()

        @block.vector
        def _(dve):
            st = Steps(dve, step)
            st.then(first(dve))
            dve.reciprocal(inv, inv)


def kernel(**inputs):
    import concourse.bacc as bacc
    from concourse.bass_utils import run_bass_kernel_spmd

    arrays = {k: np.asarray(v) for k, v in inputs.items()}
    arrays["L0_gnn_eps"] = arrays["L0_gnn_eps"].reshape(1)
    for name in ("L2_gnn_W1l", "L2_gnn_W1r", "L2_gnn_W2l", "L2_gnn_W2r", "L3_gnn_W"):
        arrays[name] = arrays[name].T
    w1, b1, w2 = arrays["L1_ffn_w1"], arrays["L1_ffn_b1"], arrays["L1_ffn_w2"]
    arrays["L1_ffn_w1"] = w1.reshape(D, 2, -1).transpose(1, 0, 2)
    arrays["L1_ffn_b1"] = b1.reshape(2, -1)
    arrays["L1_ffn_w2"] = w2.reshape(2, -1, D)
    del arrays["L1_ffn_attention_mask"]
    arrays = {k: np.ascontiguousarray(v) for k, v in arrays.items()}

    nc = bacc.Bacc("TRN2", target_bir_lowering=False, num_devices=1)
    aps = {k: nc.dram_tensor("in_" + k, v.shape, mybir.dt.from_np(v.dtype), kind="ExternalInput").ap()
           for k, v in arrays.items()}
    out = nc.dram_tensor("out", (N, D), F32, kind="ExternalOutput").ap()
    residual_layers(nc, aps, out)
    r = run_bass_kernel_spmd(nc, [{"in_" + k: v for k, v in arrays.items()}], core_ids=[0])
    return r.results[0]["out"]
```
